# Optimizing a Trainium2 kernel written in Bass

```python
import numpy as np
import jax
import jax.numpy as jnp

def _softmax(x, axis=-1):
    return jax.nn.softmax(x, axis=axis)

def _gelu(x):
    return jax.nn.gelu(x, approximate=True)

def _silu(x):
    return jax.nn.silu(x)

def _sigmoid(x):
    return jax.nn.sigmoid(x)

def _layernorm(x, axis=-1, eps=1e-05):
    m = jnp.mean(x, axis=axis, keepdims=True)
    v = jnp.var(x, axis=axis, keepdims=True)
    return (x - m) / jnp.sqrt(v + eps)

def _scatter_add(tgt, idx, src, axis=0):
    return tgt.at[idx].add(src)

def _segment_sum(src, seg, n):
    return jax.ops.segment_sum(src, seg, n)
kernel_name = 'mk_gnn_ffn_d2_gnn_r32_1b0150'

def setup_inputs(seed: int=0):
    np.random.seed(seed)
    _w = jnp.asarray

    def _rec_inputs():
        import jax
        import jax.numpy as jnp
        _gk = jax.random.key(seed)
        x = -0.0002117 + 1 * jax.random.normal(jax.random.fold_in(_gk, 1), (3125, 256), jnp.float32)
        src = jax.random.randint(jax.random.fold_in(_gk, 2), (50000,), 0, 3125, jnp.int32)
        dst = jax.random.randint(jax.random.fold_in(_gk, 3), (50000,), 0, 3125, jnp.int32)
        _o = jnp.argsort(dst, stable=True)
        src = src[_o]
        dst = dst[_o]
        return (x, src, dst)
    x, src, dst = _rec_inputs()

    def _L0_gnn_setup():
        import jax, jax.numpy as jnp
        import numpy as np
        N = 3125
        E = 50000
        IN_FEATS = 256
        OUT_FEATS = 256
        MAXK = 32

        def _maxk(x, k):
            _, idx = jax.lax.top_k(x, k)
            rows = jnp.arange(x.shape[0])[:, None]
            mask = jnp.zeros_like(x).at[rows, idx].set(1.0)
            return x * mask
        key = jax.random.key(seed)
        k1, k2, k3, k4, k5 = jax.random.split(key, 5)
        feat = jax.random.normal(k1, (N, IN_FEATS), dtype=jnp.float32)
        W_self = jax.random.normal(k2, (IN_FEATS, OUT_FEATS), dtype=jnp.float32) * (1.0 / np.sqrt(IN_FEATS))
        W_neigh = jax.random.normal(k3, (IN_FEATS, OUT_FEATS), dtype=jnp.float32) * (1.0 / np.sqrt(IN_FEATS))
        src = jax.random.randint(k4, (E,), 0, N, dtype=jnp.int64)
        dst = jax.random.randint(k5, (E,), 0, N, dtype=jnp.int64)
        return {'feat': feat, 'W_self': W_self, 'W_neigh': W_neigh, 'src': src, 'dst': dst}
    _L0_gnn_all = _L0_gnn_setup()
    _L0_gnn_in = {k: v for k, v in _L0_gnn_all.items() if k in ('W_self', 'W_neigh')}
    del _L0_gnn_all

    def _L0_ffn_setup():
        import jax, jax.numpy as jnp
        import numpy as np
        B, S, H, F, E, K = (8, 128, 256, 512, 16, 2)
        EPS = 1e-05
        key = jax.random.key(seed)
        ks = jax.random.split(key, 9)
        sc = 0.02
        return {'x': jax.random.normal(ks[0], (B, S, H), dtype=jnp.float32), 'gate_w': jax.random.normal(ks[1], (H, E), dtype=jnp.float32) * sc, 'gate_b': jnp.zeros((E,), dtype=jnp.float32), 'w1': jax.random.normal(ks[2], (E, H, F), dtype=jnp.float32) * sc, 'b1': jnp.zeros((E, F), dtype=jnp.float32), 'w2': jax.random.normal(ks[3], (E, F, H), dtype=jnp.float32) * sc, 'b2': jnp.zeros((E, H), dtype=jnp.float32), 'gamma': jnp.ones((H,), dtype=jnp.float32), 'beta': jnp.zeros((H,), dtype=jnp.float32)}
    _L0_ffn_all = _L0_ffn_setup()
    _L0_ffn_in = {k: v for k, v in _L0_ffn_all.items() if k in ('gate_w', 'gate_b', 'w1', 'b1', 'w2', 'b2', 'gamma', 'beta')}
    del _L0_ffn_all

    def _L1_gnn_setup():
        import jax, jax.numpy as jnp
        import numpy as np
        N = 50000
        E = 25000
        HEADS = 4
        C = 64
        IN = 256
        NEG_SLOPE = 0.2

        def _gat_forward(x, edge_index, W, att_src, att_dst, bias):
            n = x.shape[0]
            h = (x @ W).reshape(n, HEADS, C)
            loop = jnp.arange(n, dtype=edge_index.dtype)
            src = jnp.concatenate([edge_index[0], loop])
            dst = jnp.concatenate([edge_index[1], loop])
            a_src = jnp.einsum('nhc,hc->nh', h, att_src)
            a_dst = jnp.einsum('nhc,hc->nh', h, att_dst)
            logits = a_src[src] + a_dst[dst]
            logits = jnp.where(logits >= 0, logits, NEG_SLOPE * logits)
            seg_max = jax.ops.segment_max(logits, dst, num_segments=n)
            seg_max = jnp.where(jnp.isfinite(seg_max), seg_max, 0.0)
            ex = jnp.exp(logits - seg_max[dst])
            denom = jax.ops.segment_sum(ex, dst, num_segments=n)
            alpha = ex / (denom[dst] + 1e-16)
            msgs = alpha[:, :, None] * h[src]
            out = jax.ops.segment_sum(msgs, dst, num_segments=n)
            out = out.reshape(n, HEADS * C) + bias
            return jax.nn.relu(out)
        key = jax.random.key(seed)
        k = jax.random.split(key, 6)
        x = jax.random.normal(k[0], (N, IN), dtype=jnp.float32)
        edge_index = jax.random.randint(k[1], (2, E), 0, N, dtype=jnp.int64)
        W = jax.random.normal(k[2], (IN, HEADS * C), dtype=jnp.float32) * (1.0 / np.sqrt(IN))
        att_src = jax.random.normal(k[3], (HEADS, C), dtype=jnp.float32) * (1.0 / np.sqrt(C))
        att_dst = jax.random.normal(k[4], (HEADS, C), dtype=jnp.float32) * (1.0 / np.sqrt(C))
        bias = jax.random.normal(k[5], (HEADS * C,), dtype=jnp.float32) * 0.02
        return {'x': x, 'edge_index': edge_index, 'W': W, 'att_src': att_src, 'att_dst': att_dst, 'bias': bias}
    _L1_gnn_all = _L1_gnn_setup()
    _L1_gnn_in = {k: v for k, v in _L1_gnn_all.items() if k in ('W', 'att_src', 'att_dst', 'bias')}
    del _L1_gnn_all

    def _L1_ffn_setup():
        import math
        import jax, jax.numpy as jnp
        import numpy as np
        CAPACITY_FACTOR = 1.25
        TOP_K = 2
        LN_EPS = 1e-05

        def _layer_norm(x, gamma, beta):
            mu = jnp.mean(x, axis=-1, keepdims=True)
            var = jnp.var(x, axis=-1, keepdims=True)
            return (x - mu) * jax.lax.rsqrt(var + LN_EPS) * gamma + beta
        key = jax.random.key(seed)
        ks = jax.random.split(key, 4)
        B, S, D, F, E = (8, 128, 256, 512, 8)
        x = jax.random.normal(ks[0], (B, S, D), dtype=jnp.float32)
        Wr = jax.random.normal(ks[1], (D, E), dtype=jnp.float32) / np.sqrt(D)
        br = jnp.zeros((E,), jnp.float32)
        W1 = jax.random.normal(ks[2], (E, D, F), dtype=jnp.float32) / np.sqrt(D)
        b1 = jnp.zeros((E, F), jnp.float32)
        W2 = jax.random.normal(ks[3], (E, F, D), dtype=jnp.float32) / np.sqrt(F)
        b2 = jnp.zeros((E, D), jnp.float32)
        gamma = jnp.ones((D,), jnp.float32)
        beta = jnp.zeros((D,), jnp.float32)
        return {'x': x, 'Wr': Wr, 'br': br, 'W1': W1, 'b1': b1, 'W2': W2, 'b2': b2, 'gamma': gamma, 'beta': beta}
    _L1_ffn_all = _L1_ffn_setup()
    _L1_ffn_in = {k: v for k, v in _L1_ffn_all.items() if k in ('Wr', 'br', 'W1', 'b1', 'W2', 'b2', 'gamma', 'beta')}
    del _L1_ffn_all
    return {'x': x, 'src': src, 'dst': dst, 'L0_gnn_W_self': _L0_gnn_in['W_self'], 'L0_gnn_W_neigh': _L0_gnn_in['W_neigh'], 'L0_ffn_gate_w': _L0_ffn_in['gate_w'], 'L0_ffn_gate_b': _L0_ffn_in['gate_b'], 'L0_ffn_w1': _L0_ffn_in['w1'], 'L0_ffn_b1': _L0_ffn_in['b1'], 'L0_ffn_w2': _L0_ffn_in['w2'], 'L0_ffn_b2': _L0_ffn_in['b2'], 'L0_ffn_gamma': _L0_ffn_in['gamma'], 'L0_ffn_beta': _L0_ffn_in['beta'], 'L1_gnn_W': _L1_gnn_in['W'], 'L1_gnn_att_src': _L1_gnn_in['att_src'], 'L1_gnn_att_dst': _L1_gnn_in['att_dst'], 'L1_gnn_bias': _L1_gnn_in['bias'], 'L1_ffn_Wr': _L1_ffn_in['Wr'], 'L1_ffn_br': _L1_ffn_in['br'], 'L1_ffn_W1': _L1_ffn_in['W1'], 'L1_ffn_b1': _L1_ffn_in['b1'], 'L1_ffn_W2': _L1_ffn_in['W2'], 'L1_ffn_b2': _L1_ffn_in['b2'], 'L1_ffn_gamma': _L1_ffn_in['gamma'], 'L1_ffn_beta': _L1_ffn_in['beta']}

def reference(x, src, dst, L0_gnn_W_self, L0_gnn_W_neigh, L0_ffn_gate_w, L0_ffn_gate_b, L0_ffn_w1, L0_ffn_b1, L0_ffn_w2, L0_ffn_b2, L0_ffn_gamma, L0_ffn_beta, L1_gnn_W, L1_gnn_att_src, L1_gnn_att_dst, L1_gnn_bias, L1_ffn_Wr, L1_ffn_br, L1_ffn_W1, L1_ffn_b1, L1_ffn_W2, L1_ffn_b2, L1_ffn_gamma, L1_ffn_beta):
    import jax
    import jax.numpy as jnp

    def _L0_gnn_ref(feat, W_self, W_neigh, src, dst):
        import jax, jax.numpy as jnp
        import numpy as np
        N = 3125
        E = 50000
        IN_FEATS = 256
        OUT_FEATS = 256
        MAXK = 32

        def _maxk(x, k):
            _, idx = jax.lax.top_k(x, k)
            rows = jnp.arange(x.shape[0])[:, None]
            mask = jnp.zeros_like(x).at[rows, idx].set(1.0)
            return x * mask
        n = feat.shape[0]
        h_self = feat @ W_self
        h_neigh = feat @ W_neigh
        h_sparse = _maxk(h_neigh, MAXK)
        msg = h_sparse[src]
        summed = jax.ops.segment_sum(msg, dst, num_segments=n)
        deg = jax.ops.segment_sum(jnp.ones((src.shape[0],), dtype=feat.dtype), dst, num_segments=n)
        neigh = summed / jnp.maximum(deg, 1.0)[:, None]
        return h_self + neigh

    def _L0_ffn_ref(x, gate_w, gate_b, w1, b1, w2, b2, gamma, beta):
        import jax, jax.numpy as jnp
        import numpy as np
        B, S, H, F, E, K = (8, 128, 256, 512, 16, 2)
        EPS = 1e-05
        gate_logits = x @ gate_w + gate_b
        topk_vals, topk_idx = jax.lax.top_k(gate_logits, K)
        topk_w = jax.nn.softmax(topk_vals, axis=-1)
        h = jax.nn.relu(jnp.einsum('bsh,ehf->bsef', x, w1) + b1)
        expert_out = jnp.einsum('bsef,efh->bseh', h, w2) + b2
        sel = jnp.take_along_axis(expert_out, topk_idx[:, :, :, None], axis=2)
        moe = jnp.sum(topk_w[..., None] * sel, axis=2)
        y = x + moe
        mu = jnp.mean(y, axis=-1, keepdims=True)
        var = jnp.var(y, axis=-1, keepdims=True)
        return (y - mu) / jnp.sqrt(var + EPS) * gamma + beta

    def _L1_gnn_ref(x, edge_index, W, att_src, att_dst, bias):
        import jax, jax.numpy as jnp
        import numpy as np
        N = 50000
        E = 25000
        HEADS = 4
        C = 64
        IN = 256
        NEG_SLOPE = 0.2

        def _gat_forward(x, edge_index, W, att_src, att_dst, bias):
            n = x.shape[0]
            h = (x @ W).reshape(n, HEADS, C)
            loop = jnp.arange(n, dtype=edge_index.dtype)
            src = jnp.concatenate([edge_index[0], loop])
            dst = jnp.concatenate([edge_index[1], loop])
            a_src = jnp.einsum('nhc,hc->nh', h, att_src)
            a_dst = jnp.einsum('nhc,hc->nh', h, att_dst)
            logits = a_src[src] + a_dst[dst]
            logits = jnp.where(logits >= 0, logits, NEG_SLOPE * logits)
            seg_max = jax.ops.segment_max(logits, dst, num_segments=n)
            seg_max = jnp.where(jnp.isfinite(seg_max), seg_max, 0.0)
            ex = jnp.exp(logits - seg_max[dst])
            denom = jax.ops.segment_sum(ex, dst, num_segments=n)
            alpha = ex / (denom[dst] + 1e-16)
            msgs = alpha[:, :, None] * h[src]
            out = jax.ops.segment_sum(msgs, dst, num_segments=n)
            out = out.reshape(n, HEADS * C) + bias
            return jax.nn.relu(out)
        return _gat_forward(x, edge_index, W, att_src, att_dst, bias)

    def _L1_ffn_ref(x, Wr, br, W1, b1, W2, b2, gamma, beta):
        import math
        import jax, jax.numpy as jnp
        import numpy as np
        CAPACITY_FACTOR = 1.25
        TOP_K = 2
        LN_EPS = 1e-05

        def _layer_norm(x, gamma, beta):
            mu = jnp.mean(x, axis=-1, keepdims=True)
            var = jnp.var(x, axis=-1, keepdims=True)
            return (x - mu) * jax.lax.rsqrt(var + LN_EPS) * gamma + beta
        B, S, D = x.shape
        E = Wr.shape[1]
        N = B * S
        K = TOP_K
        logits = jnp.mean(x, axis=1) @ Wr + br
        routing_weights = jax.nn.softmax(logits, axis=-1)
        capacity = float(math.ceil(N * CAPACITY_FACTOR / E))
        expected_loads = routing_weights.sum(axis=0) * (N / B)
        scale = jnp.where(expected_loads > capacity, capacity / expected_loads, 1.0)
        routing_weights = jax.nn.softmax(routing_weights * scale, axis=-1)
        rw_tok = jnp.broadcast_to(routing_weights[:, None, :], (B, S, E)).reshape(N, E)
        top_w, top_i = jax.lax.top_k(rw_tok, K)
        top_w = jax.nn.softmax(top_w, axis=-1)
        xf = x.reshape(N, D)
        h = jax.nn.gelu(jnp.einsum('nd,edf->enf', xf, W1) + b1[:, None, :], approximate=False)
        y = jnp.einsum('enf,efd->end', h, W2) + b2[:, None, :]
        w_dense = jnp.zeros((N, E), x.dtype).at[jnp.arange(N)[:, None], top_i].add(top_w)
        out = jnp.einsum('ne,end->nd', w_dense, y).reshape(B, S, D)
        out = _layer_norm(out + x, gamma, beta)
        return out
    edge_index = jnp.stack([src, dst])
    x = x + _L0_gnn_ref(_layernorm(x, axis=-1), L0_gnn_W_self, L0_gnn_W_neigh, src, dst)
    x = x + _L0_ffn_ref(_layernorm(x, axis=-1)[None], L0_ffn_gate_w, L0_ffn_gate_b, L0_ffn_w1, L0_ffn_b1, L0_ffn_w2, L0_ffn_b2, L0_ffn_gamma, L0_ffn_beta)[0]
    x = x + _L1_gnn_ref(_layernorm(x, axis=-1), edge_index, L1_gnn_W, L1_gnn_att_src, L1_gnn_att_dst, L1_gnn_bias)
    x = x + _L1_ffn_ref(_layernorm(x, axis=-1)[None], L1_ffn_Wr, L1_ffn_br, L1_ffn_W1, L1_ffn_b1, L1_ffn_W2, L1_ffn_b2, L1_ffn_gamma, L1_ffn_beta)[0]
    return x

_drawn_inputs = setup_inputs


def setup_inputs(seed=0):
    import zlib

    import numpy as np

    out = dict(_drawn_inputs(seed))
    spreads = {'L0_ffn_gate_b': (0.0, 0.281),
     'L0_ffn_b1': (0.0, 0.8),
     'L0_ffn_b2': (0.0, 0.1),
     'L0_ffn_gamma': (1.0, 0.2),
     'L0_ffn_beta': (0.0, 0.1),
     'L1_ffn_br': (0.0, 0.1),
     'L1_ffn_b1': (0.0, 0.613),
     'L1_ffn_b2': (0.0, 0.449),
     'L1_ffn_gamma': (1.0, 0.2),
     'L1_ffn_beta': (0.0, 0.286)}
    factors = {'L1_gnn_att_dst': 3.182, 'L1_gnn_bias': 8.0}
    for name, (base, spread) in spreads.items():
        noise = np.random.default_rng([zlib.crc32(name.encode()), seed]).standard_normal(out[name].shape)
        drawn = base * np.exp(spread * noise) if base else spread * noise
        out[name] = jnp.asarray(drawn.astype(out[name].dtype))
    for name, factor in factors.items():
        out[name] = (out[name] * factor).astype(out[name].dtype)
    return out
```

```python
from contextlib import ExitStack

import concourse.bass as bass
from concourse import mybir

ALU = mybir.AluOpType
ACT = mybir.ActivationFunctionType
AX = mybir.AxisListType
F32 = mybir.dt.float32
BF16 = mybir.dt.bfloat16
I32 = mybir.dt.int32

P = 128
N = 3125
D = 256
NT = -(-N // P)
LAST = N - (NT - 1) * P
NPAD = NT * P
E = 50000
GT = 4
GE = GT * P
NG = -(-E // GE)
HEADS = 4
C = D // HEADS
NB32 = NPAD // 32
F = 512
DC, FC = D // P, F // P
E0 = 16
E1 = 8
WT = (2 * N + E0 * (P - 1)) // P
SLOTS = WT * P
NEG = -1.0e30
LN_EPS = 1e-5
MSG = D + HEADS
CAPACITY = float(-(-N * 125 // (100 * E1)))


def cols(i, width, offset=0):
    return bass.ds(i * width + offset, width)


def tiles2(eng, count, body):
    with eng.Fori(0, count // 2) as i:
        body(i * 2, 0, i)
        body(i * 2 + 1, 1, i)
    if count % 2:
        body(count - 1, 0, count // 2)


class Done:

    def __init__(self, eng, sem, base=0):
        self.eng, self.sem, self.base, self.n = eng, sem, base, 0

    def __call__(self, ins, wait=True):
        self.n += 1
        ins.then_inc(self.sem, 1)
        if wait:
            self.eng.wait_ge(self.sem, self.base + self.n)


def program(nc, x, src_cols, dst_cols, dst_rows, w_self, w_neigh, gate_w, gate_b, w1, b1, w2, b2, g0, be0,
            gat_w, att_src, att_dst, gat_bias, wr, br, w1b, b1b, w2b, b2b, g1, be1, out):
    with ExitStack() as ctx:
        sems = [0]

        def sem(scope, name):
            sems[0] += 1
            return scope.enter_context(nc.semaphore(f"{name}_{sems[0]}"))

        def sb(scope, name, shape, dt=F32):
            return scope.enter_context(nc.sbuf_tensor(name, shape, dt))

        def ps(scope, name, width=512):
            return scope.enter_context(nc.psum_tensor(name, [P, width], F32))

        def dram(name, shape, dt=F32):
            return nc.dram_tensor(name, shape, dt).ap()

        t_neigh = dram("t_neigh", [NPAD, D])
        t_ranges = dram("t_ranges", [NG, 4], I32)
        t_xn = dram("t_xn", [NPAD, D])
        t_moe = dram("t_moe", [SLOTS, D])
        t_gat = dram("t_gat", [NPAD, MSG])
        t_as = dram("t_as", [NPAD, HEADS])

        X = sb(ctx, "X", [P, NT * D])
        ident = sb(ctx, "ident", [P, P])
        iota = sb(ctx, "iota", [P, P])
        block_neg = sb(ctx, "block_neg", [P, NT])
        node_id = sb(ctx, "node_id", [P, NT])
        src_i = sb(ctx, "src_i", [P, NG * GT], I32)
        dst_f = sb(ctx, "dst_f", [P, NG * GT])
        ranges = sb(ctx, "ranges", [1, NG * 4], I32)
        stats = sb(ctx, "stats", [P, 5 * 6])
        mv = sb(ctx, "mv", [P, NT * 2])
        mv5 = sb(ctx, "mv5", [P, 10])
        rstd = sb(ctx, "rstd", [P, NT])
        ones_row = sb(ctx, "ones_row", [1, P])
        psum = [ps(ctx, f"bank{i}") for i in range(8)]

        s_hold = sem(ctx, "hold")

        def hold(eng):
            eng.sem_inc(s_hold, 1)

        def norm_stats(dve, done, src, roots):
            s = done.base + done.n
            with dve.Fori(0, NT // 5) as i:
                for k in range(5):
                    ins = dve.bn_stats(stats[:, k * 6:k * 6 + 6], src[:, cols(i * 5 + k, D)])
                    ins.then_inc(done.sem, 1)
                dve.wait_ge(done.sem, i * 11 + (s + 5))
                hold(dve)
                for k in range(5):
                    ins = dve.bn_aggr(mv5[:, k * 2:k * 2 + 2], stats[:, k * 6:k * 6 + 6])
                    ins.then_inc(done.sem, 1)
                dve.wait_ge(done.sem, i * 11 + (s + 10))
                dve.tensor_copy(mv[:, cols(i, 10)], mv5[:]).then_inc(done.sem, 1)
                dve.wait_ge(done.sem, i * 11 + (s + 11))
            done.n += 2 * NT + NT // 5
            asked, given = roots
            dve.tensor_scalar(rstd[:], mv[:, 1:2 * NT:2], LN_EPS, None, ALU.add).then_inc(asked, 1)
            dve.wait_ge(given, 1)
            done(dve.reciprocal(rstd[:], rstd[:]))

        def take_roots(act, roots):
            asked, given = roots
            act.wait_ge(asked, 1)
            act.activation(rstd[:], rstd[:], ACT.Sqrt).then_inc(given, 1)

        def root_sems(st):
            return sem(st, "variance_ready"), sem(st, "root_ready")

        def normalised(dve, dst, src, n):
            return dve.tensor_scalar(dst, src[:, cols(n, D)], mv[:, bass.ds(n * 2, 1)], rstd[:, bass.ds(n, 1)],
                                     ALU.subtract, ALU.mult)

        def norm_onto_x(dve, done, y, tmp, gb, n):
            done(normalised(dve, tmp[:], y, n))
            done(dve.tensor_tensor(tmp[:], tmp[:], gb[:, 0:D], ALU.mult))
            done(dve.tensor_tensor(tmp[:], tmp[:], gb[:, D:2 * D], ALU.add))
            done(dve.tensor_tensor(X[:, cols(n, D)], X[:, cols(n, D)], tmp[:], ALU.add))

        with ExitStack() as st, nc.Block() as block:
            dst_i = sb(st, "dst_i", [P, NG * GT], I32)
            rows_i = sb(st, "rows_i", [NG, GE], I32)
            rng = sb(st, "rng", [NG, 4], I32)
            ids = sb(st, "ids", [P, P], I32)
            s_tail = sem(st, "tail_zeroed")
            s_ld = sem(st, "loaded")
            s_dv = sem(st, "dve_done")
            s_po = sem(st, "pool_done")
            s_rng = sem(st, "ranges_ready")
            s_rst = sem(st, "ranges_stored")
            s_rld = sem(st, "ranges_loaded")

            @block.sync
            def _(sp):
                sp.dma_start(rows_i[:], dst_rows).then_inc(s_ld, 16)
                sp.dma_start(dst_i[:], dst_cols).then_inc(s_ld, 16)
                sp.dma_start(src_i[:], src_cols).then_inc(s_ld, 16)
                sp.dma_start(X[:, 0:(NT - 1) * D].rearrange("p (t d) -> p t d", d=D),
                             x[0:(NT - 1) * P, :].rearrange("(t p) d -> p t d", p=P)).then_inc(s_ld, 16)
                sp.wait_ge(s_tail, 1)
                sp.dma_start(X[0:LAST, (NT - 1) * D:NT * D], x[(NT - 1) * P:N, :]).then_inc(s_ld, 16)
                sp.wait_ge(s_rng, 1)
                sp.dma_start(t_ranges, rng[:]).then_inc(s_rst, 16)
                sp.wait_ge(s_rst, 16)
                sp.dma_start(ranges[:], t_ranges.rearrange("(a g) f -> a (g f)", a=1)).then_inc(s_rld, 16)
                sp.wait_ge(s_rld, 16)
                sp.wait_ge(s_ld, 80)

            @block.gpsimd
            def _(pool):
                done = Done(pool, s_po)
                done(pool.memset(ident[:], 0.0))
                done(pool.affine_select(out=ident[:], in_=ident[:], compare_op=ALU.not_equal, fill=1.0, base=0,
                                        pattern=[[-1, P]], channel_multiplier=1))
                for dst, step, per_partition in ((iota, 1, 0), (node_id, P, 1), (block_neg, -P, 0)):
                    wide = dst.shape[1]
                    done(pool.iota(ids[:, 0:wide], pattern=[[step, wide]], base=0, channel_multiplier=per_partition))
                    done(pool.tensor_copy(dst[:], ids[:, 0:wide]))
                done(pool.memset(ones_row[:], 1.0))

            @block.vector
            def _(dve):
                done = Done(dve, s_dv)
                dve.memset(X[:, (NT - 1) * D:NT * D], 0.0).then_inc(s_tail, 1)
                dve.wait_ge(s_ld, 80)
                done(dve.tensor_copy(dst_f[:], dst_i[:]))
                done(dve.tensor_reduce(rng[:, 0:1], rows_i[:], AX.X, ALU.min))
                done(dve.tensor_reduce(rng[:, 1:2], rows_i[:], AX.X, ALU.max))
                done(dve.tensor_single_scalar(rng[:, 2:4], rng[:, 0:2], 5, ALU.arith_shift_right))
                done(dve.tensor_single_scalar(rng[:, 0:2], rng[:, 0:2], 7, ALU.arith_shift_right))
                done(dve.tensor_scalar(rng[:, 1:2], rng[:, 1:2], 1.0, None, ALU.add))
                dve.tensor_scalar(rng[:, 3:4], rng[:, 3:4], 1.0, None, ALU.add).then_inc(s_rng, 1)

        def transposer(pe, ready, n, xn, bank, landed):
            pe.wait_ge(ready, n + 1)
            pe.transpose(bank[:, 0:P], xn[:, 0:P], ident[:])
            pe.transpose(bank[:, P:2 * P], xn[:, P:2 * P], ident[:]).then_inc(landed, 1)

        with ExitStack() as st, nc.Block() as block:
            W = sb(st, "W_l0", [P, DC * 512])
            HS = sb(st, "HS", [P, NT * D])
            xn = [sb(st, f"xn_a{s}", [P, D]) for s in range(2)]
            xT = [sb(st, f"xT_a{s}", [P, D]) for s in range(2)]
            top = sb(st, "top", [P, 8])
            work = sb(st, "work", [P, D])
            s_w = sem(st, "weights")
            s_dv = sem(st, "dve_done")
            s_tk = sem(st, "top_done")
            s_xn = sem(st, "xn_ready")
            s_tp = sem(st, "turned")
            s_xt = sem(st, "xT_ready")
            s_mm = sem(st, "projected")
            s_hs = sem(st, "sparse_ready")
            s_st = sem(st, "table_stored")
            roots = root_sems(st)

            @block.sync
            def _(sp):
                wv = W[:].rearrange("p (c n) -> p c n", c=DC)
                sp.dma_start(wv[:, :, 0:D], w_self.rearrange("(c p) n -> p c n", p=P)).then_inc(s_w, 16)
                sp.dma_start(wv[:, :, D:2 * D], w_neigh.rearrange("(c p) n -> p c n", p=P)).then_inc(s_w, 16)

                def store(n, s, i):
                    sp.wait_ge(s_hs, n + 1)
                    sp.dma_start(t_neigh[bass.ds(n * P, P), :], HS[:, cols(n, D)]).then_inc(s_st, 16)

                tiles2(sp, NT, store)
                sp.wait_ge(s_st, 16 * NT)

            @block.vector
            def _(dve):
                norm_stats(dve, Done(dve, s_dv), X, roots)
                normalised(dve, xn[0][:], X, 0).then_inc(s_xn, 1)
                links = 9

                def tile(n, s, i):
                    dve.wait_ge(s_mm, n + 1)
                    if not (isinstance(n, int) and n == NT - 1):
                        normalised(dve, xn[1 - s][:], X, n + 1).then_inc(s_xn, 1)
                    h = psum[2 + s]
                    done = Done(dve, s_tk, n * links)
                    done(dve.tensor_tensor(X[:, cols(n, D)], X[:, cols(n, D)], h[:, 0:D], ALU.add), wait=False)
                    for r in range(4):
                        left = h[:, D:2 * D] if r == 0 else work[:]
                        done(dve.max(top[:], left))
                        hold(dve)
                        done(dve.match_replace(work[:], top[:], left, NEG))
                        if r < 3:
                            hold(dve)
                    dve.scalar_tensor_tensor(HS[:, cols(n, D)], work[:], NEG, h[:, D:2 * D], ALU.is_equal,
                                             ALU.mult).then_inc(s_hs, 1)

                tiles2(dve, NT, tile)

            @block.scalar
            def _(act):
                take_roots(act, roots)

                def turn(n, s, i):
                    act.wait_ge(s_tp, n + 1)
                    act.copy(xT[s][:], psum[s][:, 0:D]).then_inc(s_xt, 1)

                tiles2(act, NT, turn)

            @block.tensor
            def _(pe):
                pe.wait_ge(s_w, 32)

                def project(n, s, i):
                    transposer(pe, s_xn, n, xn[s], psum[s], s_tp)
                    pe.wait_ge(s_xt, n + 1)
                    for c in range(DC):
                        mm = pe.matmul(psum[2 + s][:], xT[s][:, c * P:(c + 1) * P], W[:, c * 512:(c + 1) * 512],
                                       start=(c == 0), stop=(c == DC - 1))
                    mm.then_inc(s_mm, 1)

                tiles2(pe, NT, project)

        def gather_groups(pool, sems_, table, idx, into, width, pitch):
            s_free, s_ix, s_arr = sems_

            def group(g, s, i):
                pool.wait_ge(s_free, g + 1)
                pool.tensor_copy(idx[s][:], src_i[:, cols(g, GT)]).then_inc(s_ix, 1)
                pool.wait_ge(s_ix, g + 1)
                hold(pool)
                for k in range(GT):
                    pool.indirect_dma_start(
                        into[s][:, k * pitch:k * pitch + width], None, table,
                        bass.IndirectOffsetOnAxis(ap=idx[s][:, k:k + 1], axis=0)).then_inc(s_arr[s], 16)

            tiles2(pool, NG, group)

        def block_range(eng, g, which):
            blocks = NB32 if which else NT
            lo = eng.value_load(ranges[0:1, bass.ds(g * 4 + which, 1)], min_val=0, max_val=blocks - 1)
            hi = eng.value_load(ranges[0:1, bass.ds(g * 4 + which + 1, 1)], min_val=1, max_val=blocks)
            return lo, hi

        with ExitStack() as st, nc.Block() as block:
            AW = D + 1
            acc = sb(st, "acc0", [P, NT * AW])
            G = [sb(st, f"G0_{s}", [P, GT * AW]) for s in range(2)]
            idx = [sb(st, f"idx0_{s}", [P, GT], I32) for s in range(2)]
            S = sb(st, "S0", [P, GE])
            deg = sb(st, "deg", [P, NT])
            s_dv = sem(st, "dve_done")
            s_free = sem(st, "rows_free")
            s_ix = sem(st, "idx_ready")
            s_arr = [sem(st, f"rows_arrived{s}") for s in range(2)]
            s_ones = sem(st, "ones_ready")
            s_sel = sem(st, "selector_ready")
            s_mm = sem(st, "summed")
            s_acc = sem(st, "added")

            @block.gpsimd
            def _(pool):
                gather_groups(pool, (s_free, s_ix, s_arr), t_neigh, idx, G, D, AW)

            @block.vector
            def _(dve):
                done = Done(dve, s_dv)
                dve.sem_inc(s_free, 2)
                for s in range(2):
                    ones = G[s][:].rearrange("p (k w) -> p k w", k=GT)[:, :, D:AW]
                    dve.memset(ones, 1.0).then_inc(s_ones, 1)
                done(dve.memset(acc[:], 0.0))
                item = dve.alloc_register("dve_item0")
                dve.reg_mov(item, 0)

                def group(g, s, i):
                    lo, hi = block_range(dve, g, 0)
                    with dve.Fori(lo, hi) as b:
                        w = dve.snap(item)
                        for k in range(GT):
                            ins = dve.tensor_scalar(S[:, k * P:(k + 1) * P], iota[:], dst_f[:, bass.ds(g * GT + k, 1)],
                                                    block_neg[:, bass.ds(b, 1)], ALU.subtract, ALU.is_equal)
                        ins.then_inc(s_sel, 1)
                        dve.wait_ge(s_mm, w + 1)
                        dve.tensor_tensor(acc[:, cols(b, AW)], acc[:, cols(b, AW)], psum[0][:, 0:AW],
                                          ALU.add).then_inc(s_acc, 1)
                        dve.wait_ge(s_acc, w + 1)
                        dve.reg_add(item, item, 1)
                    dve.sem_inc(s_free, 1)

                tiles2(dve, NG, group)
                count = acc[:].rearrange("p (t w) -> p t w", w=AW)[:, :, D]
                done(dve.tensor_scalar(deg[:], count, 1.0, None, ALU.max))
                done(dve.reciprocal(deg[:], deg[:]))

                def mean(n, s, i):
                    dve.scalar_tensor_tensor(X[:, cols(n, D)], acc[:, bass.ds(n * AW, D)], deg[:, bass.ds(n, 1)],
                                             X[:, cols(n, D)], ALU.mult, ALU.add)

                tiles2(dve, NT, mean)

            @block.tensor
            def _(pe):
                item = pe.alloc_register("pe_item0")
                pe.reg_mov(item, 0)
                pe.wait_ge(s_ones, 2)

                def group(g, s, i):
                    lo, hi = block_range(pe, g, 0)
                    with pe.Fori(lo, hi):
                        w = pe.snap(item)
                        pe.wait_ge(s_arr[s], i * (16 * GT) + 16 * GT)
                        pe.wait_ge(s_sel, w + 1)
                        for k in range(GT):
                            mm = pe.matmul(psum[0][:, 0:AW], S[:, k * P:(k + 1) * P], G[s][:, k * AW:(k + 1) * AW],
                                           start=(k == 0), stop=(k == GT - 1))
                        mm.then_inc(s_mm, 1)
                        pe.reg_add(item, item, 1)

                tiles2(pe, NG, group)

        if PHASES < 3:
            return store_out(nc, sem, X, out)

        ffn0 = ctx.enter_context(ExitStack())
        XN = sb(ffn0, "XN", [P, NT * D])
        mix = sb(ffn0, "mix", [P, 2 * NT])
        place = sb(ffn0, "place", [P, 2 * NT], I32)
        token = sb(ffn0, "token", [P, WT], I32)
        tile_e = sb(ffn0, "tile_e", [P, WT], I32)
        tile_hot = sb(ffn0, "tile_hot", [E0, WT])
        with ExitStack() as st, nc.Block() as block:
            TE = NT * E0
            gw = sb(st, "gw", [P, DC * E0])
            gb = sb(st, "gb", [1, E0])
            xn = [sb(st, f"xn_b{s}", [P, D]) for s in range(2)]
            xT = [sb(st, f"xT_b{s}", [P, D]) for s in range(2)]
            L = sb(st, "L", [P, TE])
            cand = sb(st, "cand", [P, TE])
            M = [sb(st, f"M{j}", [P, TE]) for j in range(2)]
            Mb = sb(st, "Mb", [P, TE], BF16)
            tot = sb(st, "tot", [P, TE])
            scan = [sb(st, f"scan{j}", [P, TE]) for j in range(2)]
            val = [sb(st, f"val{j}", [P, NT]) for j in range(2)]
            best = sb(st, "best", [P, NT])
            real = sb(st, "real", [P, NT])
            pos_i = sb(st, "pos_i", [P, 2 * NT], I32)
            pos_w = sb(st, "pos_w", [P, 2 * NT])
            pos_r = sb(st, "pos_r", [P, 2 * NT])
            hot_r = [sb(st, f"hot_r{c}", [P, P], BF16) for c in range(2)]
            hot_w = [sb(st, f"hot_w{c}", [P, 2 * WT], BF16) for c in range(2)]
            pos = sb(st, "pos", [P, 2 * NT])
            et = [sb(st, f"et{j}", [P, E0]) for j in range(3)]
            ni = sb(st, "ni", [P, E0], I32)
            cmp = sb(st, "cmp", [P, WT * E0])
            te_f = sb(st, "te_f", [P, WT])
            upper = sb(st, "upper", [P, P], BF16)
            ones_b = sb(st, "ones_b", [P, P], BF16)
            s_w = sem(st, "weights")
            s_dv = sem(st, "dve_done")
            s_po = sem(st, "pool_done")
            s_xn = sem(st, "xn_ready")
            s_tp = sem(st, "turned")
            s_xt = sem(st, "xT_ready")
            s_xc = sem(st, "XN_kept")
            s_mm = sem(st, "logits_done")
            s_mb = sem(st, "choice_ready")
            s_rk = sem(st, "ranked")
            s_e = sem(st, "exp_in")
            s_ex = sem(st, "exp_out")
            s_hot = sem(st, "hot_ready")
            s_inv = sem(st, "inverted")
            s_st = sem(st, "rows_stored")
            roots = root_sems(st)

            @block.sync
            def _(sp):
                sp.dma_start(gw[:].rearrange("p (c n) -> p c n", c=DC),
                             gate_w.rearrange("(c p) n -> p c n", p=P)).then_inc(s_w, 16)
                sp.dma_start(gb[:], gate_b.rearrange("(a n) -> a n", a=1)).then_inc(s_w, 16)

                def store(n, s, i):
                    sp.wait_ge(s_xc, n + 1)
                    sp.dma_start(t_xn[bass.ds(n * P, P), :], XN[:, cols(n, D)]).then_inc(s_st, 16)

                tiles2(sp, NT, store)
                sp.wait_ge(s_st, 16 * NT)

            @block.gpsimd
            def _(pool):
                done = Done(pool, s_po)
                pool.memset(ones_b[:], 1.0).then_inc(s_po, 1)
                done.n += 1
                done(pool.memset(upper[:], 1.0))
                done(pool.affine_select(out=upper[:], in_=upper[:], compare_op=ALU.is_gt, fill=0.0, base=0,
                                        pattern=[[1, P]], channel_multiplier=-1))

            @block.vector
            def _(dve):
                done = Done(dve, s_dv)
                norm_stats(dve, done, X, roots)
                done(normalised(dve, xn[0][:], X, 0), wait=False)
                base = done.base + done.n - 1

                def tile(n, s, i):
                    dve.wait_ge(s_mm, n + 1)
                    dve.wait_ge(s_xc, n + 1)
                    if not (isinstance(n, int) and n == NT - 1):
                        normalised(dve, xn[1 - s][:], X, n + 1).then_inc(s_dv, 1)

                tiles2(dve, NT, tile)
                done.n = base + NT
                dve.wait_ge(s_mm, NT)

                def te(t):
                    return t.rearrange("p (t e) -> p t e", e=E0)

                def per_token(t):
                    return t.unsqueeze(2).broadcast_to([P, NT, E0])

                def per_expert(t):
                    return t.unsqueeze(1).broadcast_to([P, NT, E0])

                e_id = iota[:, 0:E0]
                done(dve.tensor_copy(L[:], psum[2][:, 0:TE]))
                done(dve.tensor_scalar(real[:], node_id[:], float(N), None, ALU.is_lt), wait=False)
                for j in range(2):
                    done(dve.tensor_reduce(val[j][:], te(L[:]), AX.X, ALU.max))
                    done(dve.tensor_tensor(te(cand[:]), te(L[:]), per_token(val[j][:]), ALU.is_ge))
                    done(dve.scalar_tensor_tensor(te(cand[:]), te(cand[:]), -1000.0, per_expert(e_id),
                                                  ALU.mult, ALU.add))
                    done(dve.tensor_reduce(best[:], te(cand[:]), AX.X, ALU.min))
                    done(dve.tensor_tensor(te(M[j][:]), te(cand[:]), per_token(best[:]), ALU.is_equal))
                    if j == 0:
                        done(dve.scalar_tensor_tensor(L[:], M[0][:], NEG, L[:], ALU.mult, ALU.add))
                dve.tensor_tensor(best[:], val[1][:], val[0][:], ALU.subtract).then_inc(s_e, 1)
                for j in range(2):
                    done(dve.tensor_tensor(te(M[j][:]), te(M[j][:]), per_token(real[:]), ALU.mult))
                dve.tensor_tensor(Mb[:], M[0][:], M[1][:], ALU.add).then_inc(s_mb, 1)
                dve.wait_ge(s_ex, 1)
                done(dve.tensor_scalar(val[1][:], val[0][:], 1.0, None, ALU.add))
                done(dve.reciprocal(mix[:, 0:NT], val[1][:]))
                done(dve.tensor_tensor(mix[:, NT:2 * NT], mix[:, 0:NT], val[0][:], ALU.mult))
                dve.wait_ge(s_rk, 1)
                done(dve.tensor_copy(tot[:], psum[4][:, 0:TE]))
                at, step = tot, 1
                for r in range(5):
                    to = scan[r % 2]
                    w = step * E0
                    done(dve.tensor_copy(to[:, 0:w], at[:, 0:w]))
                    done(dve.tensor_tensor(to[:, w:TE], at[:, w:TE], at[:, 0:TE - w], ALU.add))
                    at, step = to, step * 2
                done(dve.tensor_scalar(ni[:], at[:, TE - E0:TE], float(P - 1), None, ALU.add))
                done(dve.tensor_single_scalar(ni[:], ni[:], 7, ALU.arith_shift_right))
                done(dve.tensor_copy(et[2][:], ni[:]))
                cur, step = et[2], 1
                for r in range(4):
                    to = et[r % 2]
                    done(dve.tensor_copy(to[:, 0:step], cur[:, 0:step]))
                    done(dve.tensor_tensor(to[:, step:E0], cur[:, step:E0], cur[:, 0:E0 - step], ALU.add))
                    cur, step = to, step * 2
                start = et[0]
                assert cur is et[1] and at is scan[0]
                done(dve.tensor_tensor(start[:], cur[:], et[2][:], ALU.subtract))
                slot = scan[1]
                done(dve.tensor_tensor(slot[:], at[:], tot[:], ALU.subtract))
                done(dve.tensor_tensor(slot[:], slot[:], psum[3][:, 0:TE], ALU.add))
                done(dve.scalar_tensor_tensor(te(slot[:]), per_expert(start[:]), float(P), te(slot[:]),
                                              ALU.mult, ALU.add))
                for j in range(2):
                    done(dve.tensor_tensor(cand[:], M[j][:], slot[:], ALU.mult))
                    done(dve.tensor_reduce(pos[:, j * NT:(j + 1) * NT], te(cand[:]), AX.X, ALU.add))
                done(dve.tensor_copy(place[:], pos[:]))
                done(dve.tensor_scalar(best[:], real[:], 1.0, None, ALU.subtract))
                for j in range(2):
                    done(dve.tensor_tensor(pos[:, j * NT:(j + 1) * NT], pos[:, j * NT:(j + 1) * NT], best[:],
                                           ALU.add))
                done(dve.tensor_copy(pos_i[:], pos[:]))
                done(dve.tensor_single_scalar(pos_i[:], pos_i[:], 7, ALU.arith_shift_right))
                done(dve.tensor_copy(pos_w[:], pos_i[:]))
                done(dve.scalar_tensor_tensor(pos_r[:], pos_w[:], -float(P), pos[:], ALU.mult, ALU.add))

                def hot(t, c):
                    j = bass.ds(t + c * NT, 1)
                    dve.tensor_scalar(hot_r[c][:], iota[:], pos_r[:, j], None, ALU.is_equal)
                    dve.tensor_scalar(hot_w[c][:, 0:WT], iota[:, 0:WT], pos_w[:, j], node_id[:, 0:1],
                                      ALU.is_equal, ALU.mult)
                    dve.tensor_scalar(hot_w[c][:, WT:2 * WT], iota[:, 0:WT], pos_w[:, j], iota[:, bass.ds(t, 1)],
                                      ALU.is_equal, ALU.mult).then_inc(s_hot, 1)

                for c in range(2):
                    hot(0, c)
                with dve.Fori(1, NT) as t:
                    for c in range(2):
                        dve.wait_ge(s_inv, t * 2 + (c - 1))
                        hot(t, c)
                dve.wait_ge(s_inv, 2 * NT)
                done(dve.tensor_copy(te_f[:], psum[5][:, 0:WT]))
                done(dve.scalar_tensor_tensor(te_f[:], psum[5][:, WT:2 * WT], float(P), te_f[:], ALU.mult, ALU.add))
                done(dve.tensor_copy(token[:], te_f[:]))
                done(dve.tensor_tensor(cmp[:].rearrange("p (w e) -> p w e", e=E0),
                                       iota[:, 0:WT].unsqueeze(2).broadcast_to([P, WT, E0]),
                                       cur[:].unsqueeze(1).broadcast_to([P, WT, E0]), ALU.is_ge))
                done(dve.tensor_reduce(te_f[:], cmp[:].rearrange("p (w e) -> p w e", e=E0), AX.X, ALU.add))
                done(dve.tensor_scalar(te_f[:], te_f[:], float(E0 - 1), None, ALU.min))
                done(dve.tensor_copy(tile_e[:], te_f[:]))
                done(dve.tensor_scalar(tile_hot[:], te_f[0:E0, :], node_id[0:E0, 0:1], None, ALU.is_equal))

            @block.scalar
            def _(act):
                take_roots(act, roots)

                def turn(n, s, i):
                    act.wait_ge(s_tp, n + 1)
                    act.copy(xT[s][:], psum[s][:, 0:D]).then_inc(s_xt, 1)
                    act.copy(XN[:, cols(n, D)], xn[s][:]).then_inc(s_xc, 1)

                tiles2(act, NT, turn)
                act.wait_ge(s_e, 1)
                act.activation(val[0][:], best[:], ACT.Exp).then_inc(s_ex, 1)

            @block.tensor
            def _(pe):
                pe.wait_ge(s_w, 32)
                first = 2 * NT + NT // 5 + 1

                def logits(n, s, i):
                    pe.wait_ge(s_dv, n + (first + 1))
                    pe.transpose(psum[s][:, 0:P], xn[s][:, 0:P], ident[:])
                    pe.transpose(psum[s][:, P:2 * P], xn[s][:, P:2 * P], ident[:]).then_inc(s_tp, 1)
                    pe.wait_ge(s_xt, n + 1)
                    at = psum[2][:, cols(n, E0)]
                    for c in range(DC):
                        pe.matmul(at, xT[s][:, c * P:(c + 1) * P], gw[:, c * E0:(c + 1) * E0],
                                  start=(c == 0), stop=False, skip_group_check=True)
                    pe.matmul(at, ones_row[:], gb[:], start=False, stop=True, skip_group_check=True).then_inc(s_mm, 1)

                tiles2(pe, NT, logits)
                pe.wait_ge(s_mb, 1)
                pe.wait_ge(s_po, 3)
                pe.matmul(psum[3][:, 0:TE], upper[:], Mb[:], start=True, stop=True)
                pe.matmul(psum[4][:, 0:TE], ones_b[:], Mb[:], start=True, stop=True).then_inc(s_rk, 1)

                def invert(t, c, start=False, stop=False):
                    pe.wait_ge(s_hot, t * 2 + (c + 1))
                    pe.matmul(psum[5][:, 0:2 * WT], hot_r[c][:], hot_w[c][:], start=start, stop=stop).then_inc(s_inv, 1)

                invert(0, 0, start=True)
                invert(0, 1)
                with pe.Fori(1, NT - 1) as t:
                    invert(t, 0)
                    invert(t, 1)
                invert(NT - 1, 0)
                invert(NT - 1, 1, stop=True)

        def expert_pipeline(block, st, items, func, load_in, weights, bias_sel, take_out, dve_first, dve_start,
                            dve_end, act_end):
            xT = [sb(st, f"xT_f{items}_{s}", [P, D]) for s in range(2)]
            h = [sb(st, f"h_f{items}_{s}", [P, F]) for s in range(2)]
            hT = [sb(st, f"hT_f{items}_{s}", [P, F]) for s in range(2)]
            s_tp, s_xt, s_h, s_hr, s_ht, s_hc, s_y, s_yo = (
                sem(st, n) for n in ("turned", "xT_ready", "hidden", "act_done", "h_turned", "hT_ready", "result", "taken"))

            @block.tensor
            def _(pe):
                def turn(w, s, i):
                    tile = load_in(pe, w, s, i)
                    pe.transpose(psum[s][:, 0:P], tile[:, 0:P], ident[:])
                    pe.transpose(psum[s][:, P:2 * P], tile[:, P:2 * P], ident[:]).then_inc(s_tp, 1)

                def up(w, s, ww):
                    pe.wait_ge(s_xt, w + 1)
                    for c in range(DC):
                        pe.matmul(psum[2 + s][:], xT[s][:, c * P:(c + 1) * P], ww[0](c), start=(c == 0), stop=False)
                    sel, bias = bias_sel(s, 0)
                    pe.matmul(psum[2 + s][:], sel, bias, start=False, stop=True).then_inc(s_h, 1)

                def turn_h(w, s):
                    pe.wait_ge(s_hr, w + 1)
                    for c in range(FC):
                        mm = pe.transpose(psum[4 + s][:, c * P:(c + 1) * P], h[s][:, c * P:(c + 1) * P], ident[:])
                    mm.then_inc(s_ht, 1)

                def down(w, s, ww):
                    pe.wait_ge(s_hc, w + 1)
                    for c in range(FC):
                        pe.matmul(psum[6 + s][:, 0:D], hT[s][:, c * P:(c + 1) * P], ww[1](c), start=(c == 0), stop=False)
                    sel, bias = bias_sel(s, 1)
                    pe.matmul(psum[6 + s][:, 0:D], sel, bias, start=False, stop=True).then_inc(s_y, 1)

                weights_of = weights(pe)
                turn(0, 0, 0)
                turn(1, 1, 0)
                up(0, 0, weights_of(0, 0))
                turn_h(0, 0)
                with pe.Fori(0, (items - 2) // 2) as i:
                    for j in (0, 1):
                        turn(i * 2 + (2 + j), j, i + 1)
                        up(i * 2 + (1 + j), 1 - j, weights_of(i * 2 + (1 + j), 1 - j))
                        down(i * 2 + j, j, weights_of(i * 2 + j, j))
                        turn_h(i * 2 + (1 + j), 1 - j)
                up(items - 1, 1, weights_of(items - 1, 1))
                down(items - 2, 0, weights_of(items - 2, 0))
                turn_h(items - 1, 1)
                pe.wait_ge(s_xt, items + 1)
                down(items - 1, 1, weights_of(items - 1, 1))

            @block.scalar
            def _(act):
                def hidden(w, s, i):
                    act.wait_ge(s_h, w + 1)
                    act.activation(h[s][:], psum[2 + s][:], func).then_inc(s_hr, 1)
                    act.wait_ge(s_ht, w + 1)
                    act.copy(hT[s][:], psum[4 + s][:]).then_inc(s_hc, 1)

                tiles2(act, items, hidden)
                act_end(act)

            @block.vector
            def _(dve):
                dve_start(dve)

                def copy_in(w, s, i):
                    dve.wait_ge(s_tp, w + 1)
                    dve_first(dve, w, s)
                    dve.tensor_copy(xT[s][:], psum[s][:, 0:D]).then_inc(s_xt, 1)

                def result(w, s, i):
                    dve.wait_ge(s_y, w + 1)
                    take_out(dve, w, s, i, psum[6 + s][:, 0:D])

                copy_in(0, 0, 0)
                copy_in(1, 1, 0)
                with dve.Fori(0, (items - 2) // 2) as i:
                    for j in (0, 1):
                        copy_in(i * 2 + (2 + j), j, i + 1)
                        result(i * 2 + j, j, i)
                dve.wait_ge(s_y, items - 2)
                dve_first(dve, items, 0)
                dve.tensor_copy(xT[0][:], xT[0][:]).then_inc(s_xt, 1)
                result(items - 2, 0, items // 2 - 1)
                result(items - 1, 1, items // 2 - 1)
                dve_end(dve)

        with ExitStack() as st, nc.Block() as block:
            W1 = sb(st, "W1", [P, E0 * DC * F])
            W2 = sb(st, "W2", [P, E0 * FC * D])
            B1 = sb(st, "B1", [E0, F])
            B2 = sb(st, "B2", [E0, D])
            xin = [sb(st, f"xin{s}", [P, D]) for s in range(2)]
            yout = [sb(st, f"yout{s}", [P, D]) for s in range(2)]
            sel = [[sb(st, f"sel{j}_{s}", [E0, P]) for s in range(2)] for j in range(2)]
            ti = [sb(st, f"ti{s}", [P, 1], I32) for s in range(2)]
            s_ti = sem(st, "token_copied")
            s_w = sem(st, "weights")
            s_in = [sem(st, f"tile_in{s}") for s in range(2)]
            s_inf = sem(st, "tile_used")
            s_yr = sem(st, "y_ready")
            s_out = sem(st, "y_away")
            s_ys = [sem(st, f"y_stored{s}") for s in range(2)]

            def load_in(pe, w, s, i):
                pe.wait_ge(s_in[s], i * 16 + 16)
                return xin[s]

            def weights(pe):
                pe.wait_ge(s_w, 64)

                def of(w, s):
                    e = pe.value_load(tile_e[0:1, bass.ds(w, 1)], min_val=0, max_val=E0 - 1)
                    return (lambda c: W1[:, bass.ds(e * (DC * F) + c * F, F)],
                            lambda c: W2[:, bass.ds(e * (FC * D) + c * D, D)])

                return of

            def bias_sel(s, which):
                return sel[which][s][:], (B2 if which else B1)[:]

            def dve_first(dve, w, s):
                hold(dve)
                if not (isinstance(w, int) and w == 0):
                    dve.tensor_copy(sel[1][1 - s][:], tile_hot[:, bass.ds(w - 1, 1)].broadcast_to([E0, P]))
                if not (isinstance(w, int) and w == WT):
                    dve.tensor_copy(sel[0][s][:], tile_hot[:, bass.ds(w, 1)].broadcast_to([E0, P])).then_inc(s_inf, 1)

            @block.sync
            def _(sp):
                for half, (dst_, src_) in enumerate(((W1, w1), (W2, w2))):
                    sp.dma_start(dst_[:].rearrange("p (e c f) -> p e c f", e=E0, f=src_.shape[2]),
                                 src_.rearrange("e (c p) f -> p e c f", p=P)).then_inc(s_w, 16)
                sp.dma_start(B1[:], b1).then_inc(s_w, 16)
                sp.dma_start(B2[:], b2).then_inc(s_w, 16)

                def store(w, s, i):
                    sp.wait_ge(s_yr, w + 1)
                    sp.dma_start(t_moe[bass.ds(w * P, P), :], yout[s][:]).then_inc(s_ys[s], 16)
                    sp.wait_ge(s_ys[s], i * 16 + 16)
                    sp.sem_inc(s_out, 1)

                sp.sem_inc(s_out, 2)
                tiles2(sp, WT, store)

            def take_out0(dve, w, s, i, y):
                dve.wait_ge(s_out, w + 1)
                dve.tensor_copy(yout[s][:], y).then_inc(s_yr, 1)

            @block.gpsimd
            def _(pool):
                pool.sem_inc(s_inf, 2)

                def fetch(w, s, i):
                    pool.wait_ge(s_inf, w + 1)
                    pool.tensor_copy(ti[s][:], token[:, bass.ds(w, 1)]).then_inc(s_ti, 1)
                    pool.wait_ge(s_ti, w + 1)
                    hold(pool)
                    pool.indirect_dma_start(xin[s][:], None, t_xn, bass.IndirectOffsetOnAxis(
                        ap=ti[s][:, 0:1], axis=0)).then_inc(s_in[s], 16)

                tiles2(pool, WT, fetch)

            expert_pipeline(block, st, WT, ACT.Relu, load_in, weights, bias_sel, take_out0, dve_first,
                            lambda dve: None, lambda dve: None, lambda act: None)

        with ExitStack() as st, nc.Block() as block:
            Y = [sb(st, f"Y{s}", [P, 2 * D]) for s in range(2)]
            gi = [sb(st, f"gi{s}", [P, 2], I32) for s in range(2)]
            gb = sb(st, "gamma_beta0", [P, 2 * D])
            tmp = sb(st, "tmp_mix", [P, D])
            roots = root_sems(st)
            s_nx = sem(st, "norm_step")
            s_gb = sem(st, "gamma_beta")
            s_free = sem(st, "Y_free")
            s_ix = sem(st, "idx_ready")
            s_arr = [sem(st, f"Y_arrived{s}") for s in range(2)]
            s_dv = sem(st, "dve_done")

            @block.sync
            def _(sp):
                sp.dma_start(gb[:, 0:D], g0.partition_broadcast(P)).then_inc(s_gb, 16)
                sp.dma_start(gb[:, D:2 * D], be0.partition_broadcast(P)).then_inc(s_gb, 16)

            @block.gpsimd
            def _(pool):
                def fetch(n, s, i):
                    pool.wait_ge(s_free, n + 1)
                    for j in range(2):
                        pool.tensor_copy(gi[s][:, j:j + 1], place[:, bass.ds(n + j * NT, 1)]).then_inc(s_ix, 1)
                    pool.wait_ge(s_ix, n * 2 + 2)
                    hold(pool)
                    for j in range(2):
                        pool.indirect_dma_start(
                            Y[s][:, j * D:(j + 1) * D], None, t_moe,
                            bass.IndirectOffsetOnAxis(ap=gi[s][:, j:j + 1], axis=0)).then_inc(s_arr[s], 16)

                tiles2(pool, NT, fetch)

            @block.vector
            def _(dve):
                dve.sem_inc(s_free, 2)
                dve.wait_ge(s_gb, 32)
                def mixed(n, s, i):
                    done = Done(dve, s_dv, n * 2)
                    xt = XN[:, cols(n, D)]
                    dve.wait_ge(s_arr[s], i * 32 + 32)
                    done(dve.scalar_tensor_tensor(xt, Y[s][:, 0:D], mix[:, bass.ds(n, 1)], xt, ALU.mult, ALU.add))
                    done(dve.scalar_tensor_tensor(xt, Y[s][:, D:2 * D], mix[:, bass.ds(n + NT, 1)], xt,
                                                  ALU.mult, ALU.add))
                    dve.sem_inc(s_free, 1)

                tiles2(dve, NT, mixed)
                norm_stats(dve, Done(dve, s_dv, 2 * NT), XN, roots)

                def tile(n, s, i):
                    norm_onto_x(dve, Done(dve, s_nx, n * 4), XN, tmp, gb, n)

                tiles2(dve, NT, tile)

            @block.scalar
            def _(act):
                take_roots(act, roots)

        ffn0.close()
        if PHASES < 4:
            return store_out(nc, sem, X, out)

        gat = ctx.enter_context(ExitStack())
        HL = sb(gat, "HL", [P, NT * MSG])
        AM = sb(gat, "AM", [P, NT * 2 * HEADS])
        with ExitStack() as st, nc.Block() as block:
            WX = MSG + HEADS
            W = sb(st, "W_l1", [P, DC * WX])
            att = sb(st, "att", [P, 2 * D])
            prod = sb(st, "prod", [P, D])
            xn = [sb(st, f"xn_c{s}", [P, D]) for s in range(2)]
            xT = [sb(st, f"xT_c{s}", [P, D]) for s in range(2)]
            s_w = sem(st, "weights")
            s_wx = sem(st, "weights_ready")
            s_dv = sem(st, "dve_done")
            s_xn = sem(st, "xn_ready")
            s_tp = sem(st, "turned")
            s_xt = sem(st, "xT_ready")
            s_mm = sem(st, "projected")
            s_hl = sem(st, "h_ready")
            s_st = sem(st, "stored")
            roots = root_sems(st)

            @block.sync
            def _(sp):
                wv = W[:].rearrange("p (c n) -> p c n", c=DC)
                sp.dma_start(wv[:, :, 0:D], gat_w.rearrange("(c p) n -> p c n", p=P)).then_inc(s_w, 16)
                sp.dma_start(att[:, 0:D], att_src.rearrange("h c -> (h c)").partition_broadcast(P)).then_inc(s_w, 16)
                sp.dma_start(att[:, D:2 * D], att_dst.rearrange("h c -> (h c)").partition_broadcast(P)).then_inc(s_w, 16)

                def store(n, s, i):
                    sp.wait_ge(s_hl, n + 1)
                    sp.dma_start(t_gat[bass.ds(n * P, P), :], HL[:, cols(n, MSG)]).then_inc(s_st, 16)
                    sp.dma_start(t_as[bass.ds(n * P, P), :], HL[:, bass.ds(n * MSG + D, HEADS)]).then_inc(s_st, 16)

                tiles2(sp, NT, store)
                sp.wait_ge(s_st, 32 * NT)

            @block.vector
            def _(dve):
                done = Done(dve, s_dv)
                norm_stats(dve, done, X, roots)
                normalised(dve, xn[0][:], X, 0).then_inc(s_xn, 1)
                dve.wait_ge(s_w, 48)
                for c in range(DC):
                    for j in range(2):
                        done(dve.tensor_tensor(prod[:], W[:, c * WX:c * WX + D], att[:, j * D:(j + 1) * D], ALU.mult))
                        done(dve.tensor_reduce(W[:, c * WX + D + j * HEADS:c * WX + D + (j + 1) * HEADS],
                                               prod[:].rearrange("p (h c) -> p h c", c=C), AX.X, ALU.add))
                dve.sem_inc(s_wx, 1)

                def tile(n, s, i):
                    dve.wait_ge(s_mm, n + 1)
                    if not (isinstance(n, int) and n == NT - 1):
                        normalised(dve, xn[1 - s][:], X, n + 1).then_inc(s_xn, 1)
                    dve.tensor_copy(AM[:, bass.ds(n * 2 * HEADS, HEADS)], psum[2 + s][:, MSG:WX])
                    dve.tensor_copy(HL[:, cols(n, MSG)], psum[2 + s][:, 0:MSG]).then_inc(s_hl, 1)

                tiles2(dve, NT, tile)

            @block.scalar
            def _(act):
                take_roots(act, roots)

                def turn(n, s, i):
                    act.wait_ge(s_tp, n + 1)
                    act.copy(xT[s][:], psum[s][:, 0:D]).then_inc(s_xt, 1)

                tiles2(act, NT, turn)

            @block.tensor
            def _(pe):
                pe.wait_ge(s_wx, 1)

                def project(n, s, i):
                    transposer(pe, s_xn, n, xn[s], psum[s], s_tp)
                    pe.wait_ge(s_xt, n + 1)
                    for c in range(DC):
                        mm = pe.matmul(psum[2 + s][:, 0:WX], xT[s][:, c * P:(c + 1) * P], W[:, c * WX:(c + 1) * WX],
                                       start=(c == 0), stop=(c == DC - 1))
                    mm.then_inc(s_mm, 1)

                tiles2(pe, NT, project)

        with ExitStack() as st, nc.Block() as block:
            GA = [sb(st, f"GA{s}", [P, GT * HEADS]) for s in range(2)]
            idx = [sb(st, f"idx1_{s}", [P, GT], I32) for s in range(2)]
            drow = [sb(st, f"drow{s}", [P, GE], I32) for s in range(2)]
            ga_rep = sb(st, "ga_rep", [P, GT * P])
            id32_i = sb(st, "id32_i", [P, NB32], I32)
            id32 = sb(st, "id32", [P, NB32])
            off = sb(st, "off", [P, GE])
            big = sb(st, "big", [P, GE])
            bmax = sb(st, "bmax", [P, 1])
            macc = sb(st, "macc", [P, NB32])
            mq = sb(st, "mq", [P, NB32])
            MX = sb(st, "MX", [P, HEADS * NT])
            s_po = sem(st, "pool_done")
            s_free = sem(st, "rows_free")
            s_ix = sem(st, "idx_ready")
            s_arr = [sem(st, f"rows_arrived{s}") for s in range(2)]
            s_dr = [sem(st, f"drow_in{s}") for s in range(2)]
            s_rep = sem(st, "replicated")
            s_mm = sem(st, "spread")
            s_dv = sem(st, "dve_done")
            s_it = sem(st, "item_step")
            s_q = sem(st, "max_ready")
            s_mx = sem(st, "max_moved")

            @block.gpsimd
            def _(pool):
                for hd in range(HEADS):
                    pool.iota(id32_i[hd * 32:(hd + 1) * 32, :], pattern=[[32, NB32]], base=0,
                              channel_multiplier=1).then_inc(s_po, 1)
                    pool.wait_ge(s_po, hd + 1)
                gather_groups(pool, (s_free, s_ix, s_arr), t_as, idx, GA, HEADS, HEADS)

            @block.sync
            def _(sp):
                def load(g, s, i):
                    sp.wait_ge(s_free, g + 1)
                    sp.dma_start(drow[s][:], dst_rows[bass.ds(g, 1), :].broadcast_to([P, GE])).then_inc(s_dr[s], 16)

                tiles2(sp, NG, load)
                sp.wait_ge(s_q, 1)
                for hd in range(HEADS):
                    for q in range(4):
                        sp.dma_start(MX[q * 32:(q + 1) * 32, hd * NT:(hd + 1) * NT],
                                     mq[hd * 32:(hd + 1) * 32, q * NT:(q + 1) * NT]).then_inc(s_mx, 16)
                sp.wait_ge(s_mx, 16 * 16)

            @block.scalar
            def _(act):
                def rep(g, s, i):
                    act.wait_ge(s_arr[s], i * (16 * GT) + 16 * GT)
                    act.wait_ge(s_mm, g + 1)
                    act.copy(ga_rep[:].rearrange("p (a r) -> p a r", r=32),
                             GA[s][:].unsqueeze(2).broadcast_to([P, GT * HEADS, 32])).then_inc(s_rep, 1)

                tiles2(act, NG, rep)

            @block.tensor
            def _(pe):
                pe.sem_inc(s_mm, 1)

                def spread(g, s, i):
                    pe.wait_ge(s_rep, g + 1)
                    pe.wait_ge(s_free, g + 1)
                    for k in range(GT):
                        mm = pe.matmul(psum[s][:, k * P:(k + 1) * P], ga_rep[:, k * P:(k + 1) * P], ident[:],
                                       start=True, stop=True)
                    mm.then_inc(s_mm, 1)

                tiles2(pe, NG, spread)

            @block.vector
            def _(dve):
                done = Done(dve, s_dv)
                dve.sem_inc(s_free, 2)
                dve.wait_ge(s_po, 4)
                done(dve.tensor_copy(id32[:], id32_i[:]))
                done(dve.memset(macc[:], NEG))
                item = dve.alloc_register("dve_item1")
                dve.reg_mov(item, 0)

                def group(g, s, i):
                    lo, hi = block_range(dve, g, 2)
                    dve.wait_ge(s_dr[s], i * 16 + 16)
                    dve.wait_ge(s_mm, g + 2)
                    hold(dve)
                    with dve.Fori(lo, hi) as b:
                        w = dve.snap(item)
                        step = Done(dve, s_it, w * 4)
                        step(dve.tensor_scalar(off[:], drow[s][:], id32[:, bass.ds(b, 1)], NEG, ALU.not_equal, ALU.mult))
                        step(dve.tensor_tensor(big[:], off[:], psum[s][:], ALU.add))
                        step(dve.tensor_reduce(bmax[:], big[:], AX.X, ALU.max))
                        step(dve.tensor_tensor(macc[:, bass.ds(b, 1)], macc[:, bass.ds(b, 1)], bmax[:], ALU.max))
                        dve.reg_add(item, item, 1)
                    dve.sem_inc(s_free, 1)

                tiles2(dve, NG, group)
                dve.tensor_copy(mq[:].rearrange("p (q t) -> p q t", q=4),
                                macc[:].rearrange("p (t q) -> p q t", q=4)).then_inc(s_q, 1)
                dve.wait_ge(s_mx, 16 * 16)

                def th(t):
                    return t.rearrange("p (h t) -> p t h", h=HEADS)

                a_src = HL[:].rearrange("p (t w) -> p t w", w=MSG)[:, :, D:MSG]
                am = AM[:].rearrange("p (t w) -> p t w", w=2 * HEADS)
                a_dst, top = am[:, :, 0:HEADS], am[:, :, HEADS:2 * HEADS]
                done(dve.tensor_tensor(top, a_src, th(MX[:]), ALU.max))
                done(dve.tensor_tensor(top, top, a_dst, ALU.add))
                done(dve.scalar_tensor_tensor(top, top, 0.2, top, ALU.mult, ALU.max))

        with ExitStack() as st, nc.Block() as block:
            acc = sb(st, "acc1", [P, NT * MSG])
            G = [sb(st, f"G1_{s}", [P, GT * MSG]) for s in range(2)]
            idx = [sb(st, f"idx2_{s}", [P, GT], I32) for s in range(2)]
            drow = [sb(st, f"drowb{s}", [P, GE], I32) for s in range(2)]
            S = sb(st, "S1", [P, GE])
            T = sb(st, "T1", [P, GE])
            lg = sb(st, "lg", [P, GT * HEADS])
            lr = sb(st, "lr", [P, GT * HEADS])
            am_e = sb(st, "am_e", [P, GT * 2 * HEADS])
            self_w = sb(st, "self_w", [P, NT * HEADS])
            self_l = sb(st, "self_l", [P, NT * HEADS])
            den = sb(st, "den", [P, NT * HEADS])
            bias = sb(st, "gat_bias", [P, D])
            tmp = sb(st, "gat_tmp", [P, D])
            s_free = sem(st, "rows_free")
            s_ix = sem(st, "idx_ready")
            s_arr = [sem(st, f"rows_arrived{s}") for s in range(2)]
            s_dr = [sem(st, f"drow_in{s}") for s in range(2)]
            s_bi = sem(st, "bias_in")
            s_dv = sem(st, "dve_done")
            s_T = sem(st, "T_ready")
            s_am = sem(st, "am_given")
            s_ams = sem(st, "am_step")
            s_lg = sem(st, "logits_ready")
            s_gs = sem(st, "group_step")
            s_ex = sem(st, "weights_ready")
            s_sel = sem(st, "selector_ready")
            s_mm = sem(st, "summed")
            s_acc = sem(st, "added")
            s_self = sem(st, "self_logit")
            s_selfw = sem(st, "self_weight")
            s_fin = sem(st, "final_step")

            @block.gpsimd
            def _(pool):
                gather_groups(pool, (s_free, s_ix, s_arr), t_gat, idx, G, MSG, MSG)

            @block.sync
            def _(sp):
                sp.dma_start(bias[:], gat_bias.partition_broadcast(P)).then_inc(s_bi, 16)

                def load(g, s, i):
                    sp.wait_ge(s_free, g + 1)
                    sp.dma_start(drow[s][:], dst_rows[bass.ds(g, 1), :].broadcast_to([P, GE])).then_inc(s_dr[s], 16)

                tiles2(sp, NG, load)

            @block.scalar
            def _(act):
                act.wait_ge(s_self, 1)
                act.activation(self_w[:], self_l[:], ACT.Exp).then_inc(s_selfw, 1)

                def weigh(g, s, i):
                    act.wait_ge(s_lg, g + 1)
                    act.activation(G[s][:].rearrange("p (k w) -> p k w", w=MSG)[:, :, D:MSG],
                                   lg[:].rearrange("p (k h) -> p k h", h=HEADS), ACT.Exp).then_inc(s_ex, 1)

                tiles2(act, NG, weigh)

            @block.tensor
            def _(pe):
                gave = pe.alloc_register("pe_gave")
                item = pe.alloc_register("pe_item2")
                pe.reg_mov(gave, 0)
                pe.reg_mov(item, 0)

                def group(g, s, i):
                    lo, hi = block_range(pe, g, 0)
                    with pe.Fori(lo, hi) as b:
                        w = pe.snap(gave)
                        pe.wait_ge(s_T, w + 1)
                        for k in range(GT):
                            mm = pe.matmul(psum[1][:, k * 8:(k + 1) * 8], T[:, k * P:(k + 1) * P],
                                           AM[:, cols(b, 2 * HEADS)], start=True, stop=True)
                        mm.then_inc(s_am, 1)
                        pe.reg_add(gave, gave, 1)
                    with pe.Fori(lo, hi):
                        w = pe.snap(item)
                        pe.wait_ge(s_sel, w + 1)
                        for k in range(GT):
                            mm = pe.matmul(psum[0][:, 0:MSG], S[:, k * P:(k + 1) * P], G[s][:, k * MSG:(k + 1) * MSG],
                                           start=(k == 0), stop=(k == GT - 1))
                        mm.then_inc(s_mm, 1)
                        pe.reg_add(item, item, 1)

                tiles2(pe, NG, group)

            @block.vector
            def _(dve):
                done = Done(dve, s_dv)
                dve.sem_inc(s_free, 2)
                am = AM[:].rearrange("p (t w) -> p t w", w=2 * HEADS)
                a_dst, top = am[:, :, 0:HEADS], am[:, :, HEADS:2 * HEADS]
                a_src = HL[:].rearrange("p (t w) -> p t w", w=MSG)[:, :, D:MSG]
                sl = self_l[:].rearrange("p (t h) -> p t h", h=HEADS)
                done(dve.tensor_tensor(sl, a_src, a_dst, ALU.add))
                done(dve.scalar_tensor_tensor(sl, sl, 0.2, sl, ALU.mult, ALU.max))
                dve.tensor_tensor(sl, sl, top, ALU.subtract).then_inc(s_self, 1)
                done(dve.memset(acc[:], 0.0))
                gave = dve.alloc_register("dve_gave")
                item = dve.alloc_register("dve_item2")
                dve.reg_mov(gave, 0)
                dve.reg_mov(item, 0)

                def group(g, s, i):
                    lo, hi = block_range(dve, g, 0)
                    dve.wait_ge(s_dr[s], i * 16 + 16)
                    gs = Done(dve, s_gs, g * 5)
                    gs(dve.memset(am_e[:], 0.0))
                    hold(dve)
                    with dve.Fori(lo, hi) as b:
                        w = dve.snap(gave)
                        dve.tensor_scalar(T[:], drow[s][:], node_id[:, bass.ds(b, 1)], None,
                                          ALU.is_equal).then_inc(s_T, 1)
                        dve.wait_ge(s_am, w + 1)
                        dve.tensor_tensor(am_e[:], am_e[:], psum[1][:, 0:GT * 2 * HEADS], ALU.add).then_inc(s_ams, 1)
                        dve.wait_ge(s_ams, w + 1)
                        dve.reg_add(gave, gave, 1)
                    dve.wait_ge(s_arr[s], i * (16 * GT) + 16 * GT)
                    Gv = G[s][:].rearrange("p (k w) -> p k w", w=MSG)
                    ae = am_e[:].rearrange("p (k w) -> p k w", w=2 * HEADS)
                    lgv = lg[:].rearrange("p (k h) -> p k h", h=HEADS)
                    lrv = lr[:].rearrange("p (k h) -> p k h", h=HEADS)
                    gs(dve.tensor_tensor(lrv, Gv[:, :, D:MSG], ae[:, :, 0:HEADS], ALU.add))
                    gs(dve.scalar_tensor_tensor(lr[:], lr[:], 0.2, lr[:], ALU.mult, ALU.max))
                    dve.tensor_tensor(lgv, lrv, ae[:, :, HEADS:2 * HEADS], ALU.subtract).then_inc(s_lg, 1)
                    dve.wait_ge(s_ex, g + 1)
                    for k in range(GT):
                        hv = G[s][:, k * MSG:k * MSG + D].rearrange("p (h c) -> p h c", c=C)
                        wv = G[s][:, k * MSG + D:(k + 1) * MSG].unsqueeze(2).broadcast_to([P, HEADS, C])
                        ins = dve.tensor_tensor(hv, hv, wv, ALU.mult)
                    gs(ins)
                    hold(dve)
                    with dve.Fori(lo, hi) as b:
                        w = dve.snap(item)
                        for k in range(GT):
                            ins = dve.tensor_scalar(S[:, k * P:(k + 1) * P], iota[:], dst_f[:, bass.ds(g * GT + k, 1)],
                                                    block_neg[:, bass.ds(b, 1)], ALU.subtract, ALU.is_equal)
                        ins.then_inc(s_sel, 1)
                        dve.wait_ge(s_mm, w + 1)
                        dve.tensor_tensor(acc[:, cols(b, MSG)], acc[:, cols(b, MSG)], psum[0][:, 0:MSG],
                                          ALU.add).then_inc(s_acc, 1)
                        dve.wait_ge(s_acc, w + 1)
                        dve.reg_add(item, item, 1)
                    gs(dve.memset(lr[:], 0.0))
                    dve.sem_inc(s_free, 1)

                tiles2(dve, NG, group)
                dve.wait_ge(s_selfw, 1)
                dve.wait_ge(s_bi, 16)
                dn = den[:].rearrange("p (t h) -> p t h", h=HEADS)
                sw = self_w[:].rearrange("p (t h) -> p t h", h=HEADS)
                done(dve.tensor_tensor(dn, acc[:].rearrange("p (t w) -> p t w", w=MSG)[:, :, D:MSG], sw, ALU.add))
                done(dve.tensor_scalar(den[:], den[:], 1e-16, None, ALU.add))
                done(dve.reciprocal(den[:], den[:]))

                def tile(n, s, i):
                    f = Done(dve, s_fin, n * 6)
                    h = HL[:, bass.ds(n * MSG, D)].rearrange("p (h c) -> p h c", c=C)
                    tv = tmp[:].rearrange("p (h c) -> p h c", c=C)

                    def heads(t):
                        return t[:, cols(n, HEADS)].unsqueeze(2).broadcast_to([P, HEADS, C])

                    f(dve.tensor_tensor(tv, h, heads(self_w), ALU.mult))
                    f(dve.tensor_tensor(tmp[:], tmp[:], acc[:, bass.ds(n * MSG, D)], ALU.add))
                    f(dve.tensor_tensor(tv, tv, heads(den), ALU.mult))
                    f(dve.tensor_tensor(tmp[:], tmp[:], bias[:], ALU.add))
                    f(dve.scalar_tensor_tensor(X[:, cols(n, D)], tmp[:], 0.0, X[:, cols(n, D)], ALU.max, ALU.add))
                    f.n += 1
                    dve.sem_inc(s_fin, 1)

                tiles2(dve, NT, tile)

        gat.close()
        if PHASES < 5:
            return store_out(nc, sem, X, out)

        ffn1 = ctx.enter_context(ExitStack())
        XN = sb(ffn1, "XN1", [P, NT * D])
        chosen = sb(ffn1, "chosen", [1, 2], I32)
        mixb = sb(ffn1, "mixb", [P, 2])
        with ExitStack() as st, nc.Block() as block:
            wrs = sb(st, "wrs", [P, DC * E1])
            brs = sb(st, "brs", [1, E1])
            part = sb(st, "part", [P, D])
            ones_col = sb(st, "ones_col", [P, 1])
            mean = sb(st, "mean", [P, DC])
            row = [sb(st, f"row{j}", [1, E1]) for j in range(4)]
            one = [sb(st, f"one{j}", [1, 1]) for j in range(8)]
            pair = sb(st, "pair", [1, 2])
            s_w = sem(st, "weights")
            s_dv = sem(st, "dve_done")
            s_pe = sem(st, "pe_done")
            s_go = sem(st, "to_pe")
            s_a = sem(st, "to_act")
            s_ab = sem(st, "from_act")
            roots = root_sems(st)

            @block.sync
            def _(sp):
                sp.dma_start(wrs[:].rearrange("p (c n) -> p c n", c=DC),
                             wr.rearrange("(c p) n -> p c n", p=P)).then_inc(s_w, 16)
                sp.dma_start(brs[:], br.rearrange("(a n) -> a n", a=1)).then_inc(s_w, 16)

            @block.vector
            def _(dve):
                done = Done(dve, s_dv)
                norm_stats(dve, done, X, roots)
                with dve.Fori(0, NT) as n:
                    normalised(dve, XN[:, cols(n, D)], X, n).then_inc(s_dv, 1)
                done.n += NT
                dve.wait_ge(s_dv, done.n)
                done(dve.tensor_scalar(part[:, 0:1], node_id[:, NT - 1:NT], float(N), None, ALU.is_lt))
                done(dve.tensor_scalar(XN[:, (NT - 1) * D:], XN[:, (NT - 1) * D:], part[:, 0:1], None, ALU.mult))
                done(dve.memset(ones_col[:], 1.0))
                done(dve.tensor_reduce(part[:], XN[:].rearrange("p (t d) -> p d t", d=D), AX.X, ALU.add))
                dve.sem_inc(s_go, 1)
                dve.wait_ge(s_pe, 1)
                done(dve.tensor_scalar(mean[:], psum[0][:, 0:DC], 1.0 / N, None, ALU.mult))
                dve.sem_inc(s_go, 1)
                dve.wait_ge(s_pe, 2)
                a, b, c, d = (r[:] for r in row)
                acts = [0]

                def softmax(to, of, width, o):
                    done(dve.tensor_reduce(one[o][:], of, AX.X, ALU.max))
                    done(dve.tensor_scalar(to, of, one[o][:], None, ALU.subtract))
                    dve.sem_inc(s_a, 1)
                    acts[0] += 1
                    dve.wait_ge(s_ab, acts[0])
                    done(dve.tensor_reduce(one[o + 1][:], to, AX.X, ALU.add))
                    done(dve.reciprocal(one[o + 1][:], one[o + 1][:]))
                    done(dve.tensor_scalar(to, to, one[o + 1][:], None, ALU.mult))

                done(dve.tensor_copy(a, psum[1][0:1, 0:E1]))
                softmax(b, a, E1, 0)
                done(dve.tensor_scalar(c, b, float(N), None, ALU.mult))
                done(dve.tensor_scalar(d, c, CAPACITY, None, ALU.max))
                done(dve.reciprocal(d, d))
                done(dve.tensor_scalar(d, d, CAPACITY, None, ALU.mult))
                done(dve.tensor_tensor(a, b, d, ALU.mult))
                softmax(b, a, E1, 2)
                for j in range(2):
                    done(dve.tensor_reduce(pair[:, j:j + 1], b, AX.X, ALU.max))
                    done(dve.tensor_scalar(c, b, pair[:, j:j + 1], None, ALU.is_ge))
                    done(dve.scalar_tensor_tensor(c, c, -1000.0, iota[0:1, 0:E1], ALU.mult, ALU.add))
                    done(dve.tensor_reduce(one[4][:], c, AX.X, ALU.min))
                    done(dve.tensor_scalar(d, c, one[4][:], None, ALU.is_equal))
                    done(dve.tensor_scalar(one[5][:], one[4][:], 1000.0, None, ALU.add))
                    done(dve.tensor_copy(chosen[:, j:j + 1], one[5][:]))
                    if j == 0:
                        done(dve.scalar_tensor_tensor(b, d, NEG, b, ALU.mult, ALU.add))
                softmax(row[0][:, 0:2], pair[:], 2, 6)
                dve.sem_inc(s_go, 1)
                dve.wait_ge(s_pe, 3)
                done(dve.tensor_copy(mixb[:], psum[2][:, 0:2]))

            @block.scalar
            def _(act):
                take_roots(act, roots)
                act.wait_ge(s_a, 1)
                act.activation(row[1][:], row[1][:], ACT.Exp).then_inc(s_ab, 1)
                act.wait_ge(s_a, 2)
                act.activation(row[1][:], row[1][:], ACT.Exp).then_inc(s_ab, 1)
                act.wait_ge(s_a, 3)
                act.activation(row[0][:, 0:2], row[0][:, 0:2], ACT.Exp).then_inc(s_ab, 1)

            @block.tensor
            def _(pe):
                pe.wait_ge(s_w, 32)
                pe.wait_ge(s_go, 1)
                for c in range(DC):
                    mm = pe.matmul(psum[0][:, c:c + 1], part[:, c * P:(c + 1) * P], ones_col[:], start=True, stop=True)
                mm.then_inc(s_pe, 1)
                pe.wait_ge(s_go, 2)
                for c in range(DC):
                    pe.matmul(psum[1][0:1, 0:E1], mean[:, c:c + 1], wrs[:, c * E1:(c + 1) * E1], start=(c == 0), stop=False)
                pe.matmul(psum[1][0:1, 0:E1], ones_row[:, 0:1], brs[:], start=False, stop=True).then_inc(s_pe, 1)
                pe.wait_ge(s_go, 3)
                pe.matmul(psum[2][:, 0:2], ones_row[:], row[0][:, 0:2], start=True, stop=True).then_inc(s_pe, 1)

        with ExitStack() as st, nc.Block() as block:
            W1 = sb(st, "W1b", [P, 2 * DC * F])
            W2 = sb(st, "W2b", [P, 2 * FC * D])
            B1 = sb(st, "B1b", [1, 2 * F])
            B2 = sb(st, "B2b", [1, 2 * D])
            gb = sb(st, "gamma_beta1", [P, 2 * D])
            xin = [sb(st, f"xinb{s}", [P, D]) for s in range(2)]
            tmp = sb(st, "tmpb", [P, D])
            roots = root_sems(st)
            s_nx = sem(st, "norm_step")
            s_w = sem(st, "weights")
            s_in = sem(st, "tile_in")
            s_gb = sem(st, "gamma_beta")
            s_used = sem(st, "tile_used")
            s_dv = sem(st, "dve_done")
            s_o = sem(st, "X_done")
            s_os = sem(st, "out_stored")

            def load_in(pe, w, s, i):
                pe.wait_ge(s_in, w + 1)
                return xin[s]

            def weights(pe):
                pe.wait_ge(s_w, 16 * 8)

                def of(w, s):
                    return (lambda c: W1[:, (s * DC + c) * F:(s * DC + c + 1) * F],
                            lambda c: W2[:, (s * FC + c) * D:(s * FC + c + 1) * D])

                return of

            def bias_sel(s, which):
                return ones_row[:], (B2[:, s * D:(s + 1) * D] if which else B1[:, s * F:(s + 1) * F])

            def dve_start(dve):
                dve.wait_ge(s_gb, 32)

            def dve_first(dve, w, s):
                if not (isinstance(w, int) and w == 2 * NT):
                    dve.sem_inc(s_used, 1)

            def take_out(dve, w, s, i, res):
                xt = XN[:, cols(i, D)]
                dve.scalar_tensor_tensor(xt, res, mixb[:, s:s + 1], xt, ALU.mult, ALU.add).then_inc(s_dv, 1)
                dve.wait_ge(s_dv, i * 2 + (s + 1))

            def dve_end(dve):
                norm_stats(dve, Done(dve, s_dv, 2 * NT), XN, roots)

                def tile(n, s, i):
                    norm_onto_x(dve, Done(dve, s_nx, n * 4), XN, tmp, gb, n)
                    dve.sem_inc(s_o, 1)

                tiles2(dve, NT, tile)

            @block.gpsimd
            def _(pool):
                pool.sem_inc(s_used, 2)

                def give(n, i):
                    for s in range(2):
                        pool.wait_ge(s_used, n * 2 + (s + 1))
                        hold(pool)
                        pool.tensor_copy(xin[s][:], XN[:, cols(n, D)]).then_inc(s_in, 1)

                with pool.Fori(0, NT) as n:
                    give(n, n)

            @block.sync
            def _(sp):
                for j in range(2):
                    e = sp.value_load(chosen[0:1, j:j + 1], min_val=0, max_val=E1 - 1)
                    sp.dma_start(W1[:, j * DC * F:(j + 1) * DC * F].rearrange("p (c f) -> p c f", f=F),
                                 w1b[bass.ds(e, 1)].rearrange("e (c p) f -> p (e c) f", p=P)).then_inc(s_w, 16)
                    sp.dma_start(W2[:, j * FC * D:(j + 1) * FC * D].rearrange("p (c f) -> p c f", f=D),
                                 w2b[bass.ds(e, 1)].rearrange("e (c p) f -> p (e c) f", p=P)).then_inc(s_w, 16)
                    sp.dma_start(B1[:, j * F:(j + 1) * F], b1b[bass.ds(e, 1), :]).then_inc(s_w, 16)
                    sp.dma_start(B2[:, j * D:(j + 1) * D], b2b[bass.ds(e, 1), :]).then_inc(s_w, 16)
                sp.dma_start(gb[:, 0:D], g1.partition_broadcast(P)).then_inc(s_gb, 16)
                sp.dma_start(gb[:, D:2 * D], be1.partition_broadcast(P)).then_inc(s_gb, 16)
                with sp.Fori(0, NT - 1) as n:
                    sp.wait_ge(s_o, n + 1)
                    sp.dma_start(out[bass.ds(n * P, P), :], X[:, cols(n, D)]).then_inc(s_os, 16)
                sp.wait_ge(s_o, NT)
                sp.dma_start(out[(NT - 1) * P:N, :], X[0:LAST, (NT - 1) * D:NT * D]).then_inc(s_os, 16)
                sp.wait_ge(s_os, 16 * NT)

            expert_pipeline(block, st, 2 * NT, ACT.Gelu, load_in, weights, bias_sel, take_out, dve_first, dve_start,
                            dve_end, lambda act: take_roots(act, roots))


PHASES = 9


def store_out(nc, sem, X, out):
    with ExitStack() as st, nc.Block() as block:
        s = sem(st, "out_stored")

        @block.sync
        def _(sp):
            sp.dma_start(out[0:(NT - 1) * P, :].rearrange("(t p) d -> p t d", p=P),
                         X[:, 0:(NT - 1) * D].rearrange("p (t d) -> p t d", d=D)).then_inc(s, 16)
            sp.dma_start(out[(NT - 1) * P:N, :], X[0:LAST, (NT - 1) * D:NT * D]).then_inc(s, 16)
            sp.wait_ge(s, 32)


_WEIGHTS = ["L0_gnn_W_self", "L0_gnn_W_neigh", "L0_ffn_gate_w", "L0_ffn_gate_b", "L0_ffn_w1", "L0_ffn_b1",
            "L0_ffn_w2", "L0_ffn_b2", "L0_ffn_gamma", "L0_ffn_beta", "L1_gnn_W", "L1_gnn_att_src",
            "L1_gnn_att_dst", "L1_gnn_bias", "L1_ffn_Wr", "L1_ffn_br", "L1_ffn_W1", "L1_ffn_b1", "L1_ffn_W2",
            "L1_ffn_b2", "L1_ffn_gamma", "L1_ffn_beta"]


def kernel(**inputs):
    import numpy as _np
    import concourse.bacc as _bacc
    from concourse import mybir as _mybir
    from concourse.bass_utils import run_bass_kernel_spmd as _run

    src = _np.zeros(NG * GE, _np.int32)
    dst = _np.full(NG * GE, NPAD - 1, _np.int32)
    src[:E] = _np.asarray(inputs["src"])
    dst[:E] = _np.asarray(inputs["dst"])
    given = {"x": inputs["x"], "src_cols": src.reshape(NG * GT, P).T, "dst_cols": dst.reshape(NG * GT, P).T,
             "dst_rows": dst.reshape(NG, GE), **{n: inputs[n] for n in _WEIGHTS}}
    nc = _bacc.Bacc("TRN2", target_bir_lowering=False, num_devices=1)
    arrays, args = {}, []
    for name, a in given.items():
        a = _np.ascontiguousarray(a)
        arrays[f"in_{name}"] = a
        args.append(nc.dram_tensor(f"in_{name}", a.shape, _mybir.dt.from_np(a.dtype), kind="ExternalInput").ap())
    args.append(nc.dram_tensor("out_x", (N, D), _mybir.dt.float32, kind="ExternalOutput").ap())
    program(nc, *args)
    r = _run(nc, [arrays], core_ids=[0])
    return r.results[0]["out_x"]
```

```python
from contextlib import ExitStack

import concourse.bass as bass
from concourse import mybir

ALU = mybir.AluOpType
ACT = mybir.ActivationFunctionType
AX = mybir.AxisListType
F32 = mybir.dt.float32
BF16 = mybir.dt.bfloat16
I32 = mybir.dt.int32
I16 = mybir.dt.int16

P = 128
N = 3125
D = 256
NT = -(-N // P)
LAST = N - (NT - 1) * P
NPAD = NT * P
E = 50000
GT = 8
GE = GT * P
NG = -(-E // GE)
MT = 4
ME = MT * P
MG = NG * GT // MT
SLOTS3 = 3
WIN, WIN32 = 2, 3
BIG = float(2 ** 100)
HEADS = 4
C = D // HEADS
NB32 = NPAD // 32
F = 512
DC, FC = D // P, F // P
E0 = 16
E1 = 8
WT = (2 * N + E0 * (P - 1)) // P
SLOTS = WT * P
NEG = -1.0e30
LN_EPS = 1e-5
MSG = D + HEADS
CAPACITY = float(-(-N * 125 // (100 * E1)))


def cols(i, width, offset=0):
    return bass.ds(i * width + offset, width)


def tiles2(eng, count, body):
    with eng.Fori(0, count // 2) as i:
        body(i * 2, 0, i)
        body(i * 2 + 1, 1, i)
    if count % 2:
        body(count - 1, 0, count // 2)


def ring(eng, first, end, body):
    rounds = (end - first) // SLOTS3
    with eng.Fori(0, rounds) as i:
        for k in range(SLOTS3):
            body(i * SLOTS3 + (first + k), (first + k) % SLOTS3, i + (first + k) // SLOTS3)
    for g in range(first + rounds * SLOTS3, end):
        body(g, g % SLOTS3, g // SLOTS3)


class Done:

    def __init__(self, eng, sem, base=0):
        self.eng, self.sem, self.base, self.n = eng, sem, base, 0

    def __call__(self, ins, wait=True):
        self.n += 1
        ins.then_inc(self.sem, 1)
        if wait:
            self.eng.wait_ge(self.sem, self.base + self.n)


def program(nc, x, src_cols, dst_cols, dst_rows, w_self, w_neigh, gate_w, gate_b, w1, b1, w2, b2, g0, be0,
            gat_w, att_src, att_dst, gat_bias, wr, br, w1b, b1b, w2b, b2b, g1, be1, out):
    with ExitStack() as ctx:
        sems = [0]
        used = []

        def sem(scope, name):
            sems[0] += 1
            handle = scope.enter_context(nc.semaphore(f"{name}_{sems[0]}"))
            if scope is not ctx:
                used.append(handle)
            return handle

        def sb(scope, name, shape, dt=F32):
            return scope.enter_context(nc.sbuf_tensor(name, shape, dt))

        def ps(scope, name, width=512):
            return scope.enter_context(nc.psum_tensor(name, [P, width], F32))

        def dram(name, shape, dt=F32):
            return nc.dram_tensor(name, shape, dt).ap()

        t_neigh = dram("t_neigh", [NPAD, D])
        t_ranges = dram("t_ranges", [NG, 4], I32)
        t_ranges32 = dram("t_ranges32", [MG, 4], I32)
        t_rel = dram("t_rel", [NG, GE], I16)
        t_rel32 = dram("t_rel32", [MG, ME], I16)
        t_xn = dram("t_xn", [NPAD, D])
        t_moe = dram("t_moe", [SLOTS, D])
        t_gat = dram("t_gat", [NPAD, MSG])
        t_as = dram("t_as", [NPAD, HEADS])

        X = sb(ctx, "X", [P, NT * D])
        ident = sb(ctx, "ident", [P, P])
        iota = sb(ctx, "iota", [P, WIN * P])
        block_neg = sb(ctx, "block_neg", [P, NT])
        node_id = sb(ctx, "node_id", [P, NT])
        src_i = sb(ctx, "src_i", [P, NG * GT], I32)
        shift = sb(ctx, "shift", [P, 1])
        dst_rel = sb(ctx, "dst_rel", [P, NG * GT])
        base = sb(ctx, "base", [P, NG])
        base32 = sb(ctx, "base32", [P, MG])
        ranges = sb(ctx, "ranges", [1, NG * 4], I32)
        ranges32 = sb(ctx, "ranges32", [1, MG * 4], I32)
        stats = sb(ctx, "stats", [P, 5 * 6])
        mv = sb(ctx, "mv", [P, NT * 2])
        mv5 = sb(ctx, "mv5", [P, 10])
        rstd = sb(ctx, "rstd", [P, NT])
        ones_row = sb(ctx, "ones_row", [1, P])
        banks = ps(ctx, "banks", 8 * 512)
        psum = [banks[:, i * 512:(i + 1) * 512] for i in range(8)]

        s_hold = sem(ctx, "hold")

        def hold(eng):
            eng.sem_inc(s_hold, 1)

        def norm_stats(dve, done, src, roots):
            s = done.base + done.n
            with dve.Fori(0, NT // 5) as i:
                for k in range(5):
                    ins = dve.bn_stats(stats[:, k * 6:k * 6 + 6], src[:, cols(i * 5 + k, D)])
                    ins.then_inc(done.sem, 1)
                dve.wait_ge(done.sem, i * 11 + (s + 5))
                hold(dve)
                for k in range(5):
                    ins = dve.bn_aggr(mv5[:, k * 2:k * 2 + 2], stats[:, k * 6:k * 6 + 6])
                    ins.then_inc(done.sem, 1)
                dve.wait_ge(done.sem, i * 11 + (s + 10))
                dve.tensor_copy(mv[:, cols(i, 10)], mv5[:]).then_inc(done.sem, 1)
                dve.wait_ge(done.sem, i * 11 + (s + 11))
            done.n += 2 * NT + NT // 5
            asked, given = roots
            dve.tensor_scalar(rstd[:], mv[:, 1:2 * NT:2], LN_EPS, None, ALU.add).then_inc(asked, 1)
            dve.wait_ge(given, 1)
            done(dve.reciprocal(rstd[:], rstd[:]))

        def take_roots(act, roots):
            asked, given = roots
            act.wait_ge(asked, 1)
            act.activation(rstd[:], rstd[:], ACT.Sqrt).then_inc(given, 1)

        def root_sems(st):
            return sem(st, "variance_ready"), sem(st, "root_ready")

        def normalised(dve, dst, src, n):
            return dve.tensor_scalar(dst, src[:, cols(n, D)], mv[:, bass.ds(n * 2, 1)], rstd[:, bass.ds(n, 1)],
                                     ALU.subtract, ALU.mult)

        def norm_onto_x(dve, done, y, tmp, gb, n):
            done(normalised(dve, tmp[:], y, n))
            done(dve.tensor_tensor(tmp[:], tmp[:], gb[:, 0:D], ALU.mult))
            done(dve.tensor_tensor(tmp[:], tmp[:], gb[:, D:2 * D], ALU.add))
            done(dve.tensor_tensor(X[:, cols(n, D)], X[:, cols(n, D)], tmp[:], ALU.add))

        with ExitStack() as st, nc.Block() as block:
            dst_i = sb(st, "dst_i", [P, NG * GT], I32)
            rows = [sb(st, "rows", [NG, GE], I32), sb(st, "rows32", [MG, ME], I32)]
            rel = [sb(st, "rel", [NG, GE], I16), sb(st, "rel32", [MG, ME], I16)]
            rng = [sb(st, "rng", [NG, 4], I32), sb(st, "rng32", [MG, 4], I32)]
            first = [sb(st, "first", [NG, 1]), sb(st, "first32", [MG, 1])]
            lo_b = [sb(st, "lo_b", [P, NG * 4], I32), sb(st, "lo_b32", [P, MG * 4], I32)]
            ids = sb(st, "ids", [P, WIN * P], I32)
            s_tail = sem(st, "tail_zeroed")
            s_ld = sem(st, "loaded")
            s_dv = sem(st, "dve_done")
            s_po = sem(st, "pool_done")
            s_rng = sem(st, "ranges_ready")
            s_rst = sem(st, "ranges_stored")
            s_rel = sem(st, "relative_stored")
            s_rld = sem(st, "ranges_loaded")

            @block.sync
            def _(sp):
                sp.dma_start(rows[0][:], dst_rows.rearrange("(g a) e -> g (a e)", a=GT // MT)).then_inc(s_ld, 16)
                sp.dma_start(rows[1][:], dst_rows).then_inc(s_ld, 16)
                sp.dma_start(dst_i[:], dst_cols).then_inc(s_ld, 16)
                sp.dma_start(src_i[:], src_cols).then_inc(s_ld, 16)
                sp.dma_start(X[:, 0:(NT - 1) * D].rearrange("p (t d) -> p t d", d=D),
                             x[0:(NT - 1) * P, :].rearrange("(t p) d -> p t d", p=P)).then_inc(s_ld, 16)
                sp.wait_ge(s_tail, 1)
                sp.dma_start(X[0:LAST, (NT - 1) * D:NT * D], x[(NT - 1) * P:N, :]).then_inc(s_ld, 16)
                sp.wait_ge(s_rng, 1)
                sp.dma_start(t_ranges, rng[0][:]).then_inc(s_rst, 16)
                sp.dma_start(t_ranges32, rng[1][:]).then_inc(s_rst, 16)
                sp.dma_start(t_rel, rel[0][:]).then_inc(s_rel, 16)
                sp.dma_start(t_rel32, rel[1][:]).then_inc(s_rel, 16)
                sp.wait_ge(s_rst, 32)
                for table, row, copies in ((t_ranges, ranges, lo_b[0]), (t_ranges32, ranges32, lo_b[1])):
                    flat = table.rearrange("(a g) f -> a (g f)", a=1)
                    sp.dma_start(row[:], flat).then_inc(s_rld, 16)
                    sp.dma_start(copies[:], flat.broadcast_to([P, copies.shape[1]])).then_inc(s_rld, 16)
                sp.wait_ge(s_rld, 64)
                sp.wait_ge(s_rel, 32)
                sp.wait_ge(s_ld, 96)

            @block.gpsimd
            def _(pool):
                done = Done(pool, s_po)
                done(pool.memset(ident[:], 0.0))
                done(pool.affine_select(out=ident[:], in_=ident[:], compare_op=ALU.not_equal, fill=1.0, base=0,
                                        pattern=[[-1, P]], channel_multiplier=1))
                for dst, step, per_partition in ((iota, 1, 0), (node_id, P, 1), (block_neg, -P, 0)):
                    wide = dst.shape[1]
                    done(pool.iota(ids[:, 0:wide], pattern=[[step, wide]], base=0, channel_multiplier=per_partition))
                    done(pool.tensor_copy(dst[:], ids[:, 0:wide]))
                done(pool.memset(ones_row[:], 1.0))

            @block.vector
            def _(dve):
                done = Done(dve, s_dv)
                dve.memset(X[:, (NT - 1) * D:NT * D], 0.0).then_inc(s_tail, 1)
                dve.wait_ge(s_ld, 96)
                for j, shift in ((0, 7), (1, 5)):
                    r = rng[j]
                    done(dve.tensor_reduce(r[:, 0:1], rows[j][:], AX.X, ALU.min))
                    done(dve.tensor_reduce(r[:, 1:2], rows[j][:], AX.X, ALU.max))
                    done(dve.tensor_single_scalar(r[:, 0:2], r[:, 0:2], shift, ALU.arith_shift_right))
                    done(dve.tensor_scalar(r[:, 1:2], r[:, 1:2], 1.0, None, ALU.add))
                    done(dve.tensor_tensor(r[:, 2:3], r[:, 1:2], r[:, 0:1], ALU.subtract))
                    done(dve.tensor_copy(r[:, 3:4], r[:, 0:1]))
                    done(dve.tensor_scalar(first[j][:], r[:, 0:1], float(2 ** shift), None, ALU.mult))
                    done(dve.tensor_scalar(rel[j][:], rows[j][:], first[j][:], None, ALU.subtract))
                dve.sem_inc(s_rng, 1)
                dve.wait_ge(s_rld, 64)
                done(dve.tensor_scalar(base[:], lo_b[0][:].rearrange("p (g f) -> p g f", f=4)[:, :, 0], float(P), None,
                                       ALU.mult))
                done(dve.tensor_scalar(base32[:], lo_b[1][:].rearrange("p (g f) -> p g f", f=4)[:, :, 0], 32.0, None,
                                       ALU.mult))
                done(dve.tensor_tensor(dst_rel[:].rearrange("p (g k) -> p g k", k=GT),
                                       dst_i[:].rearrange("p (g k) -> p g k", k=GT),
                                       base[:].unsqueeze(2).broadcast_to([P, NG, GT]), ALU.subtract))

        def transposer(pe, ready, n, xn, bank, landed):
            pe.wait_ge(ready, n + 1)
            pe.transpose(bank[:, 0:P], xn[:, 0:P], ident[:])
            pe.transpose(bank[:, P:2 * P], xn[:, P:2 * P], ident[:]).then_inc(landed, 1)

        with ExitStack() as st, nc.Block() as block:
            W = sb(st, "W_l0", [P, DC * 512])
            HS = sb(st, "HS", [P, NT * D])
            xn = [sb(st, f"xn_a{s}", [P, D]) for s in range(2)]
            xT = [sb(st, f"xT_a{s}", [P, D]) for s in range(2)]
            top = sb(st, "top", [P, 8])
            work = sb(st, "work", [P, D])
            s_w = sem(st, "weights")
            s_dv = sem(st, "dve_done")
            s_tk = sem(st, "top_done")
            s_xn = sem(st, "xn_ready")
            s_tp = sem(st, "turned")
            s_xt = sem(st, "xT_ready")
            s_mm = sem(st, "projected")
            s_hs = sem(st, "sparse_ready")
            s_st = sem(st, "table_stored")
            roots = root_sems(st)

            @block.sync
            def _(sp):
                wv = W[:].rearrange("p (c n) -> p c n", c=DC)
                sp.dma_start(wv[:, :, 0:D], w_self.rearrange("(c p) n -> p c n", p=P)).then_inc(s_w, 16)
                sp.dma_start(wv[:, :, D:2 * D], w_neigh.rearrange("(c p) n -> p c n", p=P)).then_inc(s_w, 16)

                def store(n, s, i):
                    sp.wait_ge(s_hs, n + 1)
                    sp.dma_start(t_neigh[bass.ds(n * P, P), :], HS[:, cols(n, D)]).then_inc(s_st, 16)

                tiles2(sp, NT, store)
                sp.wait_ge(s_st, 16 * NT)

            @block.vector
            def _(dve):
                norm_stats(dve, Done(dve, s_dv), X, roots)
                normalised(dve, xn[0][:], X, 0).then_inc(s_xn, 1)
                links = 9

                def tile(n, s, i):
                    dve.wait_ge(s_mm, n + 1)
                    if not (isinstance(n, int) and n == NT - 1):
                        normalised(dve, xn[1 - s][:], X, n + 1).then_inc(s_xn, 1)
                    h = psum[2 + s]
                    done = Done(dve, s_tk, n * links)
                    done(dve.tensor_tensor(X[:, cols(n, D)], X[:, cols(n, D)], h[:, 0:D], ALU.add), wait=False)
                    for r in range(4):
                        left = h[:, D:2 * D] if r == 0 else work[:]
                        done(dve.max(top[:], left))
                        hold(dve)
                        done(dve.match_replace(work[:], top[:], left, NEG))
                        if r < 3:
                            hold(dve)
                    dve.scalar_tensor_tensor(HS[:, cols(n, D)], work[:], NEG, h[:, D:2 * D], ALU.is_equal,
                                             ALU.mult).then_inc(s_hs, 1)

                tiles2(dve, NT, tile)

            @block.scalar
            def _(act):
                take_roots(act, roots)

                def turn(n, s, i):
                    act.wait_ge(s_tp, n + 1)
                    act.copy(xT[s][:], psum[s][:, 0:D]).then_inc(s_xt, 1)

                tiles2(act, NT, turn)

            @block.tensor
            def _(pe):
                pe.wait_ge(s_w, 32)

                def project(n, s, i):
                    transposer(pe, s_xn, n, xn[s], psum[s], s_tp)
                    pe.wait_ge(s_xt, n + 1)
                    for c in range(DC):
                        mm = pe.matmul(psum[2 + s][:], xT[s][:, c * P:(c + 1) * P], W[:, c * 512:(c + 1) * 512],
                                       start=(c == 0), stop=(c == DC - 1))
                    mm.then_inc(s_mm, 1)

                tiles2(pe, NT, project)

        def gather_groups(pool, sems_, table, idx, into, width, tiles, groups):
            s_free, s_ix, s_arr = sems_

            def group(g, s, i):
                pool.wait_ge(s_free, g + 1)
                pool.tensor_copy(idx[s][:], src_i[:, cols(g, tiles)]).then_inc(s_ix, 1)
                pool.wait_ge(s_ix, g + 1)
                hold(pool)
                pitch = into[s].shape[1] // tiles
                for k in range(tiles):
                    pool.indirect_dma_start(
                        into[s][:, k * pitch:k * pitch + width], None, table,
                        bass.IndirectOffsetOnAxis(ap=idx[s][:, k:k + 1], axis=0)).then_inc(s_arr[s], 16)

            ring(pool, 0, groups, group)

        def lowest(eng, table, g, blocks):
            return eng.value_load(table[0:1, bass.ds(g * 4, 1)], min_val=0, max_val=blocks - 1)

        def beyond(eng, table, g, blocks, window):
            lo = lowest(eng, table, g, blocks)
            hi = eng.value_load(table[0:1, bass.ds(g * 4 + 1, 1)], min_val=1, max_val=blocks)
            return eng.Fori(lo + window, hi)

        def named(eng, table, g, blocks):
            return eng.value_load(table[0:1, bass.ds(g * 4 + 2, 1)], min_val=1, max_val=blocks)

        def select_block(dve, S, g, b, shifted, w):
            dve.tensor_tensor(shift[:], block_neg[:, bass.ds(b, 1)], base[:, bass.ds(g, 1)],
                              ALU.add).then_inc(shifted, 1)
            dve.wait_ge(shifted, w + 1)
            for k in range(GT):
                ins = dve.tensor_scalar(S[:, k * P:(k + 1) * P], iota[:, 0:P], dst_rel[:, bass.ds(g * GT + k, 1)],
                                        shift[:], ALU.subtract, ALU.is_equal)
            return ins

        def sum_rows(pe, S, rows_, width, at, bank):
            for k in range(GT):
                mm = pe.matmul(bank[:, 0:width], S(k)[:, at:at + P], rows_[:, k * width:(k + 1) * width],
                               start=(k == 0), stop=(k == GT - 1))
            return mm

        def window_sums(s, width):
            return banks[:, 2 * s * 512:(2 * s + 2) * 512].rearrange("p (j w) -> p j w", j=WIN)[:, :, 0:width]

        with ExitStack() as st, nc.Block() as block:
            AW = D + 1
            acc = sb(st, "acc0", [P, (NT + 1) * AW])
            G = [sb(st, f"G0_{s}", [P, GT * AW]) for s in range(SLOTS3)]
            idx = [sb(st, f"idx0_{s}", [P, GT], I32) for s in range(SLOTS3)]
            S = [sb(st, f"S0_{s}", [P, GT * WIN * P]) for s in range(SLOTS3)]
            SL = sb(st, "SL0", [P, GE])
            deg = sb(st, "deg", [P, NT])
            s_dv = sem(st, "dve_done")
            s_ix = sem(st, "idx_ready")
            s_arr = [sem(st, f"rows_arrived{s}") for s in range(SLOTS3)]
            s_ones = sem(st, "ones_ready")
            s_sel = sem(st, "selector_ready")
            s_mm = sem(st, "summed")
            s_acc = sem(st, "added")
            s_sh = sem(st, "shift_ready")
            s_lsel = sem(st, "beyond_selector_ready")
            s_lmm = sem(st, "beyond_summed")
            s_lacc = sem(st, "beyond_added")

            @block.gpsimd
            def _(pool):
                gather_groups(pool, (s_mm, s_ix, s_arr), t_neigh, idx, G, D, GT, NG)

            @block.vector
            def _(dve):
                done = Done(dve, s_dv)
                for s in range(SLOTS3):
                    ones = G[s][:].rearrange("p (k w) -> p k w", k=GT)[:, :, D:AW]
                    dve.memset(ones, 1.0).then_inc(s_ones, 1)
                done(dve.memset(acc[:], 0.0))
                extra = dve.alloc_register("dve_extra0")
                dve.reg_mov(extra, 0)

                def select(g, s):
                    many = named(dve, ranges, g, NT)
                    dve.tensor_tensor(S[s][:].rearrange("p (k d) -> p k d", k=GT),
                                      iota[:].unsqueeze(1).broadcast_to([P, GT, WIN * P]),
                                      dst_rel[:, cols(g, GT)].unsqueeze(2).broadcast_to([P, GT, WIN * P]),
                                      ALU.is_equal).then_inc(s_sel, 1)
                    with dve.If(many > WIN):
                        with beyond(dve, ranges, g, NT, WIN) as b:
                            w = dve.snap(extra)
                            select_block(dve, SL, g, b, s_sh, w).then_inc(s_lsel, 1)
                            dve.wait_ge(s_lmm, w + 1)
                            dve.tensor_tensor(acc[:, cols(b, AW)], acc[:, cols(b, AW)], psum[6][:, 0:AW],
                                              ALU.add).then_inc(s_lacc, 1)
                            dve.wait_ge(s_lacc, w + 1)
                            dve.reg_add(extra, extra, 1)

                def add(g, s):
                    lo = lowest(dve, ranges, g, NT)
                    dve.wait_ge(s_mm, g + 1 + SLOTS3)
                    dve.wait_ge(s_acc, g + 1)
                    av = acc[:, bass.ds(lo * AW, WIN * AW)].rearrange("p (j w) -> p j w", j=WIN)
                    dve.tensor_tensor(av, av, window_sums(s, AW), ALU.add).then_inc(s_acc, 1)

                dve.sem_inc(s_acc, 1)
                select(0, 0)

                def group(g, s, i):
                    select(g, s)
                    add(g - 1, (s - 1) % SLOTS3)

                ring(dve, 1, NG, group)
                add(NG - 1, (NG - 1) % SLOTS3)
                dve.wait_ge(s_acc, NG + 1)
                count = acc[:, 0:NT * AW].rearrange("p (t w) -> p t w", w=AW)[:, :, D]
                done(dve.tensor_scalar(deg[:], count, 1.0, None, ALU.max))
                done(dve.reciprocal(deg[:], deg[:]))

                def mean(n, s, i):
                    dve.scalar_tensor_tensor(X[:, cols(n, D)], acc[:, bass.ds(n * AW, D)], deg[:, bass.ds(n, 1)],
                                             X[:, cols(n, D)], ALU.mult, ALU.add)

                tiles2(dve, NT, mean)

            @block.tensor
            def _(pe):
                extra = pe.alloc_register("pe_extra0")
                pe.reg_mov(extra, 0)
                pe.wait_ge(s_ones, SLOTS3)
                pe.sem_inc(s_mm, SLOTS3)

                def group(g, s, i):
                    many = named(pe, ranges, g, NT)
                    pe.wait_ge(s_arr[s], i * (16 * GT) + 16 * GT)
                    hold(pe)
                    with pe.If(many > WIN):
                        with beyond(pe, ranges, g, NT, WIN):
                            w = pe.snap(extra)
                            pe.wait_ge(s_lsel, w + 1)
                            sum_rows(pe, lambda k: SL[:, k * P:(k + 1) * P], G[s], AW, 0, psum[6]).then_inc(s_lmm, 1)
                            pe.reg_add(extra, extra, 1)
                    pe.wait_ge(s_sel, g + 1)
                    for j in range(WIN):
                        mm = sum_rows(pe, lambda k: S[s][:, k * WIN * P:(k + 1) * WIN * P], G[s], AW, j * P,
                                      psum[2 * s + j])
                    mm.then_inc(s_mm, 1)

                ring(pe, 0, NG, group)

        if PHASES < 3:
            return store_out(nc, sem, X, out)

        with nc.Block() as block:
            @block.gpsimd
            def _(pool):
                for handle in used:
                    pool.sem_clear(handle)

        ffn0 = ctx.enter_context(ExitStack())
        XN = sb(ffn0, "XN", [P, NT * D])
        mix = sb(ffn0, "mix", [P, 2 * NT])
        place = sb(ffn0, "place", [P, 2 * NT], I32)
        token = sb(ffn0, "token", [P, WT], I32)
        tile_e = sb(ffn0, "tile_e", [P, WT], I32)
        tile_hot = sb(ffn0, "tile_hot", [E0, WT])
        with ExitStack() as st, nc.Block() as block:
            TE = NT * E0
            gw = sb(st, "gw", [P, DC * E0])
            gb = sb(st, "gb", [1, E0])
            xn = [sb(st, f"xn_b{s}", [P, D]) for s in range(2)]
            xT = [sb(st, f"xT_b{s}", [P, D]) for s in range(2)]
            L = sb(st, "L", [P, TE])
            cand = sb(st, "cand", [P, TE])
            M = [sb(st, f"M{j}", [P, TE]) for j in range(2)]
            Mb = sb(st, "Mb", [P, TE], BF16)
            tot = sb(st, "tot", [P, TE])
            scan = [sb(st, f"scan{j}", [P, TE]) for j in range(2)]
            val = [sb(st, f"val{j}", [P, NT]) for j in range(2)]
            best = sb(st, "best", [P, NT])
            real = sb(st, "real", [P, NT])
            pos_i = sb(st, "pos_i", [P, 2 * NT], I32)
            pos_w = sb(st, "pos_w", [P, 2 * NT])
            pos_r = sb(st, "pos_r", [P, 2 * NT])
            hot_r = [sb(st, f"hot_r{c}", [P, P], BF16) for c in range(2)]
            hot_w = [sb(st, f"hot_w{c}", [P, 2 * WT], BF16) for c in range(2)]
            pos = sb(st, "pos", [P, 2 * NT])
            et = [sb(st, f"et{j}", [P, E0]) for j in range(3)]
            ni = sb(st, "ni", [P, E0], I32)
            cmp = sb(st, "cmp", [P, WT * E0])
            te_f = sb(st, "te_f", [P, WT])
            upper = sb(st, "upper", [P, P], BF16)
            ones_b = sb(st, "ones_b", [P, P], BF16)
            s_w = sem(st, "weights")
            s_dv = sem(st, "dve_done")
            s_po = sem(st, "pool_done")
            s_xn = sem(st, "xn_ready")
            s_tp = sem(st, "turned")
            s_xt = sem(st, "xT_ready")
            s_xc = sem(st, "XN_kept")
            s_mm = sem(st, "logits_done")
            s_mb = sem(st, "choice_ready")
            s_rk = sem(st, "ranked")
            s_e = sem(st, "exp_in")
            s_ex = sem(st, "exp_out")
            s_hot = sem(st, "hot_ready")
            s_inv = sem(st, "inverted")
            s_st = sem(st, "rows_stored")
            roots = root_sems(st)

            @block.sync
            def _(sp):
                sp.dma_start(gw[:].rearrange("p (c n) -> p c n", c=DC),
                             gate_w.rearrange("(c p) n -> p c n", p=P)).then_inc(s_w, 16)
                sp.dma_start(gb[:], gate_b.rearrange("(a n) -> a n", a=1)).then_inc(s_w, 16)

                def store(n, s, i):
                    sp.wait_ge(s_xc, n + 1)
                    sp.dma_start(t_xn[bass.ds(n * P, P), :], XN[:, cols(n, D)]).then_inc(s_st, 16)

                tiles2(sp, NT, store)
                sp.wait_ge(s_st, 16 * NT)

            @block.gpsimd
            def _(pool):
                done = Done(pool, s_po)
                pool.memset(ones_b[:], 1.0).then_inc(s_po, 1)
                done.n += 1
                done(pool.memset(upper[:], 1.0))
                done(pool.affine_select(out=upper[:], in_=upper[:], compare_op=ALU.is_gt, fill=0.0, base=0,
                                        pattern=[[1, P]], channel_multiplier=-1))

            @block.vector
            def _(dve):
                done = Done(dve, s_dv)
                norm_stats(dve, done, X, roots)
                done(normalised(dve, xn[0][:], X, 0), wait=False)
                base = done.base + done.n - 1

                def tile(n, s, i):
                    dve.wait_ge(s_mm, n + 1)
                    dve.wait_ge(s_xc, n + 1)
                    if not (isinstance(n, int) and n == NT - 1):
                        normalised(dve, xn[1 - s][:], X, n + 1).then_inc(s_dv, 1)

                tiles2(dve, NT, tile)
                done.n = base + NT
                dve.wait_ge(s_mm, NT)

                def te(t):
                    return t.rearrange("p (t e) -> p t e", e=E0)

                def per_token(t):
                    return t.unsqueeze(2).broadcast_to([P, NT, E0])

                def per_expert(t):
                    return t.unsqueeze(1).broadcast_to([P, NT, E0])

                e_id = iota[:, 0:E0]
                done(dve.tensor_copy(L[:], psum[2][:, 0:TE]))
                done(dve.tensor_scalar(real[:], node_id[:], float(N), None, ALU.is_lt), wait=False)
                for j in range(2):
                    done(dve.tensor_reduce(val[j][:], te(L[:]), AX.X, ALU.max))
                    done(dve.tensor_tensor(te(cand[:]), te(L[:]), per_token(val[j][:]), ALU.is_ge))
                    done(dve.scalar_tensor_tensor(te(cand[:]), te(cand[:]), -1000.0, per_expert(e_id),
                                                  ALU.mult, ALU.add))
                    done(dve.tensor_reduce(best[:], te(cand[:]), AX.X, ALU.min))
                    done(dve.tensor_tensor(te(M[j][:]), te(cand[:]), per_token(best[:]), ALU.is_equal))
                    if j == 0:
                        done(dve.scalar_tensor_tensor(L[:], M[0][:], NEG, L[:], ALU.mult, ALU.add))
                dve.tensor_tensor(best[:], val[1][:], val[0][:], ALU.subtract).then_inc(s_e, 1)
                for j in range(2):
                    done(dve.tensor_tensor(te(M[j][:]), te(M[j][:]), per_token(real[:]), ALU.mult))
                dve.tensor_tensor(Mb[:], M[0][:], M[1][:], ALU.add).then_inc(s_mb, 1)
                dve.wait_ge(s_ex, 1)
                done(dve.tensor_scalar(val[1][:], val[0][:], 1.0, None, ALU.add))
                done(dve.reciprocal(mix[:, 0:NT], val[1][:]))
                done(dve.tensor_tensor(mix[:, NT:2 * NT], mix[:, 0:NT], val[0][:], ALU.mult))
                dve.wait_ge(s_rk, 1)
                done(dve.tensor_copy(tot[:], psum[4][:, 0:TE]))
                at, step = tot, 1
                for r in range(5):
                    to = scan[r % 2]
                    w = step * E0
                    done(dve.tensor_copy(to[:, 0:w], at[:, 0:w]))
                    done(dve.tensor_tensor(to[:, w:TE], at[:, w:TE], at[:, 0:TE - w], ALU.add))
                    at, step = to, step * 2
                done(dve.tensor_scalar(ni[:], at[:, TE - E0:TE], float(P - 1), None, ALU.add))
                done(dve.tensor_single_scalar(ni[:], ni[:], 7, ALU.arith_shift_right))
                done(dve.tensor_copy(et[2][:], ni[:]))
                cur, step = et[2], 1
                for r in range(4):
                    to = et[r % 2]
                    done(dve.tensor_copy(to[:, 0:step], cur[:, 0:step]))
                    done(dve.tensor_tensor(to[:, step:E0], cur[:, step:E0], cur[:, 0:E0 - step], ALU.add))
                    cur, step = to, step * 2
                start = et[0]
                assert cur is et[1] and at is scan[0]
                done(dve.tensor_tensor(start[:], cur[:], et[2][:], ALU.subtract))
                slot = scan[1]
                done(dve.tensor_tensor(slot[:], at[:], tot[:], ALU.subtract))
                done(dve.tensor_tensor(slot[:], slot[:], psum[3][:, 0:TE], ALU.add))
                done(dve.scalar_tensor_tensor(te(slot[:]), per_expert(start[:]), float(P), te(slot[:]),
                                              ALU.mult, ALU.add))
                for j in range(2):
                    done(dve.tensor_tensor(cand[:], M[j][:], slot[:], ALU.mult))
                    done(dve.tensor_reduce(pos[:, j * NT:(j + 1) * NT], te(cand[:]), AX.X, ALU.add))
                done(dve.tensor_copy(place[:], pos[:]))
                done(dve.tensor_scalar(best[:], real[:], 1.0, None, ALU.subtract))
                for j in range(2):
                    done(dve.tensor_tensor(pos[:, j * NT:(j + 1) * NT], pos[:, j * NT:(j + 1) * NT], best[:],
                                           ALU.add))
                done(dve.tensor_copy(pos_i[:], pos[:]))
                done(dve.tensor_single_scalar(pos_i[:], pos_i[:], 7, ALU.arith_shift_right))
                done(dve.tensor_copy(pos_w[:], pos_i[:]))
                done(dve.scalar_tensor_tensor(pos_r[:], pos_w[:], -float(P), pos[:], ALU.mult, ALU.add))

                def hot(t, c):
                    j = bass.ds(t + c * NT, 1)
                    dve.tensor_scalar(hot_r[c][:], iota[:, 0:P], pos_r[:, j], None, ALU.is_equal)
                    dve.tensor_scalar(hot_w[c][:, 0:WT], iota[:, 0:WT], pos_w[:, j], node_id[:, 0:1],
                                      ALU.is_equal, ALU.mult)
                    dve.tensor_scalar(hot_w[c][:, WT:2 * WT], iota[:, 0:WT], pos_w[:, j], iota[:, bass.ds(t, 1)],
                                      ALU.is_equal, ALU.mult).then_inc(s_hot, 1)

                for c in range(2):
                    hot(0, c)
                with dve.Fori(1, NT) as t:
                    for c in range(2):
                        dve.wait_ge(s_inv, t * 2 + (c - 1))
                        hot(t, c)
                dve.wait_ge(s_inv, 2 * NT)
                done(dve.tensor_copy(te_f[:], psum[5][:, 0:WT]))
                done(dve.scalar_tensor_tensor(te_f[:], psum[5][:, WT:2 * WT], float(P), te_f[:], ALU.mult, ALU.add))
                done(dve.tensor_copy(token[:], te_f[:]))
                done(dve.tensor_tensor(cmp[:].rearrange("p (w e) -> p w e", e=E0),
                                       iota[:, 0:WT].unsqueeze(2).broadcast_to([P, WT, E0]),
                                       cur[:].unsqueeze(1).broadcast_to([P, WT, E0]), ALU.is_ge))
                done(dve.tensor_reduce(te_f[:], cmp[:].rearrange("p (w e) -> p w e", e=E0), AX.X, ALU.add))
                done(dve.tensor_scalar(te_f[:], te_f[:], float(E0 - 1), None, ALU.min))
                done(dve.tensor_copy(tile_e[:], te_f[:]))
                done(dve.tensor_scalar(tile_hot[:], te_f[0:E0, :], node_id[0:E0, 0:1], None, ALU.is_equal))

            @block.scalar
            def _(act):
                take_roots(act, roots)

                def turn(n, s, i):
                    act.wait_ge(s_tp, n + 1)
                    act.copy(xT[s][:], psum[s][:, 0:D]).then_inc(s_xt, 1)
                    act.copy(XN[:, cols(n, D)], xn[s][:]).then_inc(s_xc, 1)

                tiles2(act, NT, turn)
                act.wait_ge(s_e, 1)
                act.activation(val[0][:], best[:], ACT.Exp).then_inc(s_ex, 1)

            @block.tensor
            def _(pe):
                pe.wait_ge(s_w, 32)
                first = 2 * NT + NT // 5 + 1

                def logits(n, s, i):
                    pe.wait_ge(s_dv, n + (first + 1))
                    pe.transpose(psum[s][:, 0:P], xn[s][:, 0:P], ident[:])
                    pe.transpose(psum[s][:, P:2 * P], xn[s][:, P:2 * P], ident[:]).then_inc(s_tp, 1)
                    pe.wait_ge(s_xt, n + 1)
                    at = psum[2][:, cols(n, E0)]
                    for c in range(DC):
                        pe.matmul(at, xT[s][:, c * P:(c + 1) * P], gw[:, c * E0:(c + 1) * E0],
                                  start=(c == 0), stop=False, skip_group_check=True)
                    pe.matmul(at, ones_row[:], gb[:], start=False, stop=True, skip_group_check=True).then_inc(s_mm, 1)

                tiles2(pe, NT, logits)
                pe.wait_ge(s_mb, 1)
                pe.wait_ge(s_po, 3)
                pe.matmul(psum[3][:, 0:TE], upper[:], Mb[:], start=True, stop=True)
                pe.matmul(psum[4][:, 0:TE], ones_b[:], Mb[:], start=True, stop=True).then_inc(s_rk, 1)

                def invert(t, c, start=False, stop=False):
                    pe.wait_ge(s_hot, t * 2 + (c + 1))
                    pe.matmul(psum[5][:, 0:2 * WT], hot_r[c][:], hot_w[c][:], start=start, stop=stop).then_inc(s_inv, 1)

                invert(0, 0, start=True)
                invert(0, 1)
                with pe.Fori(1, NT - 1) as t:
                    invert(t, 0)
                    invert(t, 1)
                invert(NT - 1, 0)
                invert(NT - 1, 1, stop=True)

        def expert_pipeline(block, st, items, func, load_in, weights, bias_sel, take_out, dve_first, dve_start,
                            dve_end, act_end):
            xT = [sb(st, f"xT_f{items}_{s}", [P, D]) for s in range(2)]
            h = [sb(st, f"h_f{items}_{s}", [P, F]) for s in range(2)]
            hT = [sb(st, f"hT_f{items}_{s}", [P, F]) for s in range(2)]
            s_tp, s_xt, s_h, s_hr, s_ht, s_hc, s_y, s_yo = (
                sem(st, n) for n in ("turned", "xT_ready", "hidden", "act_done", "h_turned", "hT_ready", "result", "taken"))

            @block.tensor
            def _(pe):
                def turn(w, s, i):
                    tile = load_in(pe, w, s, i)
                    pe.transpose(psum[s][:, 0:P], tile[:, 0:P], ident[:])
                    pe.transpose(psum[s][:, P:2 * P], tile[:, P:2 * P], ident[:]).then_inc(s_tp, 1)

                def up(w, s, ww):
                    pe.wait_ge(s_xt, w + 1)
                    for c in range(DC):
                        pe.matmul(psum[2 + s][:], xT[s][:, c * P:(c + 1) * P], ww[0](c), start=(c == 0), stop=False)
                    sel, bias = bias_sel(s, 0)
                    pe.matmul(psum[2 + s][:], sel, bias, start=False, stop=True).then_inc(s_h, 1)

                def turn_h(w, s):
                    pe.wait_ge(s_hr, w + 1)
                    for c in range(FC):
                        mm = pe.transpose(psum[4 + s][:, c * P:(c + 1) * P], h[s][:, c * P:(c + 1) * P], ident[:])
                    mm.then_inc(s_ht, 1)

                def down(w, s, ww):
                    pe.wait_ge(s_hc, w + 1)
                    for c in range(FC):
                        pe.matmul(psum[6 + s][:, 0:D], hT[s][:, c * P:(c + 1) * P], ww[1](c), start=(c == 0), stop=False)
                    sel, bias = bias_sel(s, 1)
                    pe.matmul(psum[6 + s][:, 0:D], sel, bias, start=False, stop=True).then_inc(s_y, 1)

                weights_of = weights(pe)
                turn(0, 0, 0)
                turn(1, 1, 0)
                up(0, 0, weights_of(0, 0))
                turn_h(0, 0)
                with pe.Fori(0, (items - 2) // 2) as i:
                    for j in (0, 1):
                        turn(i * 2 + (2 + j), j, i + 1)
                        up(i * 2 + (1 + j), 1 - j, weights_of(i * 2 + (1 + j), 1 - j))
                        down(i * 2 + j, j, weights_of(i * 2 + j, j))
                        turn_h(i * 2 + (1 + j), 1 - j)
                up(items - 1, 1, weights_of(items - 1, 1))
                down(items - 2, 0, weights_of(items - 2, 0))
                turn_h(items - 1, 1)
                pe.wait_ge(s_xt, items + 1)
                down(items - 1, 1, weights_of(items - 1, 1))

            @block.scalar
            def _(act):
                def hidden(w, s, i):
                    act.wait_ge(s_h, w + 1)
                    act.activation(h[s][:], psum[2 + s][:], func).then_inc(s_hr, 1)
                    act.wait_ge(s_ht, w + 1)
                    act.copy(hT[s][:], psum[4 + s][:]).then_inc(s_hc, 1)

                tiles2(act, items, hidden)
                act_end(act)

            @block.vector
            def _(dve):
                dve_start(dve)

                def copy_in(w, s, i):
                    dve.wait_ge(s_tp, w + 1)
                    dve_first(dve, w, s)
                    dve.tensor_copy(xT[s][:], psum[s][:, 0:D]).then_inc(s_xt, 1)

                def result(w, s, i):
                    dve.wait_ge(s_y, w + 1)
                    take_out(dve, w, s, i, psum[6 + s][:, 0:D])

                copy_in(0, 0, 0)
                copy_in(1, 1, 0)
                with dve.Fori(0, (items - 2) // 2) as i:
                    for j in (0, 1):
                        copy_in(i * 2 + (2 + j), j, i + 1)
                        result(i * 2 + j, j, i)
                dve.wait_ge(s_y, items - 2)
                dve_first(dve, items, 0)
                dve.tensor_copy(xT[0][:], xT[0][:]).then_inc(s_xt, 1)
                result(items - 2, 0, items // 2 - 1)
                result(items - 1, 1, items // 2 - 1)
                dve_end(dve)

        with ExitStack() as st, nc.Block() as block:
            W1 = sb(st, "W1", [P, E0 * DC * F])
            W2 = sb(st, "W2", [P, E0 * FC * D])
            B1 = sb(st, "B1", [E0, F])
            B2 = sb(st, "B2", [E0, D])
            xin = [sb(st, f"xin{s}", [P, D]) for s in range(2)]
            yout = [sb(st, f"yout{s}", [P, D]) for s in range(2)]
            sel = [[sb(st, f"sel{j}_{s}", [E0, P]) for s in range(2)] for j in range(2)]
            ti = [sb(st, f"ti{s}", [P, 1], I32) for s in range(2)]
            s_ti = sem(st, "token_copied")
            s_w = sem(st, "weights")
            s_in = [sem(st, f"tile_in{s}") for s in range(2)]
            s_inf = sem(st, "tile_used")
            s_yr = sem(st, "y_ready")
            s_out = sem(st, "y_away")
            s_ys = [sem(st, f"y_stored{s}") for s in range(2)]

            def load_in(pe, w, s, i):
                pe.wait_ge(s_in[s], i * 16 + 16)
                return xin[s]

            def weights(pe):
                pe.wait_ge(s_w, 64)

                def of(w, s):
                    e = pe.value_load(tile_e[0:1, bass.ds(w, 1)], min_val=0, max_val=E0 - 1)
                    return (lambda c: W1[:, bass.ds(e * (DC * F) + c * F, F)],
                            lambda c: W2[:, bass.ds(e * (FC * D) + c * D, D)])

                return of

            def bias_sel(s, which):
                return sel[which][s][:], (B2 if which else B1)[:]

            def dve_first(dve, w, s):
                hold(dve)
                if not (isinstance(w, int) and w == 0):
                    dve.tensor_copy(sel[1][1 - s][:], tile_hot[:, bass.ds(w - 1, 1)].broadcast_to([E0, P]))
                if not (isinstance(w, int) and w == WT):
                    dve.tensor_copy(sel[0][s][:], tile_hot[:, bass.ds(w, 1)].broadcast_to([E0, P])).then_inc(s_inf, 1)

            @block.sync
            def _(sp):
                for half, (dst_, src_) in enumerate(((W1, w1), (W2, w2))):
                    sp.dma_start(dst_[:].rearrange("p (e c f) -> p e c f", e=E0, f=src_.shape[2]),
                                 src_.rearrange("e (c p) f -> p e c f", p=P)).then_inc(s_w, 16)
                sp.dma_start(B1[:], b1).then_inc(s_w, 16)
                sp.dma_start(B2[:], b2).then_inc(s_w, 16)

                def store(w, s, i):
                    sp.wait_ge(s_yr, w + 1)
                    sp.dma_start(t_moe[bass.ds(w * P, P), :], yout[s][:]).then_inc(s_ys[s], 16)
                    sp.wait_ge(s_ys[s], i * 16 + 16)
                    sp.sem_inc(s_out, 1)

                sp.sem_inc(s_out, 2)
                tiles2(sp, WT, store)

            def take_out0(dve, w, s, i, y):
                dve.wait_ge(s_out, w + 1)
                dve.tensor_copy(yout[s][:], y).then_inc(s_yr, 1)

            @block.gpsimd
            def _(pool):
                pool.sem_inc(s_inf, 2)

                def fetch(w, s, i):
                    pool.wait_ge(s_inf, w + 1)
                    pool.tensor_copy(ti[s][:], token[:, bass.ds(w, 1)]).then_inc(s_ti, 1)
                    pool.wait_ge(s_ti, w + 1)
                    hold(pool)
                    pool.indirect_dma_start(xin[s][:], None, t_xn, bass.IndirectOffsetOnAxis(
                        ap=ti[s][:, 0:1], axis=0)).then_inc(s_in[s], 16)

                tiles2(pool, WT, fetch)

            expert_pipeline(block, st, WT, ACT.Relu, load_in, weights, bias_sel, take_out0, dve_first,
                            lambda dve: None, lambda dve: None, lambda act: None)

        with ExitStack() as st, nc.Block() as block:
            Y = [sb(st, f"Y{s}", [P, 2 * D]) for s in range(2)]
            gi = [sb(st, f"gi{s}", [P, 2], I32) for s in range(2)]
            gb = sb(st, "gamma_beta0", [P, 2 * D])
            tmp = sb(st, "tmp_mix", [P, D])
            roots = root_sems(st)
            s_nx = sem(st, "norm_step")
            s_gb = sem(st, "gamma_beta")
            s_free = sem(st, "Y_free")
            s_ix = sem(st, "idx_ready")
            s_arr = [sem(st, f"Y_arrived{s}") for s in range(2)]
            s_dv = sem(st, "dve_done")

            @block.sync
            def _(sp):
                sp.dma_start(gb[:, 0:D], g0.partition_broadcast(P)).then_inc(s_gb, 16)
                sp.dma_start(gb[:, D:2 * D], be0.partition_broadcast(P)).then_inc(s_gb, 16)

            @block.gpsimd
            def _(pool):
                def fetch(n, s, i):
                    pool.wait_ge(s_free, n + 1)
                    for j in range(2):
                        pool.tensor_copy(gi[s][:, j:j + 1], place[:, bass.ds(n + j * NT, 1)]).then_inc(s_ix, 1)
                    pool.wait_ge(s_ix, n * 2 + 2)
                    hold(pool)
                    for j in range(2):
                        pool.indirect_dma_start(
                            Y[s][:, j * D:(j + 1) * D], None, t_moe,
                            bass.IndirectOffsetOnAxis(ap=gi[s][:, j:j + 1], axis=0)).then_inc(s_arr[s], 16)

                tiles2(pool, NT, fetch)

            @block.vector
            def _(dve):
                dve.sem_inc(s_free, 2)
                dve.wait_ge(s_gb, 32)
                def mixed(n, s, i):
                    done = Done(dve, s_dv, n * 2)
                    xt = XN[:, cols(n, D)]
                    dve.wait_ge(s_arr[s], i * 32 + 32)
                    done(dve.scalar_tensor_tensor(xt, Y[s][:, 0:D], mix[:, bass.ds(n, 1)], xt, ALU.mult, ALU.add))
                    done(dve.scalar_tensor_tensor(xt, Y[s][:, D:2 * D], mix[:, bass.ds(n + NT, 1)], xt,
                                                  ALU.mult, ALU.add))
                    dve.sem_inc(s_free, 1)

                tiles2(dve, NT, mixed)
                norm_stats(dve, Done(dve, s_dv, 2 * NT), XN, roots)

                def tile(n, s, i):
                    norm_onto_x(dve, Done(dve, s_nx, n * 4), XN, tmp, gb, n)

                tiles2(dve, NT, tile)

            @block.scalar
            def _(act):
                take_roots(act, roots)

        ffn0.close()
        if PHASES < 4:
            return store_out(nc, sem, X, out)

        gat = ctx.enter_context(ExitStack())
        HL = sb(gat, "HL", [P, NT * MSG])
        AM = sb(gat, "AM", [P, (NT + 1) * 2 * HEADS])
        with ExitStack() as st, nc.Block() as block:
            WX = MSG + HEADS
            W = sb(st, "W_l1", [P, DC * WX])
            att = sb(st, "att", [P, 2 * D])
            prod = sb(st, "prod", [P, D])
            xn = [sb(st, f"xn_c{s}", [P, D]) for s in range(2)]
            xT = [sb(st, f"xT_c{s}", [P, D]) for s in range(2)]
            s_w = sem(st, "weights")
            s_wx = sem(st, "weights_ready")
            s_dv = sem(st, "dve_done")
            s_xn = sem(st, "xn_ready")
            s_tp = sem(st, "turned")
            s_xt = sem(st, "xT_ready")
            s_mm = sem(st, "projected")
            s_hl = sem(st, "h_ready")
            s_st = sem(st, "stored")
            roots = root_sems(st)

            @block.sync
            def _(sp):
                wv = W[:].rearrange("p (c n) -> p c n", c=DC)
                sp.dma_start(wv[:, :, 0:D], gat_w.rearrange("(c p) n -> p c n", p=P)).then_inc(s_w, 16)
                sp.dma_start(att[:, 0:D], att_src.rearrange("h c -> (h c)").partition_broadcast(P)).then_inc(s_w, 16)
                sp.dma_start(att[:, D:2 * D], att_dst.rearrange("h c -> (h c)").partition_broadcast(P)).then_inc(s_w, 16)

                def store(n, s, i):
                    sp.wait_ge(s_hl, n + 1)
                    sp.dma_start(t_gat[bass.ds(n * P, P), :], HL[:, cols(n, MSG)]).then_inc(s_st, 16)
                    sp.dma_start(t_as[bass.ds(n * P, P), :], HL[:, bass.ds(n * MSG + D, HEADS)]).then_inc(s_st, 16)

                tiles2(sp, NT, store)
                sp.wait_ge(s_st, 32 * NT)

            @block.vector
            def _(dve):
                done = Done(dve, s_dv)
                norm_stats(dve, done, X, roots)
                normalised(dve, xn[0][:], X, 0).then_inc(s_xn, 1)
                dve.wait_ge(s_w, 48)
                for c in range(DC):
                    for j in range(2):
                        done(dve.tensor_tensor(prod[:], W[:, c * WX:c * WX + D], att[:, j * D:(j + 1) * D], ALU.mult))
                        done(dve.tensor_reduce(W[:, c * WX + D + j * HEADS:c * WX + D + (j + 1) * HEADS],
                                               prod[:].rearrange("p (h c) -> p h c", c=C), AX.X, ALU.add))
                dve.sem_inc(s_wx, 1)

                def tile(n, s, i):
                    dve.wait_ge(s_mm, n + 1)
                    if not (isinstance(n, int) and n == NT - 1):
                        normalised(dve, xn[1 - s][:], X, n + 1).then_inc(s_xn, 1)
                    dve.tensor_copy(AM[:, bass.ds(n * 2 * HEADS, HEADS)], psum[2 + s][:, MSG:WX])
                    dve.tensor_copy(HL[:, cols(n, MSG)], psum[2 + s][:, 0:MSG]).then_inc(s_hl, 1)

                tiles2(dve, NT, tile)

            @block.scalar
            def _(act):
                take_roots(act, roots)

                def turn(n, s, i):
                    act.wait_ge(s_tp, n + 1)
                    act.copy(xT[s][:], psum[s][:, 0:D]).then_inc(s_xt, 1)

                tiles2(act, NT, turn)

            @block.tensor
            def _(pe):
                pe.wait_ge(s_wx, 1)

                def project(n, s, i):
                    transposer(pe, s_xn, n, xn[s], psum[s], s_tp)
                    pe.wait_ge(s_xt, n + 1)
                    for c in range(DC):
                        mm = pe.matmul(psum[2 + s][:, 0:WX], xT[s][:, c * P:(c + 1) * P], W[:, c * WX:(c + 1) * WX],
                                       start=(c == 0), stop=(c == DC - 1))
                    mm.then_inc(s_mm, 1)

                tiles2(pe, NT, project)

        with ExitStack() as st, nc.Block() as block:
            GA = [sb(st, f"GA{s}", [P, MT * HEADS]) for s in range(SLOTS3)]
            idx = [sb(st, f"idx1_{s}", [P, MT], I32) for s in range(SLOTS3)]
            drow = [sb(st, f"drow{s}", [P, ME], I16) for s in range(SLOTS3)]
            ga_rep = [sb(st, f"ga_rep{s}", [P, MT * P]) for s in range(SLOTS3)]
            id32_i = sb(st, "id32_i", [P, NB32], I32)
            id32 = sb(st, "id32", [P, NB32])
            id_big = sb(st, "id_big", [P, WIN32])
            off = [sb(st, f"off{s}", [P, WIN32 * ME], BF16) for s in range(SLOTS3)]
            off_x = sb(st, "off_x", [P, ME])
            bmin = [sb(st, f"bmin{s}", [P, WIN32]) for s in range(SLOTS3)]
            bmin_x = sb(st, "bmin_x", [P, 1])
            macc = sb(st, "macc", [P, NB32 + WIN32 - 1])
            mq = sb(st, "mq", [P, NB32])
            MX = sb(st, "MX", [P, HEADS * NT])
            s_po = sem(st, "pool_done")
            s_ix = sem(st, "idx_ready")
            s_arr = [sem(st, f"rows_arrived{s}") for s in range(SLOTS3)]
            s_dr = [sem(st, f"drow_in{s}") for s in range(SLOTS3)]
            s_rep = sem(st, "replicated")
            s_off = sem(st, "offsets_ready")
            s_mm = sem(st, "spread")
            s_id = sem(st, "ids_ready")
            s_dv = sem(st, "dve_done")
            s_min = sem(st, "group_minima_ready")
            s_acc = sem(st, "group_done")
            s_it = sem(st, "beyond_step")
            s_q = sem(st, "max_ready")
            s_mx = sem(st, "max_moved")

            @block.gpsimd
            def _(pool):
                for hd in range(HEADS):
                    pool.iota(id32_i[hd * 32:(hd + 1) * 32, :], pattern=[[32, NB32]], base=0,
                              channel_multiplier=1).then_inc(s_po, 1)
                    pool.wait_ge(s_po, hd + 1)
                gather_groups(pool, (s_rep, s_ix, s_arr), t_as, idx, GA, HEADS, MT, MG)

            @block.sync
            def _(sp):
                def load(g, s, i):
                    sp.wait_ge(s_acc, g + 1)
                    sp.dma_start(drow[s][:], t_rel32[bass.ds(g, 1), :].broadcast_to([P, ME])).then_inc(s_dr[s], 16)

                ring(sp, 0, MG, load)
                sp.wait_ge(s_q, 1)
                for hd in range(HEADS):
                    for q in range(4):
                        sp.dma_start(MX[q * 32:(q + 1) * 32, hd * NT:(hd + 1) * NT],
                                     mq[hd * 32:(hd + 1) * 32, q * NT:(q + 1) * NT]).then_inc(s_mx, 16)
                sp.wait_ge(s_mx, 16 * 16)

            @block.scalar
            def _(act):
                act.wait_ge(s_id, 1)
                act.sem_inc(s_rep, SLOTS3)

                def prepare(g, s, i):
                    act.wait_ge(s_mm, g + 1)
                    act.wait_ge(s_arr[s], i * (16 * MT) + 16 * MT)
                    act.activation(ga_rep[s][:].rearrange("p (a r) -> p a r", r=32),
                                   GA[s][:].unsqueeze(2).broadcast_to([P, MT * HEADS, 32]), ACT.Copy,
                                   scale=-1.0).then_inc(s_rep, 1)
                    act.wait_ge(s_acc, g + 1)
                    act.wait_ge(s_dr[s], i * 16 + 16)
                    for j in range(WIN32):
                        ins = act.activation(off[s][:, j * ME:(j + 1) * ME], drow[s][:], ACT.Abs,
                                             bias=id_big[:, j:j + 1], scale=BIG)
                    ins.then_inc(s_off, 1)

                ring(act, 0, MG, prepare)

            @block.tensor
            def _(pe):
                pe.sem_inc(s_mm, SLOTS3)

                def spread(g, s, i):
                    pe.wait_ge(s_rep, g + 1 + SLOTS3)
                    pe.wait_ge(s_acc, g + 1)
                    for k in range(MT):
                        mm = pe.matmul(psum[s][:, k * P:(k + 1) * P], ga_rep[s][:, k * P:(k + 1) * P], ident[:],
                                       start=True, stop=True)
                    mm.then_inc(s_mm, 1)

                ring(pe, 0, MG, spread)

            @block.vector
            def _(dve):
                done = Done(dve, s_dv)
                dve.sem_inc(s_acc, SLOTS3)
                dve.wait_ge(s_po, 4)
                done(dve.tensor_copy(id32[:], id32_i[:]))
                dve.tensor_scalar(id_big[:], id32[:, 0:WIN32], -BIG, None, ALU.mult).then_inc(s_id, 1)
                done(dve.memset(macc[:], BIG))
                extra = dve.alloc_register("dve_extra1")
                dve.reg_mov(extra, 0)

                def smallest(dst, g_off, s):
                    return dve.tensor_tensor_reduce(g_off, g_off, psum[s][:], 1.0, BIG, ALU.add, ALU.min, dst)

                def group(g, s, i):
                    many = named(dve, ranges32, g, NB32)
                    lo = lowest(dve, ranges32, g, NB32)
                    dve.wait_ge(s_off, g + 1)
                    dve.wait_ge(s_mm, g + 1 + SLOTS3)
                    hold(dve)
                    for j in range(WIN32):
                        ins = smallest(bmin[s][:, j:j + 1], off[s][:, j * ME:(j + 1) * ME], s)
                    ins.then_inc(s_min, 1)
                    with dve.If(many > WIN32):
                        with beyond(dve, ranges32, g, NB32, WIN32) as b:
                            w = dve.snap(extra)
                            step = Done(dve, s_it, w * 4)
                            step(dve.tensor_scalar(off_x[:], drow[s][:], base32[:, bass.ds(g, 1)],
                                                   id32[:, bass.ds(b, 1)], ALU.add, ALU.not_equal))
                            step(dve.scalar_tensor_tensor(off_x[:], off_x[:], BIG, psum[s][:], ALU.mult, ALU.add))
                            step(dve.tensor_reduce(bmin_x[:], off_x[:], AX.X, ALU.min))
                            step(dve.tensor_tensor(macc[:, bass.ds(b, 1)], macc[:, bass.ds(b, 1)], bmin_x[:], ALU.min))
                            dve.reg_add(extra, extra, 1)
                    dve.wait_ge(s_min, g + 1)
                    dve.wait_ge(s_acc, g + SLOTS3)
                    at = macc[:, bass.ds(lo, WIN32)]
                    dve.tensor_tensor(at, at, bmin[s][:], ALU.min).then_inc(s_acc, 1)

                ring(dve, 0, MG, group)
                dve.wait_ge(s_acc, MG + SLOTS3)
                dve.tensor_scalar(mq[:].rearrange("p (q t) -> p q t", q=4),
                                  macc[:, 0:NB32].rearrange("p (t q) -> p q t", q=4), -1.0, None,
                                  ALU.mult).then_inc(s_q, 1)
                dve.wait_ge(s_mx, 16 * 16)

                def th(t):
                    return t.rearrange("p (h t) -> p t h", h=HEADS)

                a_src = HL[:].rearrange("p (t w) -> p t w", w=MSG)[:, :, D:MSG]
                am = AM[:, 0:NT * 2 * HEADS].rearrange("p (t w) -> p t w", w=2 * HEADS)
                a_dst, top = am[:, :, 0:HEADS], am[:, :, HEADS:2 * HEADS]
                done(dve.memset(AM[:, NT * 2 * HEADS:], 0.0))
                done(dve.tensor_tensor(top, a_src, th(MX[:]), ALU.max))
                done(dve.tensor_tensor(top, top, a_dst, ALU.add))
                done(dve.scalar_tensor_tensor(top, top, 0.2, top, ALU.mult, ALU.max))

        with ExitStack() as st, nc.Block() as block:
            AH = 2 * HEADS
            acc = sb(st, "acc1", [P, (NT + 1) * MSG])
            G = [sb(st, f"G1_{s}", [P, GT * MSG]) for s in range(SLOTS3)]
            idx = [sb(st, f"idx2_{s}", [P, GT], I32) for s in range(SLOTS3)]
            drow = [sb(st, f"drowb{s}", [P, GE], I16) for s in range(SLOTS3)]
            S = [sb(st, f"S1_{s}", [P, GT * WIN * P]) for s in range(SLOTS3)]
            T = sb(st, "T1", [P, WIN * GE])
            AMw = [sb(st, f"AMw{s}", [P, WIN * AH]) for s in range(SLOTS3)]
            left = sb(st, "left", [P, GE])
            lg = [sb(st, f"lg{s}", [P, GT * HEADS]) for s in range(SLOTS3)]
            lr = sb(st, "lr", [P, GT * HEADS])
            am_x = sb(st, "am_x", [P, GT * AH])
            self_w = sb(st, "self_w", [P, NT * HEADS])
            self_l = sb(st, "self_l", [P, NT * HEADS])
            den = sb(st, "den", [P, NT * HEADS])
            bias = sb(st, "gat_bias", [P, D])
            tmp = sb(st, "gat_tmp", [P, D])
            s_ix = sem(st, "idx_ready")
            s_arr = [sem(st, f"rows_arrived{s}") for s in range(SLOTS3)]
            s_dr = [sem(st, f"drow_in{s}") for s in range(SLOTS3)]
            s_bi = sem(st, "bias_in")
            s_dv = sem(st, "dve_done")
            s_T = sem(st, "T_ready")
            s_amw = sem(st, "window_am_ready")
            s_am = sem(st, "am_given")
            s_lg = sem(st, "logits_ready")
            s_gs = sem(st, "logit_step")
            s_ex = sem(st, "weights_ready")
            s_wt = sem(st, "rows_weighted")
            s_sel = sem(st, "selector_ready")
            s_abs = sem(st, "distance_ready")
            s_mm = sem(st, "summed")
            s_acc = sem(st, "added")
            s_lT = sem(st, "beyond_T_ready")
            s_lam = sem(st, "beyond_am_given")
            s_lama = sem(st, "beyond_am_added")
            s_sh = sem(st, "shift_ready")
            s_lsel = sem(st, "beyond_selector_ready")
            s_lmm = sem(st, "beyond_summed")
            s_lacc = sem(st, "beyond_added")
            s_self = sem(st, "self_logit")
            s_selfw = sem(st, "self_weight")
            s_fin = sem(st, "final_step")

            def am_of(s):
                return psum[2 * s][:, 512 - GT * AH:512]

            @block.gpsimd
            def _(pool):
                gather_groups(pool, (s_mm, s_ix, s_arr), t_gat, idx, G, MSG, GT, NG)

            @block.sync
            def _(sp):
                sp.dma_start(bias[:], gat_bias.partition_broadcast(P)).then_inc(s_bi, 16)

                def load(g, s, i):
                    sp.wait_ge(s_mm, g + 1)
                    sp.dma_start(drow[s][:], t_rel[bass.ds(g, 1), :].broadcast_to([P, GE])).then_inc(s_dr[s], 16)

                ring(sp, 0, NG, load)

            @block.scalar
            def _(act):
                act.wait_ge(s_self, 1)
                act.activation(self_w[:], self_l[:], ACT.Exp).then_inc(s_selfw, 1)

                def window_am(g, s):
                    lo = lowest(act, ranges, g, NT)
                    act.copy(AMw[s][:], AM[:, bass.ds(lo * AH, WIN * AH)]).then_inc(s_amw, 1)

                def select(g, s):
                    act.wait_ge(s_mm, g + 1)
                    hold(act)
                    for k in range(GT):
                        ins = act.activation(S[s][:, k * WIN * P:(k + 1) * WIN * P], iota[:], ACT.Abs,
                                             bias=dst_rel[:, bass.ds(g * GT + k, 1)], scale=-1.0)
                    ins.then_inc(s_abs, 1)
                    act.wait_ge(s_abs, g + 1)
                    act.activation(S[s][:], S[s][:], ACT.Relu, bias=1.0, scale=-1.0).then_inc(s_sel, 1)

                def weigh(g, s):
                    act.wait_ge(s_lg, g + 1)
                    act.activation(G[s][:].rearrange("p (k w) -> p k w", w=MSG)[:, :, D:MSG],
                                   lg[s][:].rearrange("p (k h) -> p k h", h=HEADS), ACT.Exp).then_inc(s_ex, 1)

                window_am(0, 0)
                select(0, 0)

                def group(g, s, i):
                    window_am(g, s)
                    weigh(g - 1, (s - 1) % SLOTS3)
                    select(g, s)

                ring(act, 1, NG, group)
                weigh(NG - 1, (NG - 1) % SLOTS3)

            @block.tensor
            def _(pe):
                gave = pe.alloc_register("pe_gave")
                extra = pe.alloc_register("pe_extra2")
                before = pe.alloc_register("pe_named_before")
                pe.reg_mov(gave, 0)
                pe.reg_mov(extra, 0)
                pe.sem_inc(s_mm, SLOTS3)

                def give_am(g, s):
                    many = named(pe, ranges, g, NT)
                    pe.wait_ge(s_amw, g + 1)
                    pe.wait_ge(s_T, g + 1)
                    for k in range(GT):
                        for j in range(WIN):
                            mm = pe.matmul(am_of(s)[:, k * AH:(k + 1) * AH], T[:, j * GE + k * P:j * GE + (k + 1) * P],
                                           AMw[s][:, j * AH:(j + 1) * AH], start=(j == 0), stop=(j == WIN - 1))
                    mm.then_inc(s_am, 1)
                    with pe.If(many > WIN):
                        with beyond(pe, ranges, g, NT, WIN) as b:
                            w = pe.snap(gave)
                            pe.wait_ge(s_lT, w + 1)
                            for k in range(GT):
                                mm = pe.matmul(psum[7][:, k * AH:(k + 1) * AH], left[:, k * P:(k + 1) * P],
                                               AM[:, cols(b, AH)], start=True, stop=True)
                            mm.then_inc(s_lam, 1)
                            pe.reg_add(gave, gave, 1)
                    return many

                def sum_group(g, s, many):
                    pe.wait_ge(s_wt, g + 1)
                    hold(pe)
                    with pe.If(many > WIN):
                        with beyond(pe, ranges, g, NT, WIN):
                            w = pe.snap(extra)
                            pe.wait_ge(s_lsel, w + 1)
                            sum_rows(pe, lambda k: left[:, k * P:(k + 1) * P], G[s], MSG, 0, psum[7]).then_inc(s_lmm, 1)
                            pe.reg_add(extra, extra, 1)
                    pe.wait_ge(s_sel, g + 1)
                    for j in range(WIN):
                        mm = sum_rows(pe, lambda k: S[s][:, k * WIN * P:(k + 1) * WIN * P], G[s], MSG, j * P,
                                      psum[2 * s + j])
                    mm.then_inc(s_mm, 1)

                pe.reg_mov(before, give_am(0, 0))

                def group(g, s, i):
                    many = give_am(g, s)
                    sum_group(g - 1, (s - 1) % SLOTS3, pe.snap(before))
                    pe.reg_mov(before, many)

                ring(pe, 1, NG, group)
                sum_group(NG - 1, (NG - 1) % SLOTS3, pe.snap(before))

            @block.vector
            def _(dve):
                done = Done(dve, s_dv)
                am = AM[:, 0:NT * AH].rearrange("p (t w) -> p t w", w=AH)
                a_dst, top = am[:, :, 0:HEADS], am[:, :, HEADS:AH]
                a_src = HL[:].rearrange("p (t w) -> p t w", w=MSG)[:, :, D:MSG]
                sl = self_l[:].rearrange("p (t h) -> p t h", h=HEADS)
                done(dve.tensor_tensor(sl, a_src, a_dst, ALU.add))
                done(dve.scalar_tensor_tensor(sl, sl, 0.2, sl, ALU.mult, ALU.max))
                dve.tensor_tensor(sl, sl, top, ALU.subtract).then_inc(s_self, 1)
                done(dve.memset(acc[:], 0.0))
                gave = dve.alloc_register("dve_gave")
                extra = dve.alloc_register("dve_extra2")
                before = dve.alloc_register("dve_named_before")
                dve.reg_mov(gave, 0)
                dve.reg_mov(extra, 0)
                dve.sem_inc(s_acc, 1)
                dve.sem_inc(s_gs, 1)

                def place_edges(g, s, i):
                    many = named(dve, ranges, g, NT)
                    dve.wait_ge(s_dr[s], i * 16 + 16)
                    for j in range(WIN):
                        ins = dve.tensor_scalar(T[:, j * GE:(j + 1) * GE], drow[s][:], node_id[:, j:j + 1], None,
                                                ALU.is_equal)
                    ins.then_inc(s_T, 1)
                    with dve.If(many > WIN):
                        dve.wait_ge(s_am, g + 1)
                        hold(dve)
                        with beyond(dve, ranges, g, NT, WIN) as b:
                            w = dve.snap(gave)
                            dve.tensor_scalar(left[:], drow[s][:], base[:, bass.ds(g, 1)], node_id[:, bass.ds(b, 1)],
                                              ALU.add, ALU.is_equal).then_inc(s_lT, 1)
                            dve.wait_ge(s_lam, w + 1)
                            part = Done(dve, s_lama, w * 2)
                            part(dve.tensor_copy(am_x[:], psum[7][:, 0:GT * AH]))
                            part(dve.tensor_tensor(am_of(s), am_of(s), am_x[:], ALU.add))
                            dve.reg_add(gave, gave, 1)
                    return many

                def weigh(g, s, i, many):
                    dve.wait_ge(s_am, g + 1)
                    dve.wait_ge(s_arr[s], i * (16 * GT) + 16 * GT)
                    gs = Done(dve, s_gs, g * 2 + 1)
                    Gv = G[s][:].rearrange("p (k w) -> p k w", w=MSG)
                    ae = am_of(s).rearrange("p (k w) -> p k w", w=AH)
                    lgv = lg[s][:].rearrange("p (k h) -> p k h", h=HEADS)
                    lrv = lr[:].rearrange("p (k h) -> p k h", h=HEADS)
                    gs(dve.tensor_tensor(lrv, Gv[:, :, D:MSG], ae[:, :, 0:HEADS], ALU.add))
                    gs(dve.scalar_tensor_tensor(lr[:], lr[:], 0.2, lr[:], ALU.mult, ALU.max))
                    dve.tensor_tensor(lgv, lrv, ae[:, :, HEADS:AH], ALU.subtract).then_inc(s_lg, 1)
                    dve.wait_ge(s_ex, g + 1)
                    hv = Gv[:, :, 0:D].rearrange("p k (h c) -> p k h c", c=C)
                    wv = Gv[:, :, D:MSG].unsqueeze(3).broadcast_to([P, GT, HEADS, C])
                    dve.tensor_tensor(hv, hv, wv, ALU.mult).then_inc(s_wt, 1)
                    with dve.If(many > WIN):
                        with beyond(dve, ranges, g, NT, WIN) as b:
                            w = dve.snap(extra)
                            select_block(dve, left, g, b, s_sh, w).then_inc(s_lsel, 1)
                            dve.wait_ge(s_lmm, w + 1)
                            dve.tensor_tensor(acc[:, cols(b, MSG)], acc[:, cols(b, MSG)], psum[7][:, 0:MSG],
                                              ALU.add).then_inc(s_lacc, 1)
                            dve.wait_ge(s_lacc, w + 1)
                            dve.reg_add(extra, extra, 1)

                def add(g, s):
                    lo = lowest(dve, ranges, g, NT)
                    dve.wait_ge(s_mm, g + 1 + SLOTS3)
                    dve.wait_ge(s_acc, g + 1)
                    av = acc[:, bass.ds(lo * MSG, WIN * MSG)].rearrange("p (j w) -> p j w", j=WIN)
                    dve.tensor_tensor(av, av, window_sums(s, MSG), ALU.add).then_inc(s_acc, 1)

                dve.reg_mov(before, place_edges(0, 0, 0))
                dve.wait_ge(s_am, 1)
                many = place_edges(1, 1, 0)
                weigh(0, 0, 0, dve.snap(before))
                dve.reg_mov(before, many)

                def group(g, s, i):
                    dve.wait_ge(s_am, g)
                    hold(dve)
                    many = place_edges(g, s, i)
                    weigh(g - 1, (s - 1) % SLOTS3, i - (1 if s == 0 else 0), dve.snap(before))
                    dve.reg_mov(before, many)
                    add(g - 2, (s - 2) % SLOTS3)

                ring(dve, 2, NG, group)
                last = NG - 1
                weigh(last, last % SLOTS3, last // SLOTS3, dve.snap(before))
                for g in (last - 1, last):
                    add(g, g % SLOTS3)
                dve.wait_ge(s_acc, NG + 1)
                dve.wait_ge(s_selfw, 1)
                dve.wait_ge(s_bi, 16)
                dn = den[:].rearrange("p (t h) -> p t h", h=HEADS)
                sw = self_w[:].rearrange("p (t h) -> p t h", h=HEADS)
                done(dve.tensor_tensor(dn, acc[:, 0:NT * MSG].rearrange("p (t w) -> p t w", w=MSG)[:, :, D:MSG], sw, ALU.add))
                done(dve.tensor_scalar(den[:], den[:], 1e-16, None, ALU.add))
                done(dve.reciprocal(den[:], den[:]))

                def tile(n, s, i):
                    f = Done(dve, s_fin, n * 6)
                    h = HL[:, bass.ds(n * MSG, D)].rearrange("p (h c) -> p h c", c=C)
                    tv = tmp[:].rearrange("p (h c) -> p h c", c=C)

                    def heads(t):
                        return t[:, cols(n, HEADS)].unsqueeze(2).broadcast_to([P, HEADS, C])

                    f(dve.tensor_tensor(tv, h, heads(self_w), ALU.mult))
                    f(dve.tensor_tensor(tmp[:], tmp[:], acc[:, bass.ds(n * MSG, D)], ALU.add))
                    f(dve.tensor_tensor(tv, tv, heads(den), ALU.mult))
                    f(dve.tensor_tensor(tmp[:], tmp[:], bias[:], ALU.add))
                    f(dve.scalar_tensor_tensor(X[:, cols(n, D)], tmp[:], 0.0, X[:, cols(n, D)], ALU.max, ALU.add))
                    f.n += 1
                    dve.sem_inc(s_fin, 1)

                tiles2(dve, NT, tile)

        gat.close()
        if PHASES < 5:
            return store_out(nc, sem, X, out)

        ffn1 = ctx.enter_context(ExitStack())
        XN = sb(ffn1, "XN1", [P, NT * D])
        chosen = sb(ffn1, "chosen", [1, 2], I32)
        mixb = sb(ffn1, "mixb", [P, 2])
        with ExitStack() as st, nc.Block() as block:
            wrs = sb(st, "wrs", [P, DC * E1])
            brs = sb(st, "brs", [1, E1])
            part = sb(st, "part", [P, D])
            ones_col = sb(st, "ones_col", [P, 1])
            mean = sb(st, "mean", [P, DC])
            row = [sb(st, f"row{j}", [1, E1]) for j in range(4)]
            one = [sb(st, f"one{j}", [1, 1]) for j in range(8)]
            pair = sb(st, "pair", [1, 2])
            s_w = sem(st, "weights")
            s_dv = sem(st, "dve_done")
            s_pe = sem(st, "pe_done")
            s_go = sem(st, "to_pe")
            s_a = sem(st, "to_act")
            s_ab = sem(st, "from_act")
            roots = root_sems(st)

            @block.sync
            def _(sp):
                sp.dma_start(wrs[:].rearrange("p (c n) -> p c n", c=DC),
                             wr.rearrange("(c p) n -> p c n", p=P)).then_inc(s_w, 16)
                sp.dma_start(brs[:], br.rearrange("(a n) -> a n", a=1)).then_inc(s_w, 16)

            @block.vector
            def _(dve):
                done = Done(dve, s_dv)
                norm_stats(dve, done, X, roots)
                with dve.Fori(0, NT) as n:
                    normalised(dve, XN[:, cols(n, D)], X, n).then_inc(s_dv, 1)
                done.n += NT
                dve.wait_ge(s_dv, done.n)
                done(dve.tensor_scalar(part[:, 0:1], node_id[:, NT - 1:NT], float(N), None, ALU.is_lt))
                done(dve.tensor_scalar(XN[:, (NT - 1) * D:], XN[:, (NT - 1) * D:], part[:, 0:1], None, ALU.mult))
                done(dve.memset(ones_col[:], 1.0))
                done(dve.tensor_reduce(part[:], XN[:].rearrange("p (t d) -> p d t", d=D), AX.X, ALU.add))
                dve.sem_inc(s_go, 1)
                dve.wait_ge(s_pe, 1)
                done(dve.tensor_scalar(mean[:], psum[0][:, 0:DC], 1.0 / N, None, ALU.mult))
                dve.sem_inc(s_go, 1)
                dve.wait_ge(s_pe, 2)
                a, b, c, d = (r[:] for r in row)
                acts = [0]

                def softmax(to, of, width, o):
                    done(dve.tensor_reduce(one[o][:], of, AX.X, ALU.max))
                    done(dve.tensor_scalar(to, of, one[o][:], None, ALU.subtract))
                    dve.sem_inc(s_a, 1)
                    acts[0] += 1
                    dve.wait_ge(s_ab, acts[0])
                    done(dve.tensor_reduce(one[o + 1][:], to, AX.X, ALU.add))
                    done(dve.reciprocal(one[o + 1][:], one[o + 1][:]))
                    done(dve.tensor_scalar(to, to, one[o + 1][:], None, ALU.mult))

                done(dve.tensor_copy(a, psum[1][0:1, 0:E1]))
                softmax(b, a, E1, 0)
                done(dve.tensor_scalar(c, b, float(N), None, ALU.mult))
                done(dve.tensor_scalar(d, c, CAPACITY, None, ALU.max))
                done(dve.reciprocal(d, d))
                done(dve.tensor_scalar(d, d, CAPACITY, None, ALU.mult))
                done(dve.tensor_tensor(a, b, d, ALU.mult))
                softmax(b, a, E1, 2)
                for j in range(2):
                    done(dve.tensor_reduce(pair[:, j:j + 1], b, AX.X, ALU.max))
                    done(dve.tensor_scalar(c, b, pair[:, j:j + 1], None, ALU.is_ge))
                    done(dve.scalar_tensor_tensor(c, c, -1000.0, iota[0:1, 0:E1], ALU.mult, ALU.add))
                    done(dve.tensor_reduce(one[4][:], c, AX.X, ALU.min))
                    done(dve.tensor_scalar(d, c, one[4][:], None, ALU.is_equal))
                    done(dve.tensor_scalar(one[5][:], one[4][:], 1000.0, None, ALU.add))
                    done(dve.tensor_copy(chosen[:, j:j + 1], one[5][:]))
                    if j == 0:
                        done(dve.scalar_tensor_tensor(b, d, NEG, b, ALU.mult, ALU.add))
                softmax(row[0][:, 0:2], pair[:], 2, 6)
                dve.sem_inc(s_go, 1)
                dve.wait_ge(s_pe, 3)
                done(dve.tensor_copy(mixb[:], psum[2][:, 0:2]))

            @block.scalar
            def _(act):
                take_roots(act, roots)
                act.wait_ge(s_a, 1)
                act.activation(row[1][:], row[1][:], ACT.Exp).then_inc(s_ab, 1)
                act.wait_ge(s_a, 2)
                act.activation(row[1][:], row[1][:], ACT.Exp).then_inc(s_ab, 1)
                act.wait_ge(s_a, 3)
                act.activation(row[0][:, 0:2], row[0][:, 0:2], ACT.Exp).then_inc(s_ab, 1)

            @block.tensor
            def _(pe):
                pe.wait_ge(s_w, 32)
                pe.wait_ge(s_go, 1)
                for c in range(DC):
                    mm = pe.matmul(psum[0][:, c:c + 1], part[:, c * P:(c + 1) * P], ones_col[:], start=True, stop=True)
                mm.then_inc(s_pe, 1)
                pe.wait_ge(s_go, 2)
                for c in range(DC):
                    pe.matmul(psum[1][0:1, 0:E1], mean[:, c:c + 1], wrs[:, c * E1:(c + 1) * E1], start=(c == 0), stop=False)
                pe.matmul(psum[1][0:1, 0:E1], ones_row[:, 0:1], brs[:], start=False, stop=True).then_inc(s_pe, 1)
                pe.wait_ge(s_go, 3)
                pe.matmul(psum[2][:, 0:2], ones_row[:], row[0][:, 0:2], start=True, stop=True).then_inc(s_pe, 1)

        with ExitStack() as st, nc.Block() as block:
            W1 = sb(st, "W1b", [P, 2 * DC * F])
            W2 = sb(st, "W2b", [P, 2 * FC * D])
            B1 = sb(st, "B1b", [1, 2 * F])
            B2 = sb(st, "B2b", [1, 2 * D])
            gb = sb(st, "gamma_beta1", [P, 2 * D])
            xin = [sb(st, f"xinb{s}", [P, D]) for s in range(2)]
            tmp = sb(st, "tmpb", [P, D])
            roots = root_sems(st)
            s_nx = sem(st, "norm_step")
            s_w = sem(st, "weights")
            s_in = sem(st, "tile_in")
            s_gb = sem(st, "gamma_beta")
            s_used = sem(st, "tile_used")
            s_dv = sem(st, "dve_done")
            s_o = sem(st, "X_done")
            s_os = sem(st, "out_stored")

            def load_in(pe, w, s, i):
                pe.wait_ge(s_in, w + 1)
                return xin[s]

            def weights(pe):
                pe.wait_ge(s_w, 16 * 8)

                def of(w, s):
                    return (lambda c: W1[:, (s * DC + c) * F:(s * DC + c + 1) * F],
                            lambda c: W2[:, (s * FC + c) * D:(s * FC + c + 1) * D])

                return of

            def bias_sel(s, which):
                return ones_row[:], (B2[:, s * D:(s + 1) * D] if which else B1[:, s * F:(s + 1) * F])

            def dve_start(dve):
                dve.wait_ge(s_gb, 32)

            def dve_first(dve, w, s):
                if not (isinstance(w, int) and w == 2 * NT):
                    dve.sem_inc(s_used, 1)

            def take_out(dve, w, s, i, res):
                xt = XN[:, cols(i, D)]
                dve.scalar_tensor_tensor(xt, res, mixb[:, s:s + 1], xt, ALU.mult, ALU.add).then_inc(s_dv, 1)
                dve.wait_ge(s_dv, i * 2 + (s + 1))

            def dve_end(dve):
                norm_stats(dve, Done(dve, s_dv, 2 * NT), XN, roots)

                def tile(n, s, i):
                    norm_onto_x(dve, Done(dve, s_nx, n * 4), XN, tmp, gb, n)
                    dve.sem_inc(s_o, 1)

                tiles2(dve, NT, tile)

            @block.gpsimd
            def _(pool):
                pool.sem_inc(s_used, 2)

                def give(n, i):
                    for s in range(2):
                        pool.wait_ge(s_used, n * 2 + (s + 1))
                        hold(pool)
                        pool.tensor_copy(xin[s][:], XN[:, cols(n, D)]).then_inc(s_in, 1)

                with pool.Fori(0, NT) as n:
                    give(n, n)

            @block.sync
            def _(sp):
                for j in range(2):
                    e = sp.value_load(chosen[0:1, j:j + 1], min_val=0, max_val=E1 - 1)
                    sp.dma_start(W1[:, j * DC * F:(j + 1) * DC * F].rearrange("p (c f) -> p c f", f=F),
                                 w1b[bass.ds(e, 1)].rearrange("e (c p) f -> p (e c) f", p=P)).then_inc(s_w, 16)
                    sp.dma_start(W2[:, j * FC * D:(j + 1) * FC * D].rearrange("p (c f) -> p c f", f=D),
                                 w2b[bass.ds(e, 1)].rearrange("e (c p) f -> p (e c) f", p=P)).then_inc(s_w, 16)
                    sp.dma_start(B1[:, j * F:(j + 1) * F], b1b[bass.ds(e, 1), :]).then_inc(s_w, 16)
                    sp.dma_start(B2[:, j * D:(j + 1) * D], b2b[bass.ds(e, 1), :]).then_inc(s_w, 16)
                sp.dma_start(gb[:, 0:D], g1.partition_broadcast(P)).then_inc(s_gb, 16)
                sp.dma_start(gb[:, D:2 * D], be1.partition_broadcast(P)).then_inc(s_gb, 16)
                with sp.Fori(0, NT - 1) as n:
                    sp.wait_ge(s_o, n + 1)
                    sp.dma_start(out[bass.ds(n * P, P), :], X[:, cols(n, D)]).then_inc(s_os, 16)
                sp.wait_ge(s_o, NT)
                sp.dma_start(out[(NT - 1) * P:N, :], X[0:LAST, (NT - 1) * D:NT * D]).then_inc(s_os, 16)
                sp.wait_ge(s_os, 16 * NT)

            expert_pipeline(block, st, 2 * NT, ACT.Gelu, load_in, weights, bias_sel, take_out, dve_first, dve_start,
                            dve_end, lambda act: take_roots(act, roots))


PHASES = 9


def store_out(nc, sem, X, out):
    with ExitStack() as st, nc.Block() as block:
        s = sem(st, "out_stored")

        @block.sync
        def _(sp):
            sp.dma_start(out[0:(NT - 1) * P, :].rearrange("(t p) d -> p t d", p=P),
                         X[:, 0:(NT - 1) * D].rearrange("p (t d) -> p t d", d=D)).then_inc(s, 16)
            sp.dma_start(out[(NT - 1) * P:N, :], X[0:LAST, (NT - 1) * D:NT * D]).then_inc(s, 16)
            sp.wait_ge(s, 32)


_WEIGHTS = ["L0_gnn_W_self", "L0_gnn_W_neigh", "L0_ffn_gate_w", "L0_ffn_gate_b", "L0_ffn_w1", "L0_ffn_b1",
            "L0_ffn_w2", "L0_ffn_b2", "L0_ffn_gamma", "L0_ffn_beta", "L1_gnn_W", "L1_gnn_att_src",
            "L1_gnn_att_dst", "L1_gnn_bias", "L1_ffn_Wr", "L1_ffn_br", "L1_ffn_W1", "L1_ffn_b1", "L1_ffn_W2",
            "L1_ffn_b2", "L1_ffn_gamma", "L1_ffn_beta"]


def kernel(**inputs):
    import numpy as _np
    import concourse.bacc as _bacc
    from concourse import mybir as _mybir
    from concourse.bass_utils import run_bass_kernel_spmd as _run

    src = _np.zeros(NG * GE, _np.int32)
    dst = _np.full(NG * GE, NPAD - 1, _np.int32)
    src[:E] = _np.asarray(inputs["src"])
    dst[:E] = _np.asarray(inputs["dst"])
    given = {"x": inputs["x"], "src_cols": src.reshape(NG * GT, P).T, "dst_cols": dst.reshape(NG * GT, P).T,
             "dst_rows": dst.reshape(MG, ME), **{n: inputs[n] for n in _WEIGHTS}}
    nc = _bacc.Bacc("TRN2", target_bir_lowering=False, num_devices=1)
    arrays, args = {}, []
    for name, a in given.items():
        a = _np.ascontiguousarray(a)
        arrays[f"in_{name}"] = a
        args.append(nc.dram_tensor(f"in_{name}", a.shape, _mybir.dt.from_np(a.dtype), kind="ExternalInput").ap())
    args.append(nc.dram_tensor("out_x", (N, D), _mybir.dt.float32, kind="ExternalOutput").ap())
    program(nc, *args)
    r = _run(nc, [arrays], core_ids=[0])
    return r.results[0]["out_x"]
```

```python
from contextlib import ExitStack

import concourse.bass as bass
from concourse import mybir

ALU = mybir.AluOpType
ACT = mybir.ActivationFunctionType
AX = mybir.AxisListType
F32 = mybir.dt.float32
BF16 = mybir.dt.bfloat16
I32 = mybir.dt.int32
I16 = mybir.dt.int16

P = 128
N = 3125
D = 256
NT = -(-N // P)
LAST = N - (NT - 1) * P
NPAD = NT * P
E = 50000
GT = 8
GE = GT * P
NG = -(-E // GE)
MT = 4
ME = MT * P
MG = NG * GT // MT
SLOTS3 = 3
WIN, WIN32 = 2, 3
NORM = 5
BIG = float(2 ** 100)
HEADS = 4
C = D // HEADS
NB32 = NPAD // 32
F = 512
DC, FC = D // P, F // P
E0 = 16
E1 = 8
WT = (2 * N + E0 * (P - 1)) // P
SLOTS = WT * P
LEAST = -(-2 * N // P)
NEG = -1.0e30
LN_EPS = 1e-5
MSG = D + HEADS
CAPACITY = float(-(-N * 125 // (100 * E1)))


def cols(i, width, offset=0):
    return bass.ds(i * width + offset, width)


def tiles2(eng, count, body, tail=None):
    rounds = (count - (count % 2 if tail is None else tail)) // 2
    with eng.Fori(0, rounds) as i:
        body(i * 2, 0, i)
        body(i * 2 + 1, 1, i)
    for n in range(rounds * 2, count):
        body(n, n % 2, n // 2)


def within(n, count):
    return not isinstance(n, int) or n < count


def ring(eng, first, end, body):
    rounds = (end - first) // SLOTS3
    with eng.Fori(0, rounds) as i:
        for k in range(SLOTS3):
            body(i * SLOTS3 + (first + k), (first + k) % SLOTS3, i + (first + k) // SLOTS3)
    for g in range(first + rounds * SLOTS3, end):
        body(g, g % SLOTS3, g // SLOTS3)


class Done:

    def __init__(self, eng, sem, base=0):
        self.eng, self.sem, self.base, self.n = eng, sem, base, 0

    def __call__(self, ins, wait=True):
        self.n += 1
        ins.then_inc(self.sem, 1)
        if wait:
            self.eng.wait_ge(self.sem, self.base + self.n)


def program(nc, x, src_cols, dst_cols, dst_rows, w_self, w_neigh, gate_w, gate_b, w1, b1, w2, b2, g0, be0,
            gat_w, att_src, att_dst, gat_bias, wr, br, w1b, b1b, w2b, b2b, g1, be1, out):
    with ExitStack() as ctx:
        sems = [0]
        used = []

        def sem(scope, name):
            sems[0] += 1
            handle = scope.enter_context(nc.semaphore(f"{name}_{sems[0]}"))
            if scope is not ctx:
                used.append(handle)
            return handle

        def sb(scope, name, shape, dt=F32):
            return scope.enter_context(nc.sbuf_tensor(name, shape, dt))

        def ps(scope, name, width=512):
            return scope.enter_context(nc.psum_tensor(name, [P, width], F32))

        def dram(name, shape, dt=F32):
            return nc.dram_tensor(name, shape, dt).ap()

        t_neigh = dram("t_neigh", [NPAD, D])
        t_ranges = dram("t_ranges", [NG, 4], I32)
        t_ranges32 = dram("t_ranges32", [MG, 4], I32)
        t_rel = dram("t_rel", [NG, GE], I16)
        t_rel32 = dram("t_rel32", [MG, ME], I16)
        t_xn = dram("t_xn", [NPAD, D])
        t_moe = dram("t_moe", [SLOTS, D])
        t_gat = dram("t_gat", [NPAD, MSG])
        t_as = dram("t_as", [NPAD, HEADS])

        X = sb(ctx, "X", [P, NT * D])
        ident = sb(ctx, "ident", [P, P])
        iota = sb(ctx, "iota", [P, WIN * P])
        block_neg = sb(ctx, "block_neg", [P, NT])
        node_id = sb(ctx, "node_id", [P, NT])
        src_i = sb(ctx, "src_i", [P, NG * GT], I32)
        shift = sb(ctx, "shift", [P, 1])
        dst_rel = sb(ctx, "dst_rel", [P, NG * GT])
        base = sb(ctx, "base", [P, NG])
        base32 = sb(ctx, "base32", [P, MG])
        ranges = sb(ctx, "ranges", [1, NG * 4], I32)
        ranges32 = sb(ctx, "ranges32", [1, MG * 4], I32)
        stats = sb(ctx, "stats", [P, NT * 6])
        mv = sb(ctx, "mv", [P, NT * 2])
        rstd = sb(ctx, "rstd", [P, NT])
        ones_row = sb(ctx, "ones_row", [1, P])
        banks = ps(ctx, "banks", 8 * 512)
        psum = [banks[:, i * 512:(i + 1) * 512] for i in range(8)]

        s_hold = sem(ctx, "hold")

        def hold(eng):
            eng.sem_inc(s_hold, 1)

        def norm_stats(dve, done, src, roots):
            with dve.Fori(0, NT // NORM) as i:
                for k in range(NORM):
                    dve.bn_stats(stats[:, cols(i * NORM + k, 6)], src[:, cols(i * NORM + k, D)]).then_inc(done.sem, 1)
            done.n += NT
            aggregate(dve, done, roots)

        def aggregate(dve, done, roots):
            dve.wait_ge(done.sem, done.base + done.n)
            for n in range(NT):
                done(dve.bn_aggr(mv[:, n * 2:n * 2 + 2], stats[:, n * 6:n * 6 + 6]), wait=(n == NT - 1))
            asked, given = roots
            dve.tensor_scalar(rstd[:], mv[:, 1:2 * NT:2], LN_EPS, None, ALU.add).then_inc(asked, 1)
            dve.wait_ge(given, 1)
            done(dve.reciprocal(rstd[:], rstd[:]))

        def take_roots(act, roots):
            asked, given = roots
            act.wait_ge(asked, 1)
            act.activation(rstd[:], rstd[:], ACT.Sqrt).then_inc(given, 1)

        def root_sems(st):
            return sem(st, "variance_ready"), sem(st, "root_ready")

        def normalised(dve, dst, src, n):
            return dve.tensor_scalar(dst, src[:, cols(n, D)], mv[:, bass.ds(n * 2, 1)], rstd[:, bass.ds(n, 1)],
                                     ALU.subtract, ALU.mult)

        def norm_onto_x(dve, step, y, tmp, gb, ready):
            def some(n):
                for j in range(NORM):
                    dve.scalar_tensor_tensor(tmp[j][:], y[:, cols(n + j, D)], mv[:, bass.ds(n * 2 + j * 2, 1)], gb[:, 0:D],
                                             ALU.subtract, ALU.mult).then_inc(step, 1)
                for j in range(NORM):
                    dve.wait_ge(step, n + (1 + j))
                    xt = X[:, cols(n + j, D)]
                    dve.scalar_tensor_tensor(xt, tmp[j][:], rstd[:, bass.ds(n + j, 1)], xt,
                                             ALU.mult, ALU.add).then_inc(ready, 1)
                dve.wait_ge(ready, n + NORM)

            with dve.Fori(0, NT // NORM) as i:
                some(i * NORM)

        with ExitStack() as st, nc.Block() as block:
            dst_i = sb(st, "dst_i", [P, NG * GT], I32)
            rows = [sb(st, "rows", [NG, GE], I32), sb(st, "rows32", [MG, ME], I32)]
            rel = [sb(st, "rel", [NG, GE], I16), sb(st, "rel32", [MG, ME], I16)]
            rng = [sb(st, "rng", [NG, 4], I32), sb(st, "rng32", [MG, 4], I32)]
            first = [sb(st, "first", [NG, 1]), sb(st, "first32", [MG, 1])]
            lo_b = [sb(st, "lo_b", [P, NG * 4], I32), sb(st, "lo_b32", [P, MG * 4], I32)]
            ids = sb(st, "ids", [P, WIN * P], I32)
            s_tail = sem(st, "tail_zeroed")
            s_ld = sem(st, "loaded")
            s_dv = sem(st, "dve_done")
            s_po = sem(st, "pool_done")
            s_rng = sem(st, "ranges_ready")
            s_rst = sem(st, "ranges_stored")
            s_rel = sem(st, "relative_stored")
            s_rld = sem(st, "ranges_loaded")

            @block.sync
            def _(sp):
                sp.dma_start(rows[0][:], dst_rows.rearrange("(g a) e -> g (a e)", a=GT // MT)).then_inc(s_ld, 16)
                sp.dma_start(rows[1][:], dst_rows).then_inc(s_ld, 16)
                sp.dma_start(dst_i[:], dst_cols).then_inc(s_ld, 16)
                sp.dma_start(src_i[:], src_cols).then_inc(s_ld, 16)
                sp.dma_start(X[:, 0:(NT - 1) * D].rearrange("p (t d) -> p t d", d=D),
                             x[0:(NT - 1) * P, :].rearrange("(t p) d -> p t d", p=P)).then_inc(s_ld, 16)
                sp.wait_ge(s_tail, 1)
                sp.dma_start(X[0:LAST, (NT - 1) * D:NT * D], x[(NT - 1) * P:N, :]).then_inc(s_ld, 16)
                sp.wait_ge(s_rng, 1)
                sp.dma_start(t_ranges, rng[0][:]).then_inc(s_rst, 16)
                sp.dma_start(t_ranges32, rng[1][:]).then_inc(s_rst, 16)
                sp.dma_start(t_rel, rel[0][:]).then_inc(s_rel, 16)
                sp.dma_start(t_rel32, rel[1][:]).then_inc(s_rel, 16)
                sp.wait_ge(s_rst, 32)
                for table, row, copies in ((t_ranges, ranges, lo_b[0]), (t_ranges32, ranges32, lo_b[1])):
                    flat = table.rearrange("(a g) f -> a (g f)", a=1)
                    sp.dma_start(row[:], flat).then_inc(s_rld, 16)
                    sp.dma_start(copies[:], flat.broadcast_to([P, copies.shape[1]])).then_inc(s_rld, 16)
                sp.wait_ge(s_rld, 64)
                sp.wait_ge(s_rel, 32)
                sp.wait_ge(s_ld, 96)

            @block.gpsimd
            def _(pool):
                done = Done(pool, s_po)
                done(pool.memset(ident[:], 0.0))
                done(pool.affine_select(out=ident[:], in_=ident[:], compare_op=ALU.not_equal, fill=1.0, base=0,
                                        pattern=[[-1, P]], channel_multiplier=1))
                for dst, step, per_partition in ((iota, 1, 0), (node_id, P, 1), (block_neg, -P, 0)):
                    wide = dst.shape[1]
                    done(pool.iota(ids[:, 0:wide], pattern=[[step, wide]], base=0, channel_multiplier=per_partition))
                    done(pool.tensor_copy(dst[:], ids[:, 0:wide]))
                done(pool.memset(ones_row[:], 1.0))

            @block.vector
            def _(dve):
                done = Done(dve, s_dv)
                dve.memset(X[:, (NT - 1) * D:NT * D], 0.0).then_inc(s_tail, 1)
                dve.wait_ge(s_ld, 96)
                for j, shift in ((0, 7), (1, 5)):
                    r = rng[j]
                    done(dve.tensor_reduce(r[:, 0:1], rows[j][:], AX.X, ALU.min))
                    done(dve.tensor_reduce(r[:, 1:2], rows[j][:], AX.X, ALU.max))
                    done(dve.tensor_single_scalar(r[:, 0:2], r[:, 0:2], shift, ALU.arith_shift_right))
                    done(dve.tensor_scalar(r[:, 1:2], r[:, 1:2], 1.0, None, ALU.add))
                    done(dve.tensor_tensor(r[:, 2:3], r[:, 1:2], r[:, 0:1], ALU.subtract))
                    done(dve.tensor_copy(r[:, 3:4], r[:, 0:1]))
                    done(dve.tensor_scalar(first[j][:], r[:, 0:1], float(2 ** shift), None, ALU.mult))
                    done(dve.tensor_scalar(rel[j][:], rows[j][:], first[j][:], None, ALU.subtract))
                dve.sem_inc(s_rng, 1)
                dve.wait_ge(s_rld, 64)
                done(dve.tensor_scalar(base[:], lo_b[0][:].rearrange("p (g f) -> p g f", f=4)[:, :, 0], float(P), None,
                                       ALU.mult))
                done(dve.tensor_scalar(base32[:], lo_b[1][:].rearrange("p (g f) -> p g f", f=4)[:, :, 0], 32.0, None,
                                       ALU.mult))
                done(dve.tensor_tensor(dst_rel[:].rearrange("p (g k) -> p g k", k=GT),
                                       dst_i[:].rearrange("p (g k) -> p g k", k=GT),
                                       base[:].unsqueeze(2).broadcast_to([P, NG, GT]), ALU.subtract))

        def transposer(pe, ready, n, xn, bank, landed):
            pe.wait_ge(ready, n + 1)
            pe.transpose(bank[:, 0:P], xn[:, 0:P], ident[:])
            pe.transpose(bank[:, P:2 * P], xn[:, P:2 * P], ident[:]).then_inc(landed, 1)

        with ExitStack() as st, nc.Block() as block:
            W = sb(st, "W_l0", [P, DC * 512])
            HS = sb(st, "HS", [P, NT * D])
            xn = [sb(st, f"xn_a{s}", [P, D]) for s in range(2)]
            xT = [sb(st, f"xT_a{s}", [P, D]) for s in range(2)]
            shifted = sb(st, "shifted", [P, NT])
            top = [sb(st, f"top{j}", [P, 8]) for j in range(2)]
            work = [sb(st, f"work{j}", [P, D]) for j in range(2)]
            s_w = sem(st, "weights")
            s_dv = sem(st, "dve_done")
            s_tk = sem(st, "top_done")
            s_go = sem(st, "statistics_ready")
            s_xn = sem(st, "xn_ready")
            s_tp = sem(st, "turned")
            s_xt = sem(st, "xT_ready")
            s_mm = sem(st, "projected")
            s_hs = sem(st, "sparse_ready")
            s_st = sem(st, "table_stored")
            roots = root_sems(st)

            @block.sync
            def _(sp):
                wv = W[:].rearrange("p (c n) -> p c n", c=DC)
                sp.dma_start(wv[:, :, 0:D], w_self.rearrange("(c p) n -> p c n", p=P)).then_inc(s_w, 16)
                sp.dma_start(wv[:, :, D:2 * D], w_neigh.rearrange("(c p) n -> p c n", p=P)).then_inc(s_w, 16)

                def store(n, s, i):
                    sp.wait_ge(s_hs, n + 5)
                    sp.dma_start(t_neigh[bass.ds(n * P, P), :], HS[:, cols(n, D)]).then_inc(s_st, 16)

                tiles2(sp, NT, store)
                sp.wait_ge(s_st, 16 * NT)

            @block.vector
            def _(dve):
                norm_stats(dve, Done(dve, s_dv), X, roots)
                dve.scalar_tensor_tensor(shifted[:], mv[:, 0:2 * NT:2], -1.0, rstd[:], ALU.mult, ALU.mult).then_inc(s_go, 1)

                def largest(n, bank, count):
                    dve.wait_ge(s_mm, n + count)
                    done = Done(dve, s_tk, n * 9)
                    tiles = range(count)
                    h = [psum[bank + j] for j in tiles]
                    for j in tiles:
                        xt = X[:, cols(n + j, D)]
                        done(dve.tensor_tensor(xt, xt, h[j][:, 0:D], ALU.add), wait=False)
                    for r in range(4):
                        left = [h[j][:, D:2 * D] if r == 0 else work[j][:] for j in tiles]
                        for j in tiles:
                            done(dve.max(top[j][:], left[j]), wait=(j == count - 1))
                        hold(dve)
                        for j in tiles:
                            done(dve.match_replace(work[j][:], top[j][:], left[j], NEG), wait=(j == count - 1))
                        hold(dve)
                    for j in tiles:
                        dve.scalar_tensor_tensor(HS[:, cols(n + j, D)], work[j][:], NEG, h[j][:, D:2 * D],
                                                 ALU.is_equal, ALU.mult).then_inc(s_hs, 1)

                rounds = (NT - 5) // 4
                with dve.Fori(0, rounds) as i:
                    largest(i * 4, 2, 2)
                    largest(i * 4 + 2, 4, 2)
                for n in range(rounds * 4, NT, 2):
                    largest(n, 2 + n % 4, min(2, NT - n))

            @block.scalar
            def _(act):
                take_roots(act, roots)

                def make(n, s):
                    act.activation(xn[s][:], X[:, cols(n, D)], ACT.Identity, bias=shifted[:, bass.ds(n, 1)],
                                   scale=rstd[:, bass.ds(n, 1)]).then_inc(s_xn, 1)

                def turn(n, s, i):
                    act.wait_ge(s_tp, n + 1)
                    act.copy(xT[s][:], psum[s][:, 0:D]).then_inc(s_xt, 1)
                    if within(n + 2, NT):
                        make(n + 2, s)

                act.wait_ge(s_go, 1)
                make(0, 0)
                make(1, 1)
                tiles2(act, NT, turn, tail=3)

            @block.tensor
            def _(pe):
                pe.wait_ge(s_w, 32)

                pe.sem_inc(s_hs, 4)

                def project_pair(n, bank, count):
                    for j in range(count):
                        transposer(pe, s_xn, n + j, xn[j], psum[j], s_tp)
                    for j in range(count):
                        pe.wait_ge(s_hs, n + (j + 1))
                        pe.wait_ge(s_xt, n + (j + 1))
                        for c in range(DC):
                            mm = pe.matmul(psum[bank + j][:], xT[j][:, c * P:(c + 1) * P], W[:, c * 512:(c + 1) * 512],
                                           start=(c == 0), stop=(c == DC - 1))
                        mm.then_inc(s_mm, 1)

                with pe.Fori(0, NT // 4) as i:
                    project_pair(i * 4, 2, 2)
                    project_pair(i * 4 + 2, 4, 2)
                for n in range(NT // 4 * 4, NT, 2):
                    project_pair(n, 2 + n % 4, min(2, NT - n))

        def gather_groups(pool, sems_, table, idx, into, width, tiles, groups):
            s_free, s_ix, s_arr = sems_

            def gather(g, s, at):
                pool.wait_ge(s_free, g + 1)
                hold(pool)
                pitch = into[s].shape[1] // tiles
                for k in range(tiles):
                    pool.indirect_dma_start(
                        into[s][:, k * pitch:k * pitch + width], None, table,
                        bass.IndirectOffsetOnAxis(ap=at[:, s * tiles + k:s * tiles + k + 1],
                                                  axis=0)).then_inc(s_arr[s], 16)

            def three(g, half, count, copied):
                pool.wait_ge(s_free, g + 1)
                pool.tensor_copy(idx[half][:, 0:count * tiles],
                                 src_i[:, bass.ds(g * tiles, count * tiles)]).then_inc(s_ix, 1)
                pool.wait_ge(s_ix, copied + 1)
                for s in range(count):
                    gather(g + s, s, idx[half])

            rounds = groups // (2 * SLOTS3)
            with pool.Fori(0, rounds) as i:
                for half in range(2):
                    three(i * (2 * SLOTS3) + half * SLOTS3, half, SLOTS3, i * 2 + half)
            for j, g in enumerate(range(rounds * 2 * SLOTS3, groups, SLOTS3)):
                three(g, j % 2, min(SLOTS3, groups - g), rounds * 2 + j)

        def lowest(eng, table, g, blocks):
            return eng.value_load(table[0:1, bass.ds(g * 4, 1)], min_val=0, max_val=blocks - 1)

        def beyond(eng, table, g, blocks, window):
            lo = lowest(eng, table, g, blocks)
            hi = eng.value_load(table[0:1, bass.ds(g * 4 + 1, 1)], min_val=1, max_val=blocks)
            return eng.Fori(lo + window, hi)

        def named(eng, table, g, blocks):
            return eng.value_load(table[0:1, bass.ds(g * 4 + 2, 1)], min_val=1, max_val=blocks)

        def select_block(dve, S, g, b, shifted, w):
            dve.tensor_tensor(shift[:], block_neg[:, bass.ds(b, 1)], base[:, bass.ds(g, 1)],
                              ALU.add).then_inc(shifted, 1)
            dve.wait_ge(shifted, w + 1)
            for k in range(GT):
                ins = dve.tensor_scalar(S[:, k * P:(k + 1) * P], iota[:, 0:P], dst_rel[:, bass.ds(g * GT + k, 1)],
                                        shift[:], ALU.subtract, ALU.is_equal)
            return ins

        def sum_rows(pe, S, rows_, width, at, bank):
            for k in range(GT):
                mm = pe.matmul(bank[:, 0:width], S(k)[:, at:at + P], rows_[:, k * width:(k + 1) * width],
                               start=(k == 0), stop=(k == GT - 1))
            return mm

        def window_sums(s, width):
            return banks[:, 2 * s * 512:(2 * s + 2) * 512].rearrange("p (j w) -> p j w", j=WIN)[:, :, 0:width]

        with ExitStack() as st, nc.Block() as block:
            AW = D + 1
            acc = sb(st, "acc0", [P, (NT + 1) * AW])
            G = [sb(st, f"G0_{s}", [P, GT * AW]) for s in range(SLOTS3)]
            idx = [sb(st, f"idx0_{s}", [P, SLOTS3 * GT], I32) for s in range(2)]
            S = [sb(st, f"S0_{s}", [P, GT * WIN * P]) for s in range(SLOTS3)]
            SL = sb(st, "SL0", [P, GE])
            deg = sb(st, "deg", [P, NT])
            s_dv = sem(st, "dve_done")
            s_ix = sem(st, "idx_ready")
            s_arr = [sem(st, f"rows_arrived{s}") for s in range(SLOTS3)]
            s_ones = sem(st, "ones_ready")
            s_sel = sem(st, "selector_ready")
            s_mm = sem(st, "summed")
            s_acc = sem(st, "added")
            s_sh = sem(st, "shift_ready")
            s_lsel = sem(st, "beyond_selector_ready")
            s_lmm = sem(st, "beyond_summed")
            s_lacc = sem(st, "beyond_added")

            @block.gpsimd
            def _(pool):
                gather_groups(pool, (s_mm, s_ix, s_arr), t_neigh, idx, G, D, GT, NG)

            @block.vector
            def _(dve):
                done = Done(dve, s_dv)
                for s in range(SLOTS3):
                    ones = G[s][:].rearrange("p (k w) -> p k w", k=GT)[:, :, D:AW]
                    dve.memset(ones, 1.0).then_inc(s_ones, 1)
                done(dve.memset(acc[:], 0.0))
                extra = dve.alloc_register("dve_extra0")
                dve.reg_mov(extra, 0)

                def select(g, s):
                    many = named(dve, ranges, g, NT)
                    dve.tensor_tensor(S[s][:].rearrange("p (k d) -> p k d", k=GT),
                                      iota[:].unsqueeze(1).broadcast_to([P, GT, WIN * P]),
                                      dst_rel[:, cols(g, GT)].unsqueeze(2).broadcast_to([P, GT, WIN * P]),
                                      ALU.is_equal).then_inc(s_sel, 1)
                    with dve.If(many > WIN):
                        with beyond(dve, ranges, g, NT, WIN) as b:
                            w = dve.snap(extra)
                            select_block(dve, SL, g, b, s_sh, w).then_inc(s_lsel, 1)
                            dve.wait_ge(s_lmm, w + 1)
                            dve.tensor_tensor(acc[:, cols(b, AW)], acc[:, cols(b, AW)], psum[6][:, 0:AW],
                                              ALU.add).then_inc(s_lacc, 1)
                            dve.wait_ge(s_lacc, w + 1)
                            dve.reg_add(extra, extra, 1)

                def add(g, s):
                    lo = lowest(dve, ranges, g, NT)
                    dve.wait_ge(s_mm, g + 1 + SLOTS3)
                    dve.wait_ge(s_acc, g + 1)
                    av = acc[:, bass.ds(lo * AW, WIN * AW)].rearrange("p (j w) -> p j w", j=WIN)
                    dve.tensor_tensor(av, av, window_sums(s, AW), ALU.add).then_inc(s_acc, 1)

                dve.sem_inc(s_acc, 1)
                select(0, 0)

                def group(g, s, i):
                    select(g, s)
                    add(g - 1, (s - 1) % SLOTS3)

                ring(dve, 1, NG, group)
                add(NG - 1, (NG - 1) % SLOTS3)
                dve.wait_ge(s_acc, NG + 1)
                count = acc[:, 0:NT * AW].rearrange("p (t w) -> p t w", w=AW)[:, :, D]
                done(dve.tensor_scalar(deg[:], count, 1.0, None, ALU.max))
                done(dve.reciprocal(deg[:], deg[:]))

                with dve.Fori(0, NT // NORM) as i:
                    for k in range(NORM):
                        n = i * NORM + k
                        dve.scalar_tensor_tensor(X[:, cols(n, D)], acc[:, bass.ds(n * AW, D)], deg[:, bass.ds(n, 1)],
                                                 X[:, cols(n, D)], ALU.mult, ALU.add)

            @block.tensor
            def _(pe):
                extra = pe.alloc_register("pe_extra0")
                pe.reg_mov(extra, 0)
                pe.wait_ge(s_ones, SLOTS3)
                pe.sem_inc(s_mm, SLOTS3)

                def group(g, s, i):
                    many = named(pe, ranges, g, NT)
                    pe.wait_ge(s_arr[s], i * (16 * GT) + 16 * GT)
                    hold(pe)
                    with pe.If(many > WIN):
                        with beyond(pe, ranges, g, NT, WIN):
                            w = pe.snap(extra)
                            pe.wait_ge(s_lsel, w + 1)
                            sum_rows(pe, lambda k: SL[:, k * P:(k + 1) * P], G[s], AW, 0, psum[6]).then_inc(s_lmm, 1)
                            pe.reg_add(extra, extra, 1)
                    pe.wait_ge(s_sel, g + 1)
                    for j in range(WIN):
                        mm = sum_rows(pe, lambda k: S[s][:, k * WIN * P:(k + 1) * WIN * P], G[s], AW, j * P,
                                      psum[2 * s + j])
                    mm.then_inc(s_mm, 1)

                ring(pe, 0, NG, group)

        with nc.Block() as block:
            @block.gpsimd
            def _(pool):
                for handle in used:
                    pool.sem_clear(handle)

        ffn0 = ctx.enter_context(ExitStack())
        mix = sb(ffn0, "mix", [P, 2 * NT])
        place = sb(ffn0, "place", [P, 2 * NT], I32)
        W1 = sb(ffn0, "W1", [P, E0 * DC * F])
        W2 = sb(ffn0, "W2", [P, E0 * FC * D])
        s_w0 = sem(ffn0, "expert_weights")
        token = sb(ffn0, "token", [P, WT], I32)
        tile_e = sb(ffn0, "tile_e", [P, WT], I32)
        tile_hot = sb(ffn0, "tile_hot", [E0, WT])
        pairs = sb(ffn0, "pairs", [P, 1], I32)
        with ExitStack() as st, nc.Block() as block:
            TE = NT * E0
            kept = [sb(st, f"kept{s}", [P, D]) for s in range(2)]
            gw = sb(st, "gw", [P, DC * E0])
            gb = sb(st, "gb", [1, E0])
            xn = [sb(st, f"xn_b{s}", [P, D]) for s in range(2)]
            xT = [sb(st, f"xT_b{s}", [P, D]) for s in range(2)]
            L = sb(st, "L", [P, TE])
            cand = sb(st, "cand", [P, TE])
            M = [sb(st, f"M{j}", [P, TE]) for j in range(2)]
            Mb = sb(st, "Mb", [P, TE], BF16)
            tot = sb(st, "tot", [P, TE])
            scan = [sb(st, f"scan{j}", [P, TE]) for j in range(2)]
            val = [sb(st, f"val{j}", [P, NT]) for j in range(2)]
            best = sb(st, "best", [P, NT])
            real = sb(st, "real", [P, NT])
            pos_i = sb(st, "pos_i", [P, 2 * NT], I32)
            pos_w = sb(st, "pos_w", [P, 2 * NT])
            pos_r = sb(st, "pos_r", [P, 2 * NT])
            hot_r = [sb(st, f"hot_r{c}", [P, P], BF16) for c in range(4)]
            hot_t = [sb(st, f"hot_t{c}", [P, WT], BF16) for c in range(4)]
            hot_w = [sb(st, f"hot_w{c}", [P, 2 * WT], BF16) for c in range(4)]
            pos = sb(st, "pos", [P, 2 * NT])
            et = [sb(st, f"et{j}", [P, E0]) for j in range(3)]
            ni = sb(st, "ni", [P, E0], I32)
            cmp = sb(st, "cmp", [P, WT * E0])
            te_f = sb(st, "te_f", [P, WT])
            pairs_f = sb(st, "pairs_f", [P, 1])
            upper = sb(st, "upper", [P, P], BF16)
            ones_b = sb(st, "ones_b", [P, P], BF16)
            s_w = sem(st, "weights")
            s_dv = sem(st, "dve_done")
            s_po = sem(st, "pool_done")
            s_xn = sem(st, "xn_ready")
            s_tp = sem(st, "turned")
            s_xt = sem(st, "xT_ready")
            s_xc = sem(st, "XN_kept")
            s_mm = sem(st, "logits_done")
            s_mb = sem(st, "choice_ready")
            s_rk = sem(st, "ranked")
            s_e = sem(st, "exp_in")
            s_ex = sem(st, "exp_out")
            s_hot = sem(st, "hot_ready")
            s_tok = sem(st, "tokens_ready")
            s_inv = sem(st, "inverted")
            s_fill = sem(st, "spare_rows_filled")
            s_st = [sem(st, f"rows_stored{s}") for s in range(2)]
            roots = root_sems(st)

            @block.sync
            def _(sp):
                sp.dma_start(gw[:].rearrange("p (c n) -> p c n", c=DC),
                             gate_w.rearrange("(c p) n -> p c n", p=P)).then_inc(s_w, 16)
                sp.dma_start(t_moe[LEAST * P:, :].rearrange("(t p) d -> p t d", p=P),
                             X[:, 0:(WT - LEAST) * D].rearrange("p (t d) -> p t d", d=D)).then_inc(s_fill, 16)
                sp.dma_start(gb[:], gate_b.rearrange("(a n) -> a n", a=1)).then_inc(s_w, 16)

                def store(n, s, i):
                    sp.wait_ge(s_xc, n + 1)
                    sp.dma_start(t_xn[bass.ds(n * P, P), :], kept[s][:]).then_inc(s_st[s], 16)

                tiles2(sp, NT, store)
                sp.wait_ge(s_fill, 16)
                sp.wait_ge(s_st[0], 16 * (NT // 2 + 1))
                sp.wait_ge(s_st[1], 16 * (NT // 2))

            @block.gpsimd
            def _(pool):
                done = Done(pool, s_po)
                pool.memset(ones_b[:], 1.0).then_inc(s_po, 1)
                done.n += 1
                done(pool.memset(upper[:], 1.0))
                done(pool.affine_select(out=upper[:], in_=upper[:], compare_op=ALU.is_gt, fill=0.0, base=0,
                                        pattern=[[1, P]], channel_multiplier=-1))

            @block.vector
            def _(dve):
                done = Done(dve, s_dv)
                norm_stats(dve, done, X, roots)
                base = done.base + done.n
                for n in range(2):
                    done(normalised(dve, xn[n][:], X, n), wait=False)

                def tile(n, s, i):
                    dve.wait_ge(s_tp, n + 1)
                    dve.wait_ge(s_xc, n + 1)
                    if within(n + 2, NT):
                        normalised(dve, xn[s][:], X, n + 2).then_inc(s_dv, 1)

                tiles2(dve, NT, tile, tail=3)
                done.n = base + NT
                dve.wait_ge(s_mm, NT)

                def te(t):
                    return t.rearrange("p (t e) -> p t e", e=E0)

                def per_token(t):
                    return t.unsqueeze(2).broadcast_to([P, NT, E0])

                def per_expert(t):
                    return t.unsqueeze(1).broadcast_to([P, NT, E0])

                e_id = iota[:, 0:E0]
                done(dve.tensor_copy(L[:], psum[2][:, 0:TE]))
                done(dve.tensor_scalar(real[:], node_id[:], float(N), None, ALU.is_lt), wait=False)
                for j in range(2):
                    done(dve.tensor_reduce(val[j][:], te(L[:]), AX.X, ALU.max))
                    done(dve.tensor_tensor(te(cand[:]), te(L[:]), per_token(val[j][:]), ALU.is_ge))
                    done(dve.scalar_tensor_tensor(te(cand[:]), te(cand[:]), -1000.0, per_expert(e_id),
                                                  ALU.mult, ALU.add))
                    done(dve.tensor_reduce(best[:], te(cand[:]), AX.X, ALU.min))
                    done(dve.tensor_tensor(te(M[j][:]), te(cand[:]), per_token(best[:]), ALU.is_equal))
                    if j == 0:
                        done(dve.scalar_tensor_tensor(L[:], M[0][:], NEG, L[:], ALU.mult, ALU.add))
                dve.tensor_tensor(best[:], val[1][:], val[0][:], ALU.subtract).then_inc(s_e, 1)
                for j in range(2):
                    done(dve.tensor_tensor(te(M[j][:]), te(M[j][:]), per_token(real[:]), ALU.mult))
                dve.tensor_tensor(Mb[:], M[0][:], M[1][:], ALU.add).then_inc(s_mb, 1)
                dve.wait_ge(s_ex, 1)
                done(dve.tensor_scalar(val[1][:], val[0][:], 1.0, None, ALU.add))
                done(dve.reciprocal(mix[:, 0:NT], val[1][:]))
                done(dve.tensor_tensor(mix[:, NT:2 * NT], mix[:, 0:NT], val[0][:], ALU.mult))
                dve.wait_ge(s_rk, 1)
                done(dve.tensor_copy(tot[:], psum[4][:, 0:TE]))
                at, step = tot, 1
                for r in range(5):
                    to = scan[r % 2]
                    w = step * E0
                    done(dve.tensor_copy(to[:, 0:w], at[:, 0:w]))
                    done(dve.tensor_tensor(to[:, w:TE], at[:, w:TE], at[:, 0:TE - w], ALU.add))
                    at, step = to, step * 2
                done(dve.tensor_scalar(ni[:], at[:, TE - E0:TE], float(P - 1), None, ALU.add))
                done(dve.tensor_single_scalar(ni[:], ni[:], 7, ALU.arith_shift_right))
                done(dve.tensor_copy(et[2][:], ni[:]))
                cur, step = et[2], 1
                for r in range(4):
                    to = et[r % 2]
                    done(dve.tensor_copy(to[:, 0:step], cur[:, 0:step]))
                    done(dve.tensor_tensor(to[:, step:E0], cur[:, step:E0], cur[:, 0:E0 - step], ALU.add))
                    cur, step = to, step * 2
                start = et[0]
                assert cur is et[1] and at is scan[0]
                done(dve.tensor_tensor(start[:], cur[:], et[2][:], ALU.subtract))
                slot = scan[1]
                done(dve.tensor_tensor(slot[:], at[:], tot[:], ALU.subtract))
                done(dve.tensor_tensor(slot[:], slot[:], psum[3][:, 0:TE], ALU.add))
                done(dve.scalar_tensor_tensor(te(slot[:]), per_expert(start[:]), float(P), te(slot[:]),
                                              ALU.mult, ALU.add))
                for j in range(2):
                    done(dve.tensor_tensor(cand[:], M[j][:], slot[:], ALU.mult))
                    done(dve.tensor_reduce(pos[:, j * NT:(j + 1) * NT], te(cand[:]), AX.X, ALU.add))
                done(dve.tensor_copy(place[:], pos[:]))
                done(dve.tensor_scalar(best[:], real[:], 1.0, None, ALU.subtract))
                for j in range(2):
                    done(dve.tensor_tensor(pos[:, j * NT:(j + 1) * NT], pos[:, j * NT:(j + 1) * NT], best[:],
                                           ALU.add))
                done(dve.tensor_copy(pos_i[:], pos[:]))
                done(dve.tensor_single_scalar(pos_i[:], pos_i[:], 7, ALU.arith_shift_right))
                done(dve.tensor_copy(pos_w[:], pos_i[:]))
                done(dve.scalar_tensor_tensor(pos_r[:], pos_w[:], -float(P), pos[:], ALU.mult, ALU.add))

                def hot(t, q, i):
                    for c in range(2):
                        dve.wait_ge(s_inv, t * 2 + (c + 1))
                        hold(dve)
                        j = bass.ds(t + c * NT, 1)
                        dve.tensor_scalar(hot_r[2 * q + c][:], iota[:, 0:P], pos_r[:, j], None, ALU.is_equal)
                        dve.tensor_scalar(hot_t[2 * q + c][:], iota[:, 0:WT], pos_w[:, j], None,
                                          ALU.is_equal).then_inc(s_hot, 1)

                tiles2(dve, NT, hot)
                dve.wait_ge(s_inv, 2 * NT + 4)
                done(dve.tensor_copy(te_f[:], psum[5][:, 0:WT]))
                done(dve.scalar_tensor_tensor(te_f[:], psum[5][:, WT:2 * WT], float(P), te_f[:], ALU.mult, ALU.add))
                done(dve.tensor_copy(token[:], te_f[:]))
                done(dve.tensor_scalar(pairs_f[:], cur[:, E0 - 1:E0], 1.0, None, ALU.subtract))
                done(dve.tensor_copy(pairs[:], pairs_f[:]))
                done(dve.tensor_single_scalar(pairs[:], pairs[:], 1, ALU.arith_shift_right))
                done(dve.tensor_tensor(cmp[:].rearrange("p (w e) -> p w e", e=E0),
                                       iota[:, 0:WT].unsqueeze(2).broadcast_to([P, WT, E0]),
                                       cur[:].unsqueeze(1).broadcast_to([P, WT, E0]), ALU.is_ge))
                done(dve.tensor_reduce(te_f[:], cmp[:].rearrange("p (w e) -> p w e", e=E0), AX.X, ALU.add))
                done(dve.tensor_scalar(te_f[:], te_f[:], float(E0 - 1), None, ALU.min))
                done(dve.tensor_copy(tile_e[:], te_f[:]))
                done(dve.tensor_scalar(tile_hot[:], te_f[0:E0, :], node_id[0:E0, 0:1], None, ALU.is_equal))

            @block.scalar
            def _(act):
                take_roots(act, roots)

                def turn(n, s, i):
                    act.wait_ge(s_tp, n + 1)
                    act.copy(xT[s][:], psum[s][:, 0:D]).then_inc(s_xt, 1)
                    if not (isinstance(i, int) and i == 0):
                        act.wait_ge(s_st[s], i * 16)
                    act.copy(kept[s][:], xn[s][:]).then_inc(s_xc, 1)

                for dst_, src_ in ((W1, w1), (W2, w2)):
                    act.dma_start(dst_[:].rearrange("p (e c f) -> p e c f", e=E0, f=src_.shape[2]),
                                  src_.rearrange("e (c p) f -> p e c f", p=P)).then_inc(s_w0, 16)
                turn(0, 0, 0)
                turn(1, 1, 0)
                with act.Fori(1, NT // 2) as i:
                    turn(i * 2, 0, i)
                    turn(i * 2 + 1, 1, i)
                turn(NT - 1, 0, NT // 2)
                act.wait_ge(s_e, 1)
                act.activation(val[0][:], best[:], ACT.Exp).then_inc(s_ex, 1)

                def name_tokens(t, q, i):
                    for c in range(2):
                        act.wait_ge(s_hot, t * 2 + (c + 1))
                        hold(act)
                        at, to = hot_t[2 * q + c], hot_w[2 * q + c]
                        act.activation(to[:, 0:WT], at[:], ACT.Identity, scale=node_id[:, 0:1])
                        act.activation(to[:, WT:2 * WT], at[:], ACT.Identity,
                                       scale=iota[:, bass.ds(t, 1)]).then_inc(s_tok, 1)

                tiles2(act, NT, name_tokens)

            @block.tensor
            def _(pe):
                pe.wait_ge(s_w, 32)
                first = 2 * NT + 1

                def turn(n, s):
                    pe.wait_ge(s_dv, n + (first + 1))
                    pe.transpose(psum[s][:, 0:P], xn[s][:, 0:P], ident[:])
                    pe.transpose(psum[s][:, P:2 * P], xn[s][:, P:2 * P], ident[:]).then_inc(s_tp, 1)

                turn(0, 0)

                def logits(n, s, i):
                    if within(n + 1, NT):
                        turn(n + 1, 1 - s)
                    pe.wait_ge(s_xt, n + 1)
                    at = psum[2][:, cols(n, E0)]
                    for c in range(DC):
                        pe.matmul(at, xT[s][:, c * P:(c + 1) * P], gw[:, c * E0:(c + 1) * E0],
                                  start=(c == 0), stop=False, skip_group_check=True)
                    pe.matmul(at, ones_row[:], gb[:], start=False, stop=True, skip_group_check=True).then_inc(s_mm, 1)

                tiles2(pe, NT, logits)
                pe.wait_ge(s_mb, 1)
                pe.wait_ge(s_po, 3)
                pe.matmul(psum[3][:, 0:TE], upper[:], Mb[:], start=True, stop=True)
                pe.matmul(psum[4][:, 0:TE], ones_b[:], Mb[:], start=True, stop=True).then_inc(s_rk, 1)

                pe.sem_inc(s_inv, 4)

                def invert(t, q, i):
                    for c in range(2):
                        pe.wait_ge(s_tok, t * 2 + (c + 1))
                        whole = isinstance(t, int)
                        pe.matmul(psum[5][:, 0:2 * WT], hot_r[2 * q + c][:], hot_w[2 * q + c][:],
                                  start=(whole and t == 0 and c == 0),
                                  stop=(whole and t == NT - 1 and c == 1)).then_inc(s_inv, 1)

                invert(0, 0, 0)
                invert(1, 1, 0)
                with pe.Fori(1, NT // 2) as i:
                    invert(i * 2, 0, i)
                    invert(i * 2 + 1, 1, i)
                invert(NT - 1, 0, NT // 2)

        with ExitStack() as st, nc.Block() as block:
            B1 = sb(st, "B1", [E0, F])
            B1T = sb(st, "B1T", [P, E0 * FC])
            B2 = sb(st, "B2", [E0, D])
            ti = [sb(st, f"ti{s}", [P, 1], I32) for s in range(2)]
            xin = [sb(st, f"xin{s}", [P, D]) for s in range(2)]
            xT = [sb(st, f"xT_f{s}", [P, D]) for s in range(2)]
            w1_of = [sb(st, f"w1_of{s}", [P, DC * F]) for s in range(2)]
            sel = [sb(st, f"sel_{s}", [E0, P]) for s in range(2)]
            hT = [sb(st, f"hT_f{s}", [P, F]) for s in range(2)]
            yout = [sb(st, f"yout{s}", [P, D]) for s in range(2)]
            s_w = sem(st, "weights")
            s_bt = sem(st, "bias_turned")
            s_b = sem(st, "bias_ready")
            s_ti = sem(st, "token_copied")
            s_in = [sem(st, f"tile_in{s}") for s in range(2)]
            s_tp = sem(st, "turned")
            s_xt = sem(st, "xT_and_weights_ready")
            s_h = sem(st, "half_hidden")
            s_hr = sem(st, "half_hidden_ready")
            s_y = sem(st, "result")
            s_yr = sem(st, "y_taken")
            s_out = sem(st, "y_away")
            s_ys = [sem(st, f"y_stored{s}") for s in range(2)]

            def tile_pairs(eng):
                return eng.value_load(pairs[0:1, 0:1], min_val=LEAST // 2 - 1, max_val=WT // 2 - 1)

            def each_tile(eng, body):
                with eng.Fori(0, tile_pairs(eng) + 1) as i:
                    body(i * 2, 0, i)
                    body(i * 2 + 1, 1, i)

            def expert(eng, w):
                return eng.value_load(tile_e[0:1, bass.ds(w, 1)], min_val=0, max_val=E0 - 1)

            @block.sync
            def _(sp):
                sp.dma_start(B1[:], b1).then_inc(s_w, 16)
                sp.dma_start(B2[:], b2).then_inc(s_w, 16)

                def store(w, s, i):
                    sp.wait_ge(s_yr, w + 3)
                    sp.dma_start(t_moe[bass.ds(w * P, P), :], yout[s][:]).then_inc(s_ys[s], 16)
                    sp.wait_ge(s_ys[s], i * 16 + 16)
                    sp.sem_inc(s_out, 1)

                sp.sem_inc(s_out, 2)
                each_tile(sp, store)

            @block.gpsimd
            def _(pool):
                def fetch(w, s, i):
                    pool.wait_ge(s_xt, w + 1)
                    pool.tensor_copy(ti[s][:], token[:, bass.ds(w, 1)]).then_inc(s_ti, 1)
                    pool.wait_ge(s_ti, w + 1)
                    hold(pool)
                    pool.indirect_dma_start(xin[s][:], None, t_xn, bass.IndirectOffsetOnAxis(
                        ap=ti[s][:, 0:1], axis=0)).then_inc(s_in[s], 16)

                each_tile(pool, fetch)

            @block.tensor
            def _(pe):
                def turn(w, s, i):
                    pe.wait_ge(s_in[s], i * 16 + 16)
                    pe.transpose(psum[s][:, 0:P], xin[s][:, 0:P], ident[:])
                    pe.transpose(psum[s][:, P:2 * P], xin[s][:, P:2 * P], ident[:]).then_inc(s_tp, 1)

                def up(w, s):
                    pe.wait_ge(s_xt, w + 3)
                    for c in range(FC):
                        for d in range(DC):
                            mm = pe.matmul(psum[2 + 2 * s + c // 2][:, (c % 2) * P:(c % 2 + 1) * P],
                                           w1_of[s][:, d * F + c * P:d * F + (c + 1) * P], xT[s][:, d * P:(d + 1) * P],
                                           start=(d == 0), stop=(d == DC - 1))
                        if c % 2:
                            mm.then_inc(s_h, 1)
                    pe.wait_ge(s_yr, w + 1)
                    pe.matmul(psum[6 + s][:, 0:D], sel[s][:], B2[:], start=True, stop=False)

                def down(w, s):
                    e = expert(pe, w)
                    for c in range(FC):
                        if c % 2 == 0:
                            pe.wait_ge(s_hr, w * 2 + (1 + c // 2))
                            hold(pe)
                        mm = pe.matmul(psum[6 + s][:, 0:D], hT[s][:, c * P:(c + 1) * P],
                                       W2[:, bass.ds(e * (FC * D) + c * D, D)], start=False, stop=(c == FC - 1))
                    mm.then_inc(s_y, 1)

                pe.wait_ge(s_w, 32)
                pe.wait_ge(s_w0, 32)
                for c in range(FC):
                    tp = pe.transpose(psum[7][:, c * E0:(c + 1) * E0], B1[:, c * P:(c + 1) * P], ident[0:E0, 0:E0])
                tp.then_inc(s_bt, 1)
                pe.wait_ge(s_b, 1)
                turn(0, 0, 0)
                turn(1, 1, 0)
                up(0, 0)
                m = tile_pairs(pe)
                with pe.Fori(0, m) as i:
                    for j in (0, 1):
                        turn(i * 2 + (2 + j), j, i + 1)
                        up(i * 2 + (1 + j), 1 - j)
                        down(i * 2 + j, j)
                up(m * 2 + 1, 1)
                down(m * 2, 0)
                down(m * 2 + 1, 1)

            @block.scalar
            def _(act):
                act.wait_ge(s_b, 1)

                def hidden(w, s, i):
                    e = expert(act, w)
                    for half in range(2):
                        act.wait_ge(s_h, w * 2 + (1 + half))
                        hold(act)
                        for k in range(2):
                            c = half * 2 + k
                            ins = act.activation(hT[s][:, c * P:(c + 1) * P],
                                                 psum[2 + 2 * s + half][:, k * P:(k + 1) * P], ACT.Relu,
                                                 bias=B1T[:, bass.ds(e * FC + c, 1)])
                        ins.then_inc(s_hr, 1)

                each_tile(act, hidden)

            @block.vector
            def _(dve):
                dve.sem_inc(s_xt, 2)
                dve.sem_inc(s_yr, 2)
                dve.wait_ge(s_bt, 1)
                dve.tensor_copy(B1T[:].rearrange("p (e c) -> p c e", c=FC),
                                psum[7][:, 0:FC * E0].rearrange("p (c e) -> p c e", e=E0)).then_inc(s_b, 1)
                dve.wait_ge(s_w0, 32)

                def stage(w, s, i):
                    e = expert(dve, w)
                    dve.wait_ge(s_tp, w + 1)
                    hold(dve)
                    dve.tensor_copy(w1_of[s][:], W1[:, bass.ds(e * (DC * F), DC * F)])
                    dve.tensor_copy(sel[s][:], tile_hot[:, bass.ds(w, 1)].broadcast_to([E0, P]))
                    dve.tensor_copy(xT[s][:], psum[s][:, 0:D]).then_inc(s_xt, 1)

                def take(w, s):
                    dve.wait_ge(s_y, w + 1)
                    dve.wait_ge(s_out, w + 1)
                    dve.tensor_copy(yout[s][:], psum[6 + s][:, 0:D]).then_inc(s_yr, 1)

                stage(0, 0, 0)
                stage(1, 1, 0)
                m = tile_pairs(dve)
                with dve.Fori(0, m) as i:
                    for j in (0, 1):
                        stage(i * 2 + (2 + j), j, i + 1)
                        take(i * 2 + j, j)
                take(m * 2, 0)
                take(m * 2 + 1, 1)

        with ExitStack() as st, nc.Block() as block:
            Y = [sb(st, f"Y{s}", [P, 2 * D]) for s in range(SLOTS3)]
            gi = [sb(st, f"gi{s}", [P, 2], I32) for s in range(SLOTS3)]
            mixed = sb(st, "mixed", [P, NT * D])
            gb = sb(st, "gamma_beta0", [P, 2 * D])
            tmp = [sb(st, f"tmp_mix{s}", [P, D]) for s in range(NORM)]
            roots = root_sems(st)
            s_nx = sem(st, "norm_step")
            s_o = sem(st, "X_done")
            s_gb = sem(st, "gamma_beta")
            s_free = sem(st, "Y_free")
            s_ix = sem(st, "idx_ready")
            s_arr = [sem(st, f"Y_arrived{s}") for s in range(SLOTS3)]
            s_dv = sem(st, "dve_done")

            @block.sync
            def _(sp):
                sp.dma_start(gb[:, 0:D], g0.partition_broadcast(P)).then_inc(s_gb, 16)
                sp.dma_start(gb[:, D:2 * D], be0.partition_broadcast(P)).then_inc(s_gb, 16)

            @block.gpsimd
            def _(pool):
                def fetch(n, s, i):
                    pool.wait_ge(s_free, n + 1)
                    for j in range(2):
                        pool.tensor_copy(gi[s][:, j:j + 1], place[:, bass.ds(n + j * NT, 1)]).then_inc(s_ix, 1)
                    pool.wait_ge(s_ix, n * 2 + 2)
                    hold(pool)
                    for j in range(2):
                        pool.indirect_dma_start(
                            Y[s][:, j * D:(j + 1) * D], None, t_moe,
                            bass.IndirectOffsetOnAxis(ap=gi[s][:, j:j + 1], axis=0)).then_inc(s_arr[s], 16)

                ring(pool, 0, NT, fetch)

            @block.vector
            def _(dve):
                dve.sem_inc(s_free, SLOTS3)
                dve.wait_ge(s_gb, 32)

                def mix_tile(n, s, i):
                    done = Done(dve, s_dv, n * 4)
                    yt = mixed[:, cols(n, D)]
                    done(normalised(dve, yt, X, n))
                    done(dve.tensor_tensor(X[:, cols(n, D)], X[:, cols(n, D)], gb[:, D:2 * D], ALU.add), wait=False)
                    dve.wait_ge(s_arr[s], i * 32 + 32)
                    done(dve.scalar_tensor_tensor(yt, Y[s][:, 0:D], mix[:, bass.ds(n, 1)], yt, ALU.mult, ALU.add))
                    dve.scalar_tensor_tensor(yt, Y[s][:, D:2 * D], mix[:, bass.ds(n + NT, 1)], yt,
                                             ALU.mult, ALU.add).then_inc(s_free, 1)
                    dve.wait_ge(s_free, n + 1 + SLOTS3)
                    dve.bn_stats(stats[:, cols(n, 6)], yt).then_inc(s_dv, 1)

                ring(dve, 0, NT, mix_tile)
                aggregate(dve, Done(dve, s_dv, 4 * NT), roots)

                norm_onto_x(dve, s_nx, mixed, tmp, gb, s_o)

            @block.scalar
            def _(act):
                take_roots(act, roots)

        ffn0.close()
        gat = ctx.enter_context(ExitStack())
        HL = sb(gat, "HL", [P, NT * MSG])
        AM = sb(gat, "AM", [P, (NT + 1) * 2 * HEADS])
        AM3 = sb(gat, "AM3", [P, (NT + 1) * 6 * HEADS], BF16)
        with ExitStack() as st, nc.Block() as block:
            WX = MSG + HEADS
            W = sb(st, "W_l1", [P, DC * WX])
            att = sb(st, "att", [P, 2 * D])
            prod = sb(st, "prod", [P, D])
            xn = [sb(st, f"xn_c{s}", [P, D]) for s in range(2)]
            xT = [sb(st, f"xT_c{s}", [P, D]) for s in range(2)]
            s_w = sem(st, "weights")
            s_wx = sem(st, "weights_ready")
            s_dv = sem(st, "dve_done")
            s_xn = sem(st, "xn_ready")
            s_tp = sem(st, "turned")
            s_xt = sem(st, "xT_ready")
            s_mm = sem(st, "projected")
            s_hl = sem(st, "h_ready")
            s_st = sem(st, "stored")
            roots = root_sems(st)

            @block.sync
            def _(sp):
                wv = W[:].rearrange("p (c n) -> p c n", c=DC)
                sp.dma_start(wv[:, :, 0:D], gat_w.rearrange("(c p) n -> p c n", p=P)).then_inc(s_w, 16)
                sp.dma_start(att[:, 0:D], att_src.rearrange("h c -> (h c)").partition_broadcast(P)).then_inc(s_w, 16)
                sp.dma_start(att[:, D:2 * D], att_dst.rearrange("h c -> (h c)").partition_broadcast(P)).then_inc(s_w, 16)

                def store(n, s, i):
                    sp.wait_ge(s_hl, n + 1)
                    sp.dma_start(t_gat[bass.ds(n * P, P), :], HL[:, cols(n, MSG)]).then_inc(s_st, 16)
                    sp.dma_start(t_as[bass.ds(n * P, P), :], HL[:, bass.ds(n * MSG + D, HEADS)]).then_inc(s_st, 16)

                tiles2(sp, NT, store)
                sp.wait_ge(s_st, 32 * NT)

            @block.vector
            def _(dve):
                done = Done(dve, s_dv)
                norm_stats(dve, done, X, roots)
                for n in range(2):
                    normalised(dve, xn[n][:], X, n).then_inc(s_xn, 1)
                dve.wait_ge(s_w, 48)
                for c in range(DC):
                    for j in range(2):
                        done(dve.tensor_tensor(prod[:], W[:, c * WX:c * WX + D], att[:, j * D:(j + 1) * D], ALU.mult))
                        done(dve.tensor_reduce(W[:, c * WX + D + j * HEADS:c * WX + D + (j + 1) * HEADS],
                                               prod[:].rearrange("p (h c) -> p h c", c=C), AX.X, ALU.add))
                dve.sem_inc(s_wx, 1)

                def tile(n, s, i):
                    if within(n + 2, NT):
                        dve.wait_ge(s_tp, n + 1)
                        normalised(dve, xn[s][:], X, n + 2).then_inc(s_xn, 1)
                    dve.wait_ge(s_mm, n + 1)
                    dve.tensor_copy(AM[:, bass.ds(n * 2 * HEADS, HEADS)], psum[2 + s][:, MSG:WX])
                    dve.tensor_copy(HL[:, cols(n, MSG)], psum[2 + s][:, 0:MSG]).then_inc(s_hl, 1)

                tiles2(dve, NT, tile, tail=3)

            @block.scalar
            def _(act):
                take_roots(act, roots)

                def turn(n, s, i):
                    act.wait_ge(s_tp, n + 1)
                    act.copy(xT[s][:], psum[s][:, 0:D]).then_inc(s_xt, 1)

                tiles2(act, NT, turn)

            @block.tensor
            def _(pe):
                pe.wait_ge(s_wx, 1)

                transposer(pe, s_xn, 0, xn[0], psum[0], s_tp)

                def project(n, s, i):
                    if within(n + 1, NT):
                        transposer(pe, s_xn, n + 1, xn[1 - s], psum[1 - s], s_tp)
                    else:
                        pe.wait_ge(s_hl, NT - 2)
                    pe.wait_ge(s_xt, n + 1)
                    for c in range(DC):
                        mm = pe.matmul(psum[2 + s][:, 0:WX], xT[s][:, c * P:(c + 1) * P], W[:, c * WX:(c + 1) * WX],
                                       start=(c == 0), stop=(c == DC - 1))
                    mm.then_inc(s_mm, 1)

                tiles2(pe, NT, project)

        with ExitStack() as st, nc.Block() as block:
            GA = [sb(st, f"GA{s}", [P, MT * HEADS]) for s in range(SLOTS3)]
            idx = [sb(st, f"idx1_{s}", [P, SLOTS3 * MT], I32) for s in range(2)]
            drow = [sb(st, f"drow{s}", [P, ME], I16) for s in range(SLOTS3)]
            ga_rep = [sb(st, f"ga_rep{s}", [P, MT * P]) for s in range(SLOTS3)]
            id32_i = sb(st, "id32_i", [P, NB32], I32)
            id32 = sb(st, "id32", [P, NB32])
            id_big = sb(st, "id_big", [P, WIN32])
            off = [sb(st, f"off{s}", [P, WIN32 * ME], BF16) for s in range(SLOTS3)]
            off_x = sb(st, "off_x", [P, ME])
            bmin = [sb(st, f"bmin{s}", [P, WIN32]) for s in range(SLOTS3)]
            bmin_x = sb(st, "bmin_x", [P, 1])
            macc = sb(st, "macc", [P, NB32 + WIN32 - 1])
            mq = sb(st, "mq", [P, NB32])
            rest = sb(st, "rest", [P, (NT + 1) * 2 * HEADS])
            MX = sb(st, "MX", [P, HEADS * NT])
            s_po = sem(st, "pool_done")
            s_ix = sem(st, "idx_ready")
            s_arr = [sem(st, f"rows_arrived{s}") for s in range(SLOTS3)]
            s_dr = [sem(st, f"drow_in{s}") for s in range(SLOTS3)]
            s_rep = sem(st, "replicated")
            s_off = sem(st, "offsets_ready")
            s_mm = sem(st, "spread")
            s_id = sem(st, "ids_ready")
            s_dv = sem(st, "dve_done")
            s_min = sem(st, "group_minima_ready")
            s_acc = sem(st, "group_done")
            s_it = sem(st, "beyond_step")
            s_q = sem(st, "max_ready")
            s_mx = sem(st, "max_moved")

            def move_max(eng, which):
                for hd in which:
                    for q in range(4):
                        eng.dma_start(MX[q * 32:(q + 1) * 32, hd * NT:(hd + 1) * NT],
                                      mq[hd * 32:(hd + 1) * 32, q * NT:(q + 1) * NT]).then_inc(s_mx, 16)

            @block.gpsimd
            def _(pool):
                for hd in range(HEADS):
                    pool.iota(id32_i[hd * 32:(hd + 1) * 32, :], pattern=[[32, NB32]], base=0,
                              channel_multiplier=1).then_inc(s_po, 1)
                    pool.wait_ge(s_po, hd + 1)
                gather_groups(pool, (s_rep, s_ix, s_arr), t_as, idx, GA, HEADS, MT, MG)

            @block.sync
            def _(sp):
                def load(g, s, i):
                    sp.wait_ge(s_acc, g + 1)
                    sp.dma_start(drow[s][:], t_rel32[bass.ds(g, 1), :].broadcast_to([P, ME])).then_inc(s_dr[s], 16)

                ring(sp, 0, MG, load)
                sp.wait_ge(s_q, 1)
                move_max(sp, (0, 1))
                sp.wait_ge(s_mx, 16 * 16)

            @block.scalar
            def _(act):
                act.wait_ge(s_id, 1)
                act.sem_inc(s_rep, SLOTS3)

                def prepare(g, s, i):
                    act.wait_ge(s_mm, g + 1)
                    act.wait_ge(s_arr[s], i * (16 * MT) + 16 * MT)
                    act.activation(ga_rep[s][:].rearrange("p (a r) -> p a r", r=32),
                                   GA[s][:].unsqueeze(2).broadcast_to([P, MT * HEADS, 32]), ACT.Copy,
                                   scale=-1.0).then_inc(s_rep, 1)
                    act.wait_ge(s_acc, g + 1)
                    act.wait_ge(s_dr[s], i * 16 + 16)
                    for j in range(WIN32):
                        ins = act.activation(off[s][:, j * ME:(j + 1) * ME], drow[s][:], ACT.Abs,
                                             bias=id_big[:, j:j + 1], scale=BIG)
                    ins.then_inc(s_off, 1)

                ring(act, 0, MG, prepare)
                act.wait_ge(s_q, 1)
                move_max(act, (2, 3))

            @block.tensor
            def _(pe):
                pe.sem_inc(s_mm, SLOTS3)

                def spread(g, s, i):
                    pe.wait_ge(s_rep, g + 1 + SLOTS3)
                    pe.wait_ge(s_acc, g + 1)
                    for k in range(MT):
                        mm = pe.matmul(psum[s][:, k * P:(k + 1) * P], ga_rep[s][:, k * P:(k + 1) * P], ident[:],
                                       start=True, stop=True)
                    mm.then_inc(s_mm, 1)

                ring(pe, 0, MG, spread)

            @block.vector
            def _(dve):
                done = Done(dve, s_dv)
                dve.sem_inc(s_acc, SLOTS3)
                dve.wait_ge(s_po, 4)
                done(dve.tensor_copy(id32[:], id32_i[:]))
                dve.tensor_scalar(id_big[:], id32[:, 0:WIN32], -BIG, None, ALU.mult).then_inc(s_id, 1)
                done(dve.memset(macc[:], BIG))
                extra = dve.alloc_register("dve_extra1")
                dve.reg_mov(extra, 0)

                def smallest(dst, g_off, s):
                    return dve.tensor_tensor_reduce(g_off, g_off, psum[s][:], 1.0, BIG, ALU.add, ALU.min, dst)

                def group(g, s, i):
                    many = named(dve, ranges32, g, NB32)
                    lo = lowest(dve, ranges32, g, NB32)
                    dve.wait_ge(s_off, g + 1)
                    dve.wait_ge(s_mm, g + 1 + SLOTS3)
                    hold(dve)
                    for j in range(WIN32):
                        ins = smallest(bmin[s][:, j:j + 1], off[s][:, j * ME:(j + 1) * ME], s)
                    ins.then_inc(s_min, 1)
                    with dve.If(many > WIN32):
                        with beyond(dve, ranges32, g, NB32, WIN32) as b:
                            w = dve.snap(extra)
                            step = Done(dve, s_it, w * 4)
                            step(dve.tensor_scalar(off_x[:], drow[s][:], base32[:, bass.ds(g, 1)],
                                                   id32[:, bass.ds(b, 1)], ALU.add, ALU.not_equal))
                            step(dve.scalar_tensor_tensor(off_x[:], off_x[:], BIG, psum[s][:], ALU.mult, ALU.add))
                            step(dve.tensor_reduce(bmin_x[:], off_x[:], AX.X, ALU.min))
                            step(dve.tensor_tensor(macc[:, bass.ds(b, 1)], macc[:, bass.ds(b, 1)], bmin_x[:], ALU.min))
                            dve.reg_add(extra, extra, 1)
                    dve.wait_ge(s_min, g + 1)
                    dve.wait_ge(s_acc, g + SLOTS3)
                    at = macc[:, bass.ds(lo, WIN32)]
                    dve.tensor_tensor(at, at, bmin[s][:], ALU.min).then_inc(s_acc, 1)

                ring(dve, 0, MG, group)
                dve.wait_ge(s_acc, MG + SLOTS3)
                dve.tensor_scalar(mq[:].rearrange("p (q t) -> p q t", q=4),
                                  macc[:, 0:NB32].rearrange("p (t q) -> p q t", q=4), -1.0, None,
                                  ALU.mult).then_inc(s_q, 1)
                dve.wait_ge(s_mx, 16 * 16)

                def th(t):
                    return t.rearrange("p (h t) -> p t h", h=HEADS)

                a_src = HL[:].rearrange("p (t w) -> p t w", w=MSG)[:, :, D:MSG]
                am = AM[:, 0:NT * 2 * HEADS].rearrange("p (t w) -> p t w", w=2 * HEADS)
                a_dst, top = am[:, :, 0:HEADS], am[:, :, HEADS:2 * HEADS]
                done(dve.memset(AM[:, NT * 2 * HEADS:], 0.0))
                done(dve.tensor_tensor(top, a_src, th(MX[:]), ALU.max))
                done(dve.tensor_tensor(top, top, a_dst, ALU.add))
                done(dve.scalar_tensor_tensor(top, top, 0.2, top, ALU.mult, ALU.max))
                parts = AM3[:].rearrange("p (t q w) -> p t q w", q=3, w=2 * HEADS)
                whole, rv = (t[:].rearrange("p (t w) -> p t w", w=2 * HEADS) for t in (AM, rest))
                done(dve.tensor_copy(parts[:, :, 0], whole))
                done(dve.tensor_tensor(rv, whole, parts[:, :, 0], ALU.subtract))
                done(dve.tensor_copy(parts[:, :, 1], rv))
                done(dve.tensor_tensor(rv, rv, parts[:, :, 1], ALU.subtract))
                done(dve.tensor_copy(parts[:, :, 2], rv))

        with ExitStack() as st, nc.Block() as block:
            AH = 2 * HEADS
            AP3 = 3 * AH
            acc = sb(st, "acc1", [P, (NT + 1) * MSG])
            G = [sb(st, f"G1_{s}", [P, GT * MSG]) for s in range(SLOTS3)]
            idx = [sb(st, f"idx2_{s}", [P, SLOTS3 * GT], I32) for s in range(2)]
            drow = [sb(st, f"drowb{s}", [P, GE], I16) for s in range(SLOTS3)]
            S = [sb(st, f"S1_{s}", [P, GT * WIN * P]) for s in range(SLOTS3)]
            T = sb(st, "T1", [P, WIN * GE], BF16)
            AMw = [sb(st, f"AMw{s}", [P, WIN * AP3], BF16) for s in range(SLOTS3)]
            left = sb(st, "left", [P, GE])
            lg = [sb(st, f"lg{s}", [P, GT * HEADS]) for s in range(SLOTS3)]
            lr = sb(st, "lr", [P, GT * HEADS])
            am_x = sb(st, "am_x", [P, GT * AH])
            am_e = sb(st, "am_e", [P, GT * AH])
            self_w = sb(st, "self_w", [P, NT * HEADS])
            self_l = sb(st, "self_l", [P, NT * HEADS])
            den = sb(st, "den", [P, NT * HEADS])
            bias = sb(st, "gat_bias", [P, D])
            tmp = [sb(st, f"gat_tmp{s}", [P, D]) for s in range(NORM)]
            s_ix = sem(st, "idx_ready")
            s_arr = [sem(st, f"rows_arrived{s}") for s in range(SLOTS3)]
            s_dr = [sem(st, f"drow_in{s}") for s in range(SLOTS3)]
            s_bi = sem(st, "bias_in")
            s_dv = sem(st, "dve_done")
            s_T = sem(st, "T_ready")
            s_amw = sem(st, "window_am_ready")
            s_am = sem(st, "am_given")
            s_lg = sem(st, "logits_ready")
            s_gs = sem(st, "logit_step")
            s_ex = sem(st, "weights_ready")
            s_wt = sem(st, "rows_weighted")
            s_sel = sem(st, "selector_ready")
            s_abs = sem(st, "distance_ready")
            s_mm = sem(st, "summed")
            s_acc = sem(st, "added")
            s_lT = sem(st, "beyond_T_ready")
            s_lam = sem(st, "beyond_am_given")
            s_lama = sem(st, "beyond_am_added")
            s_sh = sem(st, "shift_ready")
            s_lsel = sem(st, "beyond_selector_ready")
            s_lmm = sem(st, "beyond_summed")
            s_lacc = sem(st, "beyond_added")
            s_self = sem(st, "self_logit")
            s_own = sem(st, "own_loops_in")
            s_selfw = sem(st, "self_weight")
            s_fin = sem(st, "final_step")

            def am_of(s):
                return psum[2 * s][:, 512 - GT * AP3:512]

            @block.gpsimd
            def _(pool):
                gather_groups(pool, (s_mm, s_ix, s_arr), t_gat, idx, G, MSG, GT, NG)

            @block.sync
            def _(sp):
                sp.dma_start(bias[:], gat_bias.partition_broadcast(P)).then_inc(s_bi, 16)

                def load(g, s, i):
                    sp.wait_ge(s_mm, g + 1)
                    sp.dma_start(drow[s][:], t_rel[bass.ds(g, 1), :].broadcast_to([P, GE])).then_inc(s_dr[s], 16)

                ring(sp, 0, NG, load)

            @block.scalar
            def _(act):
                act.wait_ge(s_self, 1)
                act.activation(self_w[:], self_l[:], ACT.Exp).then_inc(s_selfw, 1)

                def window_am(g, s):
                    lo = lowest(act, ranges, g, NT)
                    act.copy(AMw[s][:], AM3[:, bass.ds(lo * AP3, WIN * AP3)]).then_inc(s_amw, 1)

                def select(g, s):
                    act.wait_ge(s_mm, g + 1)
                    hold(act)
                    for k in range(GT):
                        ins = act.activation(S[s][:, k * WIN * P:(k + 1) * WIN * P], iota[:], ACT.Abs,
                                             bias=dst_rel[:, bass.ds(g * GT + k, 1)], scale=-1.0)
                    ins.then_inc(s_abs, 1)
                    act.wait_ge(s_abs, g + 1)
                    act.activation(S[s][:], S[s][:], ACT.Relu, bias=1.0, scale=-1.0).then_inc(s_sel, 1)

                def weigh(g, s):
                    act.wait_ge(s_lg, g + 1)
                    act.activation(G[s][:].rearrange("p (k w) -> p k w", w=MSG)[:, :, D:MSG],
                                   lg[s][:].rearrange("p (k h) -> p k h", h=HEADS), ACT.Exp).then_inc(s_ex, 1)

                window_am(0, 0)
                select(0, 0)

                def group(g, s, i):
                    window_am(g, s)
                    weigh(g - 1, (s - 1) % SLOTS3)
                    select(g, s)

                ring(act, 1, NG, group)
                weigh(NG - 1, (NG - 1) % SLOTS3)

            @block.tensor
            def _(pe):
                gave = pe.alloc_register("pe_gave")
                extra = pe.alloc_register("pe_extra2")
                before = pe.alloc_register("pe_named_before")
                pe.reg_mov(gave, 0)
                pe.reg_mov(extra, 0)
                pe.sem_inc(s_mm, SLOTS3)

                def give_am(g, s):
                    many = named(pe, ranges, g, NT)
                    pe.wait_ge(s_amw, g + 1)
                    pe.wait_ge(s_T, g + 1)
                    for k in range(GT):
                        for j in range(WIN):
                            mm = pe.matmul(am_of(s)[:, k * AP3:(k + 1) * AP3], T[:, j * GE + k * P:j * GE + (k + 1) * P],
                                           AMw[s][:, j * AP3:(j + 1) * AP3], start=(j == 0), stop=(j == WIN - 1))
                    mm.then_inc(s_am, 1)
                    with pe.If(many > WIN):
                        with beyond(pe, ranges, g, NT, WIN) as b:
                            w = pe.snap(gave)
                            pe.wait_ge(s_lT, w + 1)
                            for k in range(GT):
                                mm = pe.matmul(psum[7][:, k * AH:(k + 1) * AH], left[:, k * P:(k + 1) * P],
                                               AM[:, cols(b, AH)], start=True, stop=True)
                            mm.then_inc(s_lam, 1)
                            pe.reg_add(gave, gave, 1)
                    return many

                def sum_group(g, s, many):
                    pe.wait_ge(s_wt, g + 1)
                    hold(pe)
                    with pe.If(many > WIN):
                        with beyond(pe, ranges, g, NT, WIN):
                            w = pe.snap(extra)
                            pe.wait_ge(s_lsel, w + 1)
                            sum_rows(pe, lambda k: left[:, k * P:(k + 1) * P], G[s], MSG, 0, psum[7]).then_inc(s_lmm, 1)
                            pe.reg_add(extra, extra, 1)
                    pe.wait_ge(s_sel, g + 1)
                    for j in range(WIN):
                        mm = sum_rows(pe, lambda k: S[s][:, k * WIN * P:(k + 1) * WIN * P], G[s], MSG, j * P,
                                      psum[2 * s + j])
                    mm.then_inc(s_mm, 1)

                pe.reg_mov(before, give_am(0, 0))

                def group(g, s, i):
                    many = give_am(g, s)
                    sum_group(g - 1, (s - 1) % SLOTS3, pe.snap(before))
                    pe.reg_mov(before, many)

                ring(pe, 1, NG, group)
                sum_group(NG - 1, (NG - 1) % SLOTS3, pe.snap(before))

            @block.vector
            def _(dve):
                done = Done(dve, s_dv)
                am = AM[:, 0:NT * AH].rearrange("p (t w) -> p t w", w=AH)
                a_dst, top = am[:, :, 0:HEADS], am[:, :, HEADS:AH]
                a_src = HL[:].rearrange("p (t w) -> p t w", w=MSG)[:, :, D:MSG]
                sl = self_l[:].rearrange("p (t h) -> p t h", h=HEADS)
                done(dve.tensor_tensor(sl, a_src, a_dst, ALU.add))
                done(dve.scalar_tensor_tensor(sl, sl, 0.2, sl, ALU.mult, ALU.max))
                dve.tensor_tensor(sl, sl, top, ALU.subtract).then_inc(s_self, 1)
                dve.memset(acc[:, NT * MSG:], 0.0)
                dve.wait_ge(s_selfw, 1)
                av = acc[:, 0:NT * MSG].rearrange("p (t w) -> p t w", w=MSG)
                done(dve.tensor_copy(av[:, :, D:MSG], self_w[:].rearrange("p (t h) -> p t h", h=HEADS)), wait=False)

                def own(n, s, i):
                    ha, hs = (t[:, bass.ds(n * MSG, D)].rearrange("p (h c) -> p h c", c=C) for t in (acc, HL))
                    dve.tensor_tensor(ha, hs, self_w[:, cols(n, HEADS)].unsqueeze(2).broadcast_to([P, HEADS, C]),
                                      ALU.mult).then_inc(s_own, 1)

                tiles2(dve, NT, own)
                dve.wait_ge(s_own, NT)
                gave = dve.alloc_register("dve_gave")
                extra = dve.alloc_register("dve_extra2")
                before = dve.alloc_register("dve_named_before")
                dve.reg_mov(gave, 0)
                dve.reg_mov(extra, 0)
                dve.sem_inc(s_acc, 1)

                def place_edges(g, s, i):
                    many = named(dve, ranges, g, NT)
                    dve.wait_ge(s_dr[s], i * 16 + 16)
                    for j in range(WIN):
                        ins = dve.tensor_scalar(T[:, j * GE:(j + 1) * GE], drow[s][:], node_id[:, j:j + 1], None,
                                                ALU.is_equal)
                    ins.then_inc(s_T, 1)
                    with dve.If(many > WIN):
                        dve.wait_ge(s_am, g + 1)
                        hold(dve)
                        with beyond(dve, ranges, g, NT, WIN) as b:
                            w = dve.snap(gave)
                            dve.tensor_scalar(left[:], drow[s][:], base[:, bass.ds(g, 1)], node_id[:, bass.ds(b, 1)],
                                              ALU.add, ALU.is_equal).then_inc(s_lT, 1)
                            dve.wait_ge(s_lam, w + 1)
                            part = Done(dve, s_lama, w * 2)
                            part(dve.tensor_copy(am_x[:], psum[7][:, 0:GT * AH]))
                            first_parts = am_of(s).rearrange("p (k w) -> p k w", w=AP3)[:, :, 0:AH]
                            part(dve.tensor_tensor(first_parts, first_parts,
                                                   am_x[:].rearrange("p (k w) -> p k w", w=AH), ALU.add))
                            dve.reg_add(gave, gave, 1)
                    return many

                def weigh(g, s, i, many):
                    dve.wait_ge(s_am, g + 1)
                    dve.wait_ge(s_arr[s], i * (16 * GT) + 16 * GT)
                    gs = Done(dve, s_gs, g * 3)
                    Gv = G[s][:].rearrange("p (k w) -> p k w", w=MSG)
                    ae = am_e[:].rearrange("p (k w) -> p k w", w=AH)
                    lgv = lg[s][:].rearrange("p (k h) -> p k h", h=HEADS)
                    lrv = lr[:].rearrange("p (k h) -> p k h", h=HEADS)
                    gs(dve.tensor_reduce(ae, am_of(s).rearrange("p (k q w) -> p k w q", q=3, w=AH), AX.X, ALU.add))
                    gs(dve.tensor_tensor(lrv, Gv[:, :, D:MSG], ae[:, :, 0:HEADS], ALU.add))
                    gs(dve.scalar_tensor_tensor(lr[:], lr[:], 0.2, lr[:], ALU.mult, ALU.max))
                    dve.tensor_tensor(lgv, lrv, ae[:, :, HEADS:AH], ALU.subtract).then_inc(s_lg, 1)
                    dve.wait_ge(s_ex, g + 1)
                    hv = Gv[:, :, 0:D].rearrange("p k (h c) -> p k h c", c=C)
                    wv = Gv[:, :, D:MSG].unsqueeze(3).broadcast_to([P, GT, HEADS, C])
                    dve.tensor_tensor(hv, hv, wv, ALU.mult).then_inc(s_wt, 1)
                    with dve.If(many > WIN):
                        with beyond(dve, ranges, g, NT, WIN) as b:
                            w = dve.snap(extra)
                            select_block(dve, left, g, b, s_sh, w).then_inc(s_lsel, 1)
                            dve.wait_ge(s_lmm, w + 1)
                            dve.tensor_tensor(acc[:, cols(b, MSG)], acc[:, cols(b, MSG)], psum[7][:, 0:MSG],
                                              ALU.add).then_inc(s_lacc, 1)
                            dve.wait_ge(s_lacc, w + 1)
                            dve.reg_add(extra, extra, 1)

                def add(g, s):
                    lo = lowest(dve, ranges, g, NT)
                    dve.wait_ge(s_mm, g + 1 + SLOTS3)
                    dve.wait_ge(s_acc, g + 1)
                    av = acc[:, bass.ds(lo * MSG, WIN * MSG)].rearrange("p (j w) -> p j w", j=WIN)
                    dve.tensor_tensor(av, av, window_sums(s, MSG), ALU.add).then_inc(s_acc, 1)

                dve.reg_mov(before, place_edges(0, 0, 0))
                dve.wait_ge(s_am, 1)
                many = place_edges(1, 1, 0)
                weigh(0, 0, 0, dve.snap(before))
                dve.reg_mov(before, many)

                def group(g, s, i):
                    dve.wait_ge(s_am, g)
                    hold(dve)
                    many = place_edges(g, s, i)
                    weigh(g - 1, (s - 1) % SLOTS3, i - (1 if s == 0 else 0), dve.snap(before))
                    dve.reg_mov(before, many)
                    add(g - 2, (s - 2) % SLOTS3)

                ring(dve, 2, NG, group)
                last = NG - 1
                weigh(last, last % SLOTS3, last // SLOTS3, dve.snap(before))
                for g in (last - 1, last):
                    add(g, g % SLOTS3)
                dve.wait_ge(s_acc, NG + 1)
                dve.wait_ge(s_bi, 16)
                dn = den[:].rearrange("p (t h) -> p t h", h=HEADS)
                done(dve.tensor_scalar(dn, av[:, :, D:MSG], 1e-16, None, ALU.add))
                done(dve.reciprocal(den[:], den[:]))

                def heads(t):
                    return t.rearrange("p (h c) -> p h c", c=C)

                with dve.Fori(0, NT // NORM) as i:
                    for k in range(NORM):
                        n = i * NORM + k
                        dve.tensor_tensor(heads(tmp[k][:]), heads(acc[:, bass.ds(n * MSG, D)]),
                                          den[:, cols(n, HEADS)].unsqueeze(2).broadcast_to([P, HEADS, C]),
                                          ALU.mult).then_inc(s_fin, 1)
                    for k in range(NORM):
                        dve.wait_ge(s_fin, i * (3 * NORM) + (k + 1))
                        dve.tensor_tensor(tmp[k][:], tmp[k][:], bias[:], ALU.add).then_inc(s_fin, 1)
                    for k in range(NORM):
                        xt = X[:, cols(i * NORM + k, D)]
                        dve.wait_ge(s_fin, i * (3 * NORM) + (NORM + k + 1))
                        dve.scalar_tensor_tensor(xt, tmp[k][:], 0.0, xt, ALU.max, ALU.add).then_inc(s_fin, 1)
                    dve.wait_ge(s_fin, i * (3 * NORM) + 3 * NORM)

        gat.close()
        ffn1 = ctx.enter_context(ExitStack())
        XN = sb(ffn1, "XN1", [P, NT * D])
        chosen = sb(ffn1, "chosen", [1, 2], I32)
        mixb = sb(ffn1, "mixb", [P, 2])
        with ExitStack() as st, nc.Block() as block:
            wrs = sb(st, "wrs", [P, DC * E1])
            brs = sb(st, "brs", [1, E1])
            part = sb(st, "part", [P, D])
            ones_col = sb(st, "ones_col", [P, 1])
            mean = sb(st, "mean", [P, DC])
            row = [sb(st, f"row{j}", [1, E1]) for j in range(4)]
            one = [sb(st, f"one{j}", [1, 1]) for j in range(8)]
            pair = sb(st, "pair", [1, 2])
            s_w = sem(st, "weights")
            s_dv = sem(st, "dve_done")
            s_pe = sem(st, "pe_done")
            s_go = sem(st, "to_pe")
            s_a = sem(st, "to_act")
            s_ab = sem(st, "from_act")
            roots = root_sems(st)

            @block.sync
            def _(sp):
                sp.dma_start(wrs[:].rearrange("p (c n) -> p c n", c=DC),
                             wr.rearrange("(c p) n -> p c n", p=P)).then_inc(s_w, 16)
                sp.dma_start(brs[:], br.rearrange("(a n) -> a n", a=1)).then_inc(s_w, 16)

            @block.vector
            def _(dve):
                done = Done(dve, s_dv)
                norm_stats(dve, done, X, roots)
                with dve.Fori(0, NT // NORM) as i:
                    for k in range(NORM):
                        normalised(dve, XN[:, cols(i * NORM + k, D)], X, i * NORM + k).then_inc(s_dv, 1)
                done.n += NT
                dve.wait_ge(s_dv, done.n)
                done(dve.tensor_scalar(part[:, 0:1], node_id[:, NT - 1:NT], float(N), None, ALU.is_lt))
                done(dve.tensor_scalar(XN[:, (NT - 1) * D:], XN[:, (NT - 1) * D:], part[:, 0:1], None, ALU.mult))
                done(dve.memset(ones_col[:], 1.0))
                done(dve.tensor_reduce(part[:], XN[:].rearrange("p (t d) -> p d t", d=D), AX.X, ALU.add))
                dve.sem_inc(s_go, 1)
                dve.wait_ge(s_pe, 1)
                done(dve.tensor_scalar(mean[:], psum[0][:, 0:DC], 1.0 / N, None, ALU.mult))
                dve.sem_inc(s_go, 1)
                dve.wait_ge(s_pe, 2)
                a, b, c, d = (r[:] for r in row)
                acts = [0]

                def softmax(to, of, width, o):
                    done(dve.tensor_reduce(one[o][:], of, AX.X, ALU.max))
                    done(dve.tensor_scalar(to, of, one[o][:], None, ALU.subtract))
                    dve.sem_inc(s_a, 1)
                    acts[0] += 1
                    dve.wait_ge(s_ab, acts[0])
                    done(dve.tensor_reduce(one[o + 1][:], to, AX.X, ALU.add))
                    done(dve.reciprocal(one[o + 1][:], one[o + 1][:]))
                    done(dve.tensor_scalar(to, to, one[o + 1][:], None, ALU.mult))

                done(dve.tensor_copy(a, psum[1][0:1, 0:E1]))
                softmax(b, a, E1, 0)
                done(dve.tensor_scalar(c, b, float(N), None, ALU.mult))
                done(dve.tensor_scalar(d, c, CAPACITY, None, ALU.max))
                done(dve.reciprocal(d, d))
                done(dve.tensor_scalar(d, d, CAPACITY, None, ALU.mult))
                done(dve.tensor_tensor(a, b, d, ALU.mult))
                softmax(b, a, E1, 2)
                for j in range(2):
                    done(dve.tensor_reduce(pair[:, j:j + 1], b, AX.X, ALU.max))
                    done(dve.tensor_scalar(c, b, pair[:, j:j + 1], None, ALU.is_ge))
                    done(dve.scalar_tensor_tensor(c, c, -1000.0, iota[0:1, 0:E1], ALU.mult, ALU.add))
                    done(dve.tensor_reduce(one[4][:], c, AX.X, ALU.min))
                    done(dve.tensor_scalar(d, c, one[4][:], None, ALU.is_equal))
                    done(dve.tensor_scalar(one[5][:], one[4][:], 1000.0, None, ALU.add))
                    done(dve.tensor_copy(chosen[:, j:j + 1], one[5][:]))
                    if j == 0:
                        done(dve.scalar_tensor_tensor(b, d, NEG, b, ALU.mult, ALU.add))
                softmax(row[0][:, 0:2], pair[:], 2, 6)
                dve.sem_inc(s_go, 1)
                dve.wait_ge(s_pe, 3)
                done(dve.tensor_copy(mixb[:], psum[2][:, 0:2]))

            @block.scalar
            def _(act):
                take_roots(act, roots)
                act.wait_ge(s_a, 1)
                act.activation(row[1][:], row[1][:], ACT.Exp).then_inc(s_ab, 1)
                act.wait_ge(s_a, 2)
                act.activation(row[1][:], row[1][:], ACT.Exp).then_inc(s_ab, 1)
                act.wait_ge(s_a, 3)
                act.activation(row[0][:, 0:2], row[0][:, 0:2], ACT.Exp).then_inc(s_ab, 1)

            @block.tensor
            def _(pe):
                pe.wait_ge(s_w, 32)
                pe.wait_ge(s_go, 1)
                for c in range(DC):
                    mm = pe.matmul(psum[0][:, c:c + 1], part[:, c * P:(c + 1) * P], ones_col[:], start=True, stop=True)
                mm.then_inc(s_pe, 1)
                pe.wait_ge(s_go, 2)
                for c in range(DC):
                    pe.matmul(psum[1][0:1, 0:E1], mean[:, c:c + 1], wrs[:, c * E1:(c + 1) * E1], start=(c == 0), stop=False)
                pe.matmul(psum[1][0:1, 0:E1], ones_row[:, 0:1], brs[:], start=False, stop=True).then_inc(s_pe, 1)
                pe.wait_ge(s_go, 3)
                pe.matmul(psum[2][:, 0:2], ones_row[:], row[0][:, 0:2], start=True, stop=True).then_inc(s_pe, 1)

        with ExitStack() as st, nc.Block() as block:
            W1 = sb(st, "W1b", [P, 2 * DC * F])
            W2 = sb(st, "W2b", [P, 2 * FC * D])
            B1 = sb(st, "B1b", [1, 2 * F])
            B1T = sb(st, "B1bT", [P, 2 * FC])
            b2s = sb(st, "b2s", [P, 2 * D])
            gb = sb(st, "gamma_beta1", [P, 2 * D])
            xin = [sb(st, f"xin_g{s}", [P, D]) for s in range(2)]
            xT = [sb(st, f"xT_g{s}", [P, D]) for s in range(2)]
            hT = [sb(st, f"hT_g{j}", [P, F]) for j in range(2)]
            tmp = [sb(st, f"tmpb{s}", [P, D]) for s in range(NORM)]
            roots = root_sems(st)
            s_w = sem(st, "weights")
            s_gb = sem(st, "gamma_beta")
            s_bt = sem(st, "bias_turned")
            s_b = sem(st, "bias_and_weights_ready")
            s_tp = sem(st, "turned")
            s_xt = sem(st, "xT_ready")
            s_in = sem(st, "tile_in")
            s_h = sem(st, "hidden")
            s_hr = sem(st, "hidden_ready")
            s_y = sem(st, "result")
            s_mx = sem(st, "mix_step")
            s_dv = sem(st, "dve_done")
            s_nx = sem(st, "norm_step")
            s_o = sem(st, "X_done")
            s_os = sem(st, "out_stored")

            @block.sync
            def _(sp):
                for j in range(2):
                    e = sp.value_load(chosen[0:1, j:j + 1], min_val=0, max_val=E1 - 1)
                    sp.dma_start(B1[:, j * F:(j + 1) * F], b1b[bass.ds(e, 1), :]).then_inc(s_w, 16)
                    sp.dma_start(W1[:, j * DC * F:(j + 1) * DC * F].rearrange("p (c f) -> p c f", f=F),
                                 w1b[bass.ds(e, 1)].rearrange("e (c p) f -> p (e c) f", p=P)).then_inc(s_w, 16)
                    sp.dma_start(W2[:, j * FC * D:(j + 1) * FC * D].rearrange("p (c f) -> p c f", f=D),
                                 w2b[bass.ds(e, 1)].rearrange("e (c p) f -> p (e c) f", p=P)).then_inc(s_w, 16)
                    sp.dma_start(b2s[:, j * D:(j + 1) * D], b2b[bass.ds(e, 1), :].broadcast_to([P, D])).then_inc(s_w, 16)
                sp.dma_start(gb[:, 0:D], g1.partition_broadcast(P)).then_inc(s_gb, 16)
                sp.dma_start(gb[:, D:2 * D], be1.partition_broadcast(P)).then_inc(s_gb, 16)
                with sp.Fori(0, NT - 1) as n:
                    sp.wait_ge(s_o, n + 1)
                    sp.dma_start(out[bass.ds(n * P, P), :], X[:, cols(n, D)]).then_inc(s_os, 16)
                sp.wait_ge(s_o, NT)
                sp.dma_start(out[(NT - 1) * P:N, :], X[0:LAST, (NT - 1) * D:NT * D]).then_inc(s_os, 16)
                sp.wait_ge(s_os, 16 * NT)

            @block.gpsimd
            def _(pool):
                def give(n, s, i):
                    pool.wait_ge(s_tp, n + 1)
                    hold(pool)
                    pool.tensor_copy(xin[s][:], XN[:, cols(n, D)]).then_inc(s_in, 1)

                tiles2(pool, NT, give)

            @block.tensor
            def _(pe):
                pe.sem_inc(s_tp, 2)
                pe.wait_ge(s_w, 16 * 8)
                for j in range(2 * FC):
                    mm = pe.matmul(psum[7][:, j:j + 1], B1[:, j * P:(j + 1) * P], ones_row[:, 0:1], start=True, stop=True)
                mm.then_inc(s_bt, 1)
                pe.wait_ge(s_b, 1)

                def turn(n, s):
                    pe.wait_ge(s_in, n + 1)
                    pe.transpose(psum[s][:, 0:P], xin[s][:, 0:P], ident[:])
                    pe.transpose(psum[s][:, P:2 * P], xin[s][:, P:2 * P], ident[:]).then_inc(s_tp, 1)

                def up(n, s):
                    pe.wait_ge(s_xt, n + 1)
                    for j in range(2):
                        for c in range(FC):
                            for d in range(DC):
                                at = (j * DC + d) * F + c * P
                                mm = pe.matmul(psum[2 + j][:, c * P:(c + 1) * P], W1[:, at:at + P],
                                               xT[s][:, d * P:(d + 1) * P], start=(d == 0), stop=(d == DC - 1))
                        mm.then_inc(s_h, 1)

                def down(n, s):
                    for j in range(2):
                        pe.wait_ge(s_hr, n * 2 + (j + 1))
                        for c in range(FC):
                            at = (j * FC + c) * D
                            mm = pe.matmul(psum[4 + s][:, 0:D], hT[j][:, c * P:(c + 1) * P], W2[:, at:at + D],
                                           start=(j == 0 and c == 0), stop=(j == 1 and c == FC - 1))
                    mm.then_inc(s_y, 1)

                def tile(n, s, i):
                    up(n, s)
                    if not (isinstance(n, int) and n == NT - 1):
                        turn(n + 1, 1 - s)
                    down(n, s)

                turn(0, 0)
                tiles2(pe, NT, tile)

            @block.scalar
            def _(act):
                act.wait_ge(s_b, 1)

                def hidden(n, s, i):
                    for j in range(2):
                        act.wait_ge(s_h, n * 2 + (j + 1))
                        for c in range(FC):
                            ins = act.activation(hT[j][:, c * P:(c + 1) * P], psum[2 + j][:, c * P:(c + 1) * P],
                                                 ACT.Gelu, bias=B1T[:, j * FC + c:j * FC + c + 1])
                        ins.then_inc(s_hr, 1)

                tiles2(act, NT, hidden)
                take_roots(act, roots)

            @block.vector
            def _(dve):
                done = Done(dve, s_dv)
                dve.wait_ge(s_gb, 32)
                dve.wait_ge(s_w, 16 * 8)
                for j in range(2):
                    w2j = W2[:, j * FC * D:(j + 1) * FC * D]
                    done(dve.tensor_scalar(w2j, w2j, mixb[:, j:j + 1], None, ALU.mult))
                done(dve.tensor_scalar(b2s[:, 0:D], b2s[:, 0:D], mixb[:, 0:1], None, ALU.mult))
                done(dve.scalar_tensor_tensor(b2s[:, 0:D], b2s[:, D:2 * D], mixb[:, 1:2], b2s[:, 0:D],
                                              ALU.mult, ALU.add))
                dve.wait_ge(s_bt, 1)
                dve.tensor_copy(B1T[:], psum[7][:, 0:2 * FC]).then_inc(s_b, 1)

                def copy_in(n, s):
                    dve.wait_ge(s_tp, n + 3)
                    dve.tensor_copy(xT[s][:], psum[s][:, 0:D]).then_inc(s_xt, 1)

                def result(n, s, i):
                    if not (isinstance(n, int) and n == NT - 1):
                        copy_in(n + 1, 1 - s)
                    yt = XN[:, cols(n, D)]
                    step = Done(dve, s_mx, n * 3)
                    dve.tensor_tensor(X[:, cols(n, D)], X[:, cols(n, D)], gb[:, D:2 * D], ALU.add)
                    step(dve.tensor_tensor(yt, yt, b2s[:, 0:D], ALU.add))
                    dve.wait_ge(s_y, n + 1)
                    step(dve.tensor_tensor(yt, yt, psum[4 + s][:, 0:D], ALU.add))
                    step(dve.bn_stats(stats[:, cols(n, 6)], yt), wait=False)

                copy_in(0, 0)
                tiles2(dve, NT, result)
                dve.wait_ge(s_mx, 3 * NT)
                aggregate(dve, Done(dve, s_dv, done.n), roots)

                norm_onto_x(dve, s_nx, XN, tmp, gb, s_o)


_WEIGHTS = ["L0_gnn_W_self", "L0_gnn_W_neigh", "L0_ffn_gate_w", "L0_ffn_gate_b", "L0_ffn_w1", "L0_ffn_b1",
            "L0_ffn_w2", "L0_ffn_b2", "L0_ffn_gamma", "L0_ffn_beta", "L1_gnn_W", "L1_gnn_att_src",
            "L1_gnn_att_dst", "L1_gnn_bias", "L1_ffn_Wr", "L1_ffn_br", "L1_ffn_W1", "L1_ffn_b1", "L1_ffn_W2",
            "L1_ffn_b2", "L1_ffn_gamma", "L1_ffn_beta"]


def kernel(**inputs):
    import numpy as _np
    import concourse.bacc as _bacc
    from concourse import mybir as _mybir
    from concourse.bass_utils import run_bass_kernel_spmd as _run

    src = _np.zeros(NG * GE, _np.int32)
    dst = _np.full(NG * GE, NPAD - 1, _np.int32)
    src[:E] = _np.asarray(inputs["src"])
    dst[:E] = _np.asarray(inputs["dst"])
    given = {"x": inputs["x"], "src_cols": src.reshape(NG * GT, P).T, "dst_cols": dst.reshape(NG * GT, P).T,
             "dst_rows": dst.reshape(MG, ME), **{n: inputs[n] for n in _WEIGHTS}}
    nc = _bacc.Bacc("TRN2", target_bir_lowering=False, num_devices=1)
    arrays, args = {}, []
    for name, a in given.items():
        a = _np.ascontiguousarray(a)
        arrays[f"in_{name}"] = a
        args.append(nc.dram_tensor(f"in_{name}", a.shape, _mybir.dt.from_np(a.dtype), kind="ExternalInput").ap())
    args.append(nc.dram_tensor("out_x", (N, D), _mybir.dt.float32, kind="ExternalOutput").ap())
    program(nc, *args)
    r = _run(nc, [arrays], core_ids=[0])
    return r.results[0]["out_x"]
```
